# Optimizing a Trainium2 kernel written in Bass

```python
import numpy as np
import jax
import jax.numpy as jnp

def _softmax(x, axis=-1):
    return jax.nn.softmax(x, axis=axis)

def _gelu(x):
    return jax.nn.gelu(x, approximate=True)

def _silu(x):
    return jax.nn.silu(x)

def _sigmoid(x):
    return jax.nn.sigmoid(x)

def _layernorm(x, axis=-1, eps=1e-05):
    m = jnp.mean(x, axis=axis, keepdims=True)
    v = jnp.var(x, axis=axis, keepdims=True)
    return (x - m) / jnp.sqrt(v + eps)

def _scatter_add(tgt, idx, src, axis=0):
    return tgt.at[idx].add(src)

def _segment_sum(src, seg, n):
    return jax.ops.segment_sum(src, seg, n)
kernel_name = 'mk_macaron_d4_jaxref_r8_e5b5d1'

def setup_inputs(seed: int=0):
    np.random.seed(seed)
    _w = jnp.asarray

    def _L0_attn_setup():
        import jax, jax.numpy as jnp
        import numpy as np
        B, S, D = (1, 256, 256)
        H, KV = (16, 4)
        NB, NV = (8, 8)
        W = 32 // NB
        QKD = W * NB
        key = jax.random.key(seed)
        ks = jax.random.split(key, 5)
        s = 0.02
        return {'hidden_states': jax.random.normal(ks[0], (B, S, D), jnp.float32), 'Wq': jax.random.normal(ks[1], (H * NB, D), jnp.float32) * s, 'Wk': jax.random.normal(ks[2], (KV * NB, D), jnp.float32) * s, 'Wv': jax.random.normal(ks[3], (KV * NV, D), jnp.float32) * s, 'Wo': jax.random.normal(ks[4], (D, H * NV), jnp.float32) * s, 'v_emb0': jnp.full((H * NV,), -1e-05, jnp.float32), 'v_emb1': jnp.full((H * NV,), 1e-05, jnp.float32), 'tau': jnp.ones((), jnp.float32)}
    _L0_attn_in = _L0_attn_setup()

    def _L0_ffn_setup():
        import jax, jax.numpy as jnp
        import numpy as np
        DIM = 256
        HID = 704
        ZERO_POINT = 128.0

        def _qlinear(x, wq, scale):
            W = (wq.astype(jnp.float32) - ZERO_POINT) * scale[:, None]
            return jnp.einsum('bsd,hd->bsh', x, W)
        key = jax.random.key(seed)
        ks = jax.random.split(key, 7)
        B, S = (4, 256)
        sg = jax.random.uniform(ks[1], (HID,)) * (0.02 / np.sqrt(DIM)) + 0.0001
        su = jax.random.uniform(ks[3], (HID,)) * (0.02 / np.sqrt(DIM)) + 0.0001
        sd = jax.random.uniform(ks[5], (DIM,)) * (0.02 / np.sqrt(HID)) + 0.0001
        return {'x': jax.random.normal(ks[0], (B, S, DIM), dtype=jnp.float32), 'wq_gate': jax.random.randint(ks[2], (HID, DIM), 0, 32, dtype=jnp.int32), 's_gate': sg, 'wq_up': jax.random.randint(ks[4], (HID, DIM), 0, 32, dtype=jnp.int32), 's_up': su, 'wq_down': jax.random.randint(ks[6], (DIM, HID), 0, 32, dtype=jnp.int32), 's_down': sd}
    _L0_ffn_in = _L0_ffn_setup()

    def _L1_attn_setup():
        import jax, jax.numpy as jnp
        import numpy as np
        D_MODEL = 256
        D_STATE = 16
        D_INNER = D_MODEL
        B, L = (4, 512)
        key = jax.random.key(seed)
        ks = jax.random.split(key, 8)
        return {'x': jax.random.normal(ks[0], (B, L, D_INNER), jnp.float32), 'A_log': jax.random.normal(ks[1], (D_INNER, D_STATE), jnp.float32) * 0.5, 'x_proj_w': jax.random.normal(ks[2], (2 * D_STATE, D_INNER), jnp.float32) * (1.0 / np.sqrt(D_INNER)), 'x_proj_b': jnp.zeros((2 * D_STATE,), jnp.float32), 'dt_proj_w': jax.random.normal(ks[3], (D_INNER, D_INNER), jnp.float32) * (1.0 / np.sqrt(D_INNER)), 'dt_proj_b': jax.random.normal(ks[4], (D_INNER,), jnp.float32) * 0.1, 'out_proj_w': jax.random.normal(ks[5], (D_MODEL, D_INNER), jnp.float32) * (1.0 / np.sqrt(D_INNER)), 'out_proj_b': jnp.zeros((D_MODEL,), jnp.float32)}
    _L1_attn_in = _L1_attn_setup()

    def _L1_ffn_setup():
        import jax, jax.numpy as jnp
        import numpy as np
        TOP_K = 4
        key = jax.random.key(seed)
        ks = jax.random.split(key, 8)
        B, S, D, E, H, HS = (2, 256, 256, 16, 128, 512)
        scaled = lambda k, shape, fan: jax.random.normal(k, shape, jnp.float32) * fan ** (-0.5)
        return {'x': jax.random.normal(ks[0], (B, S, D), jnp.float32), 'w_router': scaled(ks[1], (D, E), D), 'we1': scaled(ks[2], (E, D, H), D), 'we3': scaled(ks[3], (E, D, H), D), 'we2': scaled(ks[4], (E, H, D), H), 'ws1': scaled(ks[5], (D, HS), D), 'ws3': scaled(ks[6], (D, HS), D), 'ws2': scaled(ks[7], (HS, D), HS)}
    _L1_ffn_in = _L1_ffn_setup()

    def _L2_attn_setup():
        import jax, jax.numpy as jnp
        import numpy as np
        H, DK, DV = (6, 32, 64)
        HID = 256
        CONV = 4
        NORM_EPS = 1e-05

        def causal_dwconv_silu(x, w):
            K = w.shape[1]
            xp = jnp.pad(x, ((0, 0), (K - 1, 0), (0, 0)))
            y = jax.lax.conv_general_dilated(jnp.transpose(xp, (0, 2, 1)), w[:, None, :], (1,), 'VALID', feature_group_count=w.shape[0])
            return jax.nn.silu(jnp.transpose(y, (0, 2, 1)))

        def l2norm(x, eps=1e-06):
            return x * jax.lax.rsqrt(jnp.sum(x * x, axis=-1, keepdims=True) + eps)
        key = jax.random.key(seed)
        ks = jax.random.split(key, 16)
        B, T = (2, 512)
        s = HID ** (-0.5)
        return dict(hidden_states=jax.random.normal(ks[0], (B, T, HID), jnp.float32), Wq=jax.random.normal(ks[1], (H * DK, HID), jnp.float32) * s, Wk=jax.random.normal(ks[2], (H * DK, HID), jnp.float32) * s, Wv=jax.random.normal(ks[3], (H * DV, HID), jnp.float32) * s, Wb=jax.random.normal(ks[4], (H, HID), jnp.float32) * s, Wa=jax.random.normal(ks[5], (H, HID), jnp.float32) * s, A_log=jnp.log(jax.random.uniform(ks[6], (H,), jnp.float32, 0.5, 16.0)), dt_bias=jax.random.normal(ks[7], (H,), jnp.float32) * 0.1, conv_wq=jax.random.normal(ks[8], (H * DK, CONV), jnp.float32) * 0.5, conv_wk=jax.random.normal(ks[9], (H * DK, CONV), jnp.float32) * 0.5, conv_wv=jax.random.normal(ks[10], (H * DV, CONV), jnp.float32) * 0.5, Wg=jax.random.normal(ks[11], (H * DV, HID), jnp.float32) * s, norm_w=jnp.ones((DV,), jnp.float32), Wo=jax.random.normal(ks[12], (HID, H * DV), jnp.float32) * (H * DV) ** (-0.5))
    _L2_attn_in = _L2_attn_setup()

    def _L2_ffn_setup():
        import jax, jax.numpy as jnp
        import numpy as np
        EPS = 1e-05
        ROPE_BASE = 150000.0
        NHEADS = 32
        KVHEADS = 8
        HEAD_DIM = 64
        TOP_K = 4

        def _rms(x, w):
            return x * jax.lax.rsqrt(jnp.mean(x * x, -1, keepdims=True) + EPS) * w

        def _rope(q, k):
            S, hd = (q.shape[1], q.shape[-1])
            half = hd // 2
            inv = 1.0 / ROPE_BASE ** (jnp.arange(half, dtype=jnp.float32) / half)
            ang = jnp.arange(S, dtype=jnp.float32)[:, None] * inv
            cos = jnp.concatenate([jnp.cos(ang), jnp.cos(ang)], -1)[None, :, None, :]
            sin = jnp.concatenate([jnp.sin(ang), jnp.sin(ang)], -1)[None, :, None, :]

            def rot(t):
                t1, t2 = (t[..., :half], t[..., half:])
                return jnp.concatenate([-t2, t1], -1)
            return (q * cos + rot(q) * sin, k * cos + rot(k) * sin)
        key = jax.random.key(seed)
        ks = jax.random.split(key, 12)
        B, S, D, H, E = (1, 128, 256, 256, 16)
        s = 0.02
        return {'x': jax.random.normal(ks[0], (B, S, D), jnp.float32), 'ln_w': jnp.ones((D,), jnp.float32), 'ff_ln_w': jnp.ones((D,), jnp.float32), 'wq': jax.random.normal(ks[1], (D, NHEADS * HEAD_DIM), jnp.float32) * s, 'wk': jax.random.normal(ks[2], (D, KVHEADS * HEAD_DIM), jnp.float32) * s, 'wv': jax.random.normal(ks[3], (D, KVHEADS * HEAD_DIM), jnp.float32) * s, 'wo': jax.random.normal(ks[4], (NHEADS * HEAD_DIM, D), jnp.float32) * s, 'wg': jax.random.normal(ks[5], (D, E), jnp.float32) * s, 'w1': jax.random.normal(ks[6], (E, D, H), jnp.float32) * s, 'w3': jax.random.normal(ks[7], (E, D, H), jnp.float32) * s, 'w2': jax.random.normal(ks[8], (E, H, D), jnp.float32) * s}
    _L2_ffn_in = _L2_ffn_setup()

    def _L3_attn_setup():
        import jax, jax.numpy as jnp
        import numpy as np
        import math
        D = 32
        N = 256
        B = 8
        N_PLUS_1 = 256
        key = jax.random.key(seed)
        k1, k2, k3, k4, k5 = jax.random.split(key, 5)
        scale = 1.0 / math.sqrt(D)
        return {'Z_in': jax.random.normal(k1, (B, D + 1, N), dtype=jnp.float32), 'A_l': jax.random.normal(k2, (D, D), dtype=jnp.float32) * scale, 'r_l': jax.random.normal(k3, (1,), dtype=jnp.float32), 'B_l': jax.random.normal(k4, (D, D), dtype=jnp.float32) * scale, 'C_l': jax.random.normal(k5, (D, D), dtype=jnp.float32) * scale}
    _L3_attn_in = _L3_attn_setup()

    def _L3_ffn_setup():
        import jax, jax.numpy as jnp
        import numpy as np
        B, T, D = (4, 256, 256)
        E = 8
        K = 2
        F = 1024 // (E // 2)
        key = jax.random.key(seed)
        ks = jax.random.split(key, 5)
        s_in = 1.0 / np.sqrt(D)
        s_mid = 1.0 / np.sqrt(F)
        x = jax.random.normal(ks[0], (B, T, D), dtype=jnp.float32)
        Wr = jax.random.normal(ks[1], (D, E), dtype=jnp.float32) * s_in
        Wg = jax.random.normal(ks[2], (E, D, F), dtype=jnp.float32) * s_in
        Wu = jax.random.normal(ks[3], (E, D, F), dtype=jnp.float32) * s_in
        Wd = jax.random.normal(ks[4], (E, F, D), dtype=jnp.float32) * s_mid
        return {'x': x, 'Wr': Wr, 'Wg': Wg, 'Wu': Wu, 'Wd': Wd}
    _L3_ffn_in = _L3_ffn_setup()
    _d = {'L0_attn_hidden_states': _L0_attn_in['hidden_states'], 'L0_attn_Wq': _L0_attn_in['Wq'], 'L0_attn_Wk': _L0_attn_in['Wk'], 'L0_attn_Wv': _L0_attn_in['Wv'], 'L0_attn_Wo': _L0_attn_in['Wo'], 'L0_attn_v_emb0': _L0_attn_in['v_emb0'], 'L0_attn_v_emb1': _L0_attn_in['v_emb1'], 'L0_attn_tau': _L0_attn_in['tau'], 'L0_ffn_wq_gate': _L0_ffn_in['wq_gate'], 'L0_ffn_s_gate': _L0_ffn_in['s_gate'], 'L0_ffn_wq_up': _L0_ffn_in['wq_up'], 'L0_ffn_s_up': _L0_ffn_in['s_up'], 'L0_ffn_wq_down': _L0_ffn_in['wq_down'], 'L0_ffn_s_down': _L0_ffn_in['s_down'], 'L1_attn_A_log': _L1_attn_in['A_log'], 'L1_attn_x_proj_w': _L1_attn_in['x_proj_w'], 'L1_attn_x_proj_b': _L1_attn_in['x_proj_b'], 'L1_attn_dt_proj_w': _L1_attn_in['dt_proj_w'], 'L1_attn_dt_proj_b': _L1_attn_in['dt_proj_b'], 'L1_attn_out_proj_w': _L1_attn_in['out_proj_w'], 'L1_attn_out_proj_b': _L1_attn_in['out_proj_b'], 'L1_ffn_w_router': _L1_ffn_in['w_router'], 'L1_ffn_we1': _L1_ffn_in['we1'], 'L1_ffn_we3': _L1_ffn_in['we3'], 'L1_ffn_we2': _L1_ffn_in['we2'], 'L1_ffn_ws1': _L1_ffn_in['ws1'], 'L1_ffn_ws3': _L1_ffn_in['ws3'], 'L1_ffn_ws2': _L1_ffn_in['ws2'], 'L2_attn_Wq': _L2_attn_in['Wq'], 'L2_attn_Wk': _L2_attn_in['Wk'], 'L2_attn_Wv': _L2_attn_in['Wv'], 'L2_attn_Wb': _L2_attn_in['Wb'], 'L2_attn_Wa': _L2_attn_in['Wa'], 'L2_attn_A_log': _L2_attn_in['A_log'], 'L2_attn_dt_bias': _L2_attn_in['dt_bias'], 'L2_attn_conv_wq': _L2_attn_in['conv_wq'], 'L2_attn_conv_wk': _L2_attn_in['conv_wk'], 'L2_attn_conv_wv': _L2_attn_in['conv_wv'], 'L2_attn_Wg': _L2_attn_in['Wg'], 'L2_attn_norm_w': _L2_attn_in['norm_w'], 'L2_attn_Wo': _L2_attn_in['Wo'], 'L2_ffn_ln_w': _L2_ffn_in['ln_w'], 'L2_ffn_ff_ln_w': _L2_ffn_in['ff_ln_w'], 'L2_ffn_wq': _L2_ffn_in['wq'], 'L2_ffn_wk': _L2_ffn_in['wk'], 'L2_ffn_wv': _L2_ffn_in['wv'], 'L2_ffn_wo': _L2_ffn_in['wo'], 'L2_ffn_wg': _L2_ffn_in['wg'], 'L2_ffn_w1': _L2_ffn_in['w1'], 'L2_ffn_w3': _L2_ffn_in['w3'], 'L2_ffn_w2': _L2_ffn_in['w2'], 'L3_attn_A_l': _L3_attn_in['A_l'], 'L3_attn_r_l': _L3_attn_in['r_l'], 'L3_attn_B_l': _L3_attn_in['B_l'], 'L3_attn_C_l': _L3_attn_in['C_l'], 'L3_ffn_Wr': _L3_ffn_in['Wr'], 'L3_ffn_Wg': _L3_ffn_in['Wg'], 'L3_ffn_Wu': _L3_ffn_in['Wu'], 'L3_ffn_Wd': _L3_ffn_in['Wd']}
    _x0 = _d['L0_attn_hidden_states']
    _d['L0_attn_hidden_states'] = jax.random.normal(jax.random.fold_in(jax.random.key(seed), 1), (1, 1024, 256), dtype=_x0.dtype)
    del _x0
    return _d

def reference(L0_attn_hidden_states, L0_attn_Wq, L0_attn_Wk, L0_attn_Wv, L0_attn_Wo, L0_attn_v_emb0, L0_attn_v_emb1, L0_attn_tau, L0_ffn_wq_gate, L0_ffn_s_gate, L0_ffn_wq_up, L0_ffn_s_up, L0_ffn_wq_down, L0_ffn_s_down, L1_attn_A_log, L1_attn_x_proj_w, L1_attn_x_proj_b, L1_attn_dt_proj_w, L1_attn_dt_proj_b, L1_attn_out_proj_w, L1_attn_out_proj_b, L1_ffn_w_router, L1_ffn_we1, L1_ffn_we3, L1_ffn_we2, L1_ffn_ws1, L1_ffn_ws3, L1_ffn_ws2, L2_attn_Wq, L2_attn_Wk, L2_attn_Wv, L2_attn_Wb, L2_attn_Wa, L2_attn_A_log, L2_attn_dt_bias, L2_attn_conv_wq, L2_attn_conv_wk, L2_attn_conv_wv, L2_attn_Wg, L2_attn_norm_w, L2_attn_Wo, L2_ffn_ln_w, L2_ffn_ff_ln_w, L2_ffn_wq, L2_ffn_wk, L2_ffn_wv, L2_ffn_wo, L2_ffn_wg, L2_ffn_w1, L2_ffn_w3, L2_ffn_w2, L3_attn_A_l, L3_attn_r_l, L3_attn_B_l, L3_attn_C_l, L3_ffn_Wr, L3_ffn_Wg, L3_ffn_Wu, L3_ffn_Wd):

    def _L0_attn_ref(hidden_states, Wq, Wk, Wv, Wo, v_emb0, v_emb1, tau):
        import jax, jax.numpy as jnp
        import numpy as np
        B, S, D = (1, 256, 256)
        H, KV = (16, 4)
        NB, NV = (8, 8)
        W = 32 // NB
        QKD = W * NB
        bsz, seq_len, _ = hidden_states.shape
        n_rep = H // KV
        q = jnp.tanh(hidden_states @ Wq.T / tau).reshape(bsz, seq_len, H, NB).transpose(0, 2, 1, 3)
        k = jnp.tanh(hidden_states @ Wk.T / tau).reshape(bsz, seq_len, KV, NB).transpose(0, 2, 1, 3)
        v = jax.nn.sigmoid(hidden_states @ Wv.T / tau).reshape(bsz, seq_len, KV, NV).transpose(0, 2, 1, 3)
        pad = ((0, 0), (0, 0), (W - 1, 0), (0, 0))
        qp = jnp.pad(q, pad)
        kp = jnp.pad(k, pad)
        idx = jnp.arange(seq_len)[:, None] + jnp.arange(W)[None, :]
        qw = qp[:, :, idx, :].reshape(bsz, H, seq_len, QKD)
        kw = kp[:, :, idx, :].reshape(bsz, KV, seq_len, QKD)
        vs = jnp.concatenate([v[:, :, 1:, :], jnp.zeros_like(v[:, :, :1, :])], axis=2)
        kw = jnp.repeat(kw, n_rep, axis=1)
        vs = jnp.repeat(vs, n_rep, axis=1)
        r = jnp.arange(seq_len, dtype=hidden_states.dtype)
        bias = r[None, :] / (r[:, None] + 1)
        mask = jnp.tril(jnp.ones((seq_len, seq_len), bool), -1)
        bias = jnp.where(mask, bias, -jnp.inf) / tau
        scale = 1.0 / np.sqrt(QKD) / tau
        scores = jnp.einsum('bhqd,bhkd->bhqk', qw, kw) * scale + bias
        m = jnp.max(scores, axis=-1, keepdims=True)
        m = jnp.where(jnp.isfinite(m), m, 0.0)
        e = jnp.exp(scores - m)
        denom = jnp.sum(e, axis=-1, keepdims=True)
        p = jnp.where(denom > 0, e / jnp.where(denom > 0, denom, 1.0), 0.0)
        out = jnp.einsum('bhqk,bhkd->bhqd', p, vs)
        out = out.transpose(0, 2, 1, 3).reshape(bsz, seq_len, H * NV)
        out = out * v_emb1 + (1.0 - out) * v_emb0
        return out @ Wo.T

    def _L0_ffn_ref(x, wq_gate, s_gate, wq_up, s_up, wq_down, s_down):
        import jax, jax.numpy as jnp
        import numpy as np
        DIM = 256
        HID = 704
        ZERO_POINT = 128.0

        def _qlinear(x, wq, scale):
            W = (wq.astype(jnp.float32) - ZERO_POINT) * scale[:, None]
            return jnp.einsum('bsd,hd->bsh', x, W)
        gate = _qlinear(x, wq_gate, s_gate)
        gate = jax.nn.silu(gate)
        up = _qlinear(x, wq_up, s_up)
        return _qlinear(gate * up, wq_down, s_down)

    def _L1_attn_ref(x, A_log, x_proj_w, x_proj_b, dt_proj_w, dt_proj_b, out_proj_w, out_proj_b):
        import jax, jax.numpy as jnp
        import numpy as np
        D_MODEL = 256
        D_STATE = 16
        D_INNER = D_MODEL
        B, L = (4, 512)
        d_state = A_log.shape[1]
        A = -jnp.exp(A_log)
        dt = jax.nn.softplus(jnp.einsum('bld,ed->ble', x, dt_proj_w) + dt_proj_b)
        bc = jnp.einsum('bld,ed->ble', x, x_proj_w) + x_proj_b
        Bs, Cs = (bc[..., :d_state], bc[..., d_state:])

        def step(h, inputs):
            xt, dtt, Bt, Ct = inputs
            dA = jnp.exp(dtt[..., None] * A)
            dBx = (dtt * xt)[..., None] * Bt[:, None, :]
            h = dA * h + dBx
            y = jnp.einsum('bdn,bn->bd', h, Ct)
            return (h, y)
        bsz, seqlen, d_inner = x.shape
        h0 = jnp.zeros((bsz, d_inner, d_state), x.dtype)
        xs = (jnp.swapaxes(x, 0, 1), jnp.swapaxes(dt, 0, 1), jnp.swapaxes(Bs, 0, 1), jnp.swapaxes(Cs, 0, 1))
        _, ys = jax.lax.scan(step, h0, xs)
        y = jnp.swapaxes(ys, 0, 1)
        return jnp.einsum('bld,md->blm', y, out_proj_w) + out_proj_b

    def _L1_ffn_ref(x, w_router, we1, we3, we2, ws1, ws3, ws2):
        import jax, jax.numpy as jnp
        import numpy as np
        TOP_K = 4
        B, S, D = x.shape
        T = B * S
        E = w_router.shape[1]
        xt = x.reshape(T, D)
        probs = jax.nn.softmax(xt @ w_router, axis=-1)
        top_w, top_i = jax.lax.top_k(probs, TOP_K)
        top_w = top_w / jnp.sum(top_w, axis=-1, keepdims=True)
        cw = jnp.zeros((T, E), xt.dtype).at[jnp.arange(T)[:, None], top_i].add(top_w)
        g = jax.nn.silu(jnp.einsum('td,edh->teh', xt, we1)) * jnp.einsum('td,edh->teh', xt, we3)
        g = g * cw[:, :, None]
        moe_out = jnp.einsum('teh,ehd->td', g, we2)
        shared = jax.nn.silu(xt @ ws1) * (xt @ ws3) @ ws2
        k = TOP_K
        out = shared / (k + 1) + moe_out * (k / (k + 1))
        return out.reshape(B, S, D)

    def _L2_attn_ref(hidden_states, Wq, Wk, Wv, Wb, Wa, A_log, dt_bias, conv_wq, conv_wk, conv_wv, Wg, norm_w, Wo):
        import jax, jax.numpy as jnp
        import numpy as np
        H, DK, DV = (6, 32, 64)
        HID = 256
        CONV = 4
        NORM_EPS = 1e-05

        def causal_dwconv_silu(x, w):
            K = w.shape[1]
            xp = jnp.pad(x, ((0, 0), (K - 1, 0), (0, 0)))
            y = jax.lax.conv_general_dilated(jnp.transpose(xp, (0, 2, 1)), w[:, None, :], (1,), 'VALID', feature_group_count=w.shape[0])
            return jax.nn.silu(jnp.transpose(y, (0, 2, 1)))

        def l2norm(x, eps=1e-06):
            return x * jax.lax.rsqrt(jnp.sum(x * x, axis=-1, keepdims=True) + eps)
        x = hidden_states
        B, T, _ = x.shape
        q = causal_dwconv_silu(x @ Wq.T, conv_wq).reshape(B, T, H, DK)
        k = causal_dwconv_silu(x @ Wk.T, conv_wk).reshape(B, T, H, DK)
        v = causal_dwconv_silu(x @ Wv.T, conv_wv).reshape(B, T, H, DV)
        beta = jax.nn.sigmoid(x @ Wb.T)
        g = -jnp.exp(A_log) * jax.nn.softplus(x @ Wa.T + dt_bias)
        q = l2norm(q) * DK ** (-0.5)
        k = l2norm(k)

        def step(S, inp):
            qt, kt, vt, gt, bt = inp
            S = S * jnp.exp(gt)[..., None, None]
            v_new = vt - jnp.einsum('bhk,bhkv->bhv', kt, S)
            S = S + bt[..., None, None] * (kt[..., :, None] * v_new[..., None, :])
            o = jnp.einsum('bhk,bhkv->bhv', qt, S)
            return (S, o)
        S0 = jnp.zeros((B, H, DK, DV), x.dtype)
        tm = lambda a: jnp.moveaxis(a, 1, 0)
        _, o = jax.lax.scan(step, S0, (tm(q), tm(k), tm(v), tm(g), tm(beta)))
        o = jnp.moveaxis(o, 0, 1)
        var = jnp.mean(jnp.square(o.astype(jnp.float32)), axis=-1, keepdims=True)
        o = o * jax.lax.rsqrt(var + NORM_EPS).astype(o.dtype) * norm_w
        gate = (x @ Wg.T).reshape(B, T, H, DV)
        o = o * jax.nn.silu(gate)
        return o.reshape(B, T, H * DV) @ Wo.T

    def _L2_ffn_ref(x, ln_w, ff_ln_w, wq, wk, wv, wo, wg, w1, w3, w2):
        import jax, jax.numpy as jnp
        import numpy as np
        EPS = 1e-05
        ROPE_BASE = 150000.0
        NHEADS = 32
        KVHEADS = 8
        HEAD_DIM = 64
        TOP_K = 4

        def _rms(x, w):
            return x * jax.lax.rsqrt(jnp.mean(x * x, -1, keepdims=True) + EPS) * w

        def _rope(q, k):
            S, hd = (q.shape[1], q.shape[-1])
            half = hd // 2
            inv = 1.0 / ROPE_BASE ** (jnp.arange(half, dtype=jnp.float32) / half)
            ang = jnp.arange(S, dtype=jnp.float32)[:, None] * inv
            cos = jnp.concatenate([jnp.cos(ang), jnp.cos(ang)], -1)[None, :, None, :]
            sin = jnp.concatenate([jnp.sin(ang), jnp.sin(ang)], -1)[None, :, None, :]

            def rot(t):
                t1, t2 = (t[..., :half], t[..., half:])
                return jnp.concatenate([-t2, t1], -1)
            return (q * cos + rot(q) * sin, k * cos + rot(k) * sin)
        B, S, D = x.shape
        h = _rms(x, ln_w)
        q = (h @ wq).reshape(B, S, NHEADS, HEAD_DIM)
        k = (h @ wk).reshape(B, S, KVHEADS, HEAD_DIM)
        v = (h @ wv).reshape(B, S, KVHEADS, HEAD_DIM)
        q, k = _rope(q, k)
        g = NHEADS // KVHEADS
        k = jnp.repeat(k, g, axis=2)
        v = jnp.repeat(v, g, axis=2)
        scores = jnp.einsum('bqhd,bkhd->bhqk', q, k) / np.float32(np.sqrt(HEAD_DIM))
        causal = jnp.tril(jnp.ones((S, S), bool))
        scores = jnp.where(causal[None, None], scores, jnp.float32(-1e+30))
        attn = jax.nn.softmax(scores, -1)
        o = jnp.einsum('bhqk,bkhd->bqhd', attn, v).reshape(B, S, NHEADS * HEAD_DIM)
        x = x + o @ wo
        h = _rms(x, ff_ln_w)
        logits = h @ wg
        topv, topi = jax.lax.top_k(logits, TOP_K)
        gate = jax.nn.softmax(topv, -1)
        bidx = jnp.arange(B)[:, None, None]
        sidx = jnp.arange(S)[None, :, None]
        weights = jnp.zeros_like(logits).at[bidx, sidx, topi].set(gate)
        a = jax.nn.silu(jnp.einsum('bsd,edh->bseh', h, w1)) * jnp.einsum('bsd,edh->bseh', h, w3)
        y = jnp.einsum('bseh,ehd->bsed', a, w2)
        moe = jnp.einsum('bsed,bse->bsd', y, weights)
        return x + moe

    def _L3_attn_ref(Z_in, A_l, r_l, B_l, C_l):
        import jax, jax.numpy as jnp
        import numpy as np
        import math
        D = 32
        N = 256
        B = 8
        N_PLUS_1 = 256
        X = Z_in[:, :D, :]
        Y = Z_in[:, D:, :]
        U = jnp.einsum('ij,bjn->bin', B_l, X)
        W = jnp.einsum('ij,bjn->bin', C_l, X)
        scores = jnp.einsum('bdn,bdm->bnm', U, W)
        att = jax.nn.relu(scores)
        att = att.at[:, N_PLUS_1 - 1, N_PLUS_1 - 1].set(0.0)
        X_att = jnp.einsum('bdn,bnm->bdm', X, att)
        X_out = X + jnp.einsum('ij,bjm->bim', A_l, X_att)
        Y_out = Y + r_l * jnp.einsum('bdn,bnm->bdm', Y, att)
        return jnp.concatenate([X_out, Y_out], axis=1)

    def _L3_ffn_ref(x, Wr, Wg, Wu, Wd):
        import jax, jax.numpy as jnp
        import numpy as np
        B, T, D = (4, 256, 256)
        E = 8
        K = 2
        F = 1024 // (E // 2)
        probs = jax.nn.softmax(x @ Wr, axis=-1)
        topk_w, topk_idx = jax.lax.top_k(probs, K)
        topk_w = topk_w / jnp.sum(topk_w, axis=-1, keepdims=True)
        output = jnp.zeros_like(x)
        for i in range(E):
            sel = topk_idx == i
            w_i = jnp.sum(topk_w * sel.astype(x.dtype), axis=-1, keepdims=True)
            h = jax.nn.silu(x @ Wg[i]) * (x @ Wu[i])
            e_out = h @ Wd[i]
            output = output + w_i * e_out
        return output
    x = L0_attn_hidden_states
    x = x + 0.5 * _L0_ffn_ref(_layernorm(x, axis=-1), L0_ffn_wq_gate, L0_ffn_s_gate, L0_ffn_wq_up, L0_ffn_s_up, L0_ffn_wq_down, L0_ffn_s_down)
    x = x + _L0_attn_ref(_layernorm(x, axis=-1), L0_attn_Wq, L0_attn_Wk, L0_attn_Wv, L0_attn_Wo, L0_attn_v_emb0, L0_attn_v_emb1, L0_attn_tau)
    x = x + 0.5 * _L0_ffn_ref(_layernorm(x, axis=-1), L0_ffn_wq_gate, L0_ffn_s_gate, L0_ffn_wq_up, L0_ffn_s_up, L0_ffn_wq_down, L0_ffn_s_down)
    x = x + 0.5 * _L1_ffn_ref(_layernorm(x, axis=-1), L1_ffn_w_router, L1_ffn_we1, L1_ffn_we3, L1_ffn_we2, L1_ffn_ws1, L1_ffn_ws3, L1_ffn_ws2)
    x = x + _L1_attn_ref(_layernorm(x, axis=-1), L1_attn_A_log, L1_attn_x_proj_w, L1_attn_x_proj_b, L1_attn_dt_proj_w, L1_attn_dt_proj_b, L1_attn_out_proj_w, L1_attn_out_proj_b)
    x = x + 0.5 * _L1_ffn_ref(_layernorm(x, axis=-1), L1_ffn_w_router, L1_ffn_we1, L1_ffn_we3, L1_ffn_we2, L1_ffn_ws1, L1_ffn_ws3, L1_ffn_ws2)
    x = x + 0.5 * _L2_ffn_ref(_layernorm(x, axis=-1), L2_ffn_ln_w, L2_ffn_ff_ln_w, L2_ffn_wq, L2_ffn_wk, L2_ffn_wv, L2_ffn_wo, L2_ffn_wg, L2_ffn_w1, L2_ffn_w3, L2_ffn_w2)
    x = x + _L2_attn_ref(_layernorm(x, axis=-1), L2_attn_Wq, L2_attn_Wk, L2_attn_Wv, L2_attn_Wb, L2_attn_Wa, L2_attn_A_log, L2_attn_dt_bias, L2_attn_conv_wq, L2_attn_conv_wk, L2_attn_conv_wv, L2_attn_Wg, L2_attn_norm_w, L2_attn_Wo)
    x = x + 0.5 * _L2_ffn_ref(_layernorm(x, axis=-1), L2_ffn_ln_w, L2_ffn_ff_ln_w, L2_ffn_wq, L2_ffn_wk, L2_ffn_wv, L2_ffn_wo, L2_ffn_wg, L2_ffn_w1, L2_ffn_w3, L2_ffn_w2)
    x = x + 0.5 * _L3_ffn_ref(_layernorm(x, axis=-1), L3_ffn_Wr, L3_ffn_Wg, L3_ffn_Wu, L3_ffn_Wd)
    x = x + _L3_attn_ref(_layernorm(x, axis=-1), L3_attn_A_l, L3_attn_r_l, L3_attn_B_l, L3_attn_C_l)
    x = x + 0.5 * _L3_ffn_ref(_layernorm(x, axis=-1), L3_ffn_Wr, L3_ffn_Wg, L3_ffn_Wu, L3_ffn_Wd)
    return x

_drawn_inputs = setup_inputs


def setup_inputs(seed=0):
    import zlib

    import numpy as np

    out = dict(_drawn_inputs(seed))
    spreads = {'L0_attn_v_emb0': (-9.999999747378752e-06, 0.6),
     'L0_attn_v_emb1': (9.999999747378752e-06, 0.6),
     'L1_attn_x_proj_b': (0.0, 0.1),
     'L1_attn_out_proj_b': (0.0, 0.1),
     'L2_attn_norm_w': (1.0, 0.2),
     'L2_ffn_ln_w': (1.0, 0.6),
     'L2_ffn_ff_ln_w': (1.0, 0.6)}
    factors = {'L0_attn_Wq': 64.0,
     'L0_attn_Wk': 64.0,
     'L0_attn_Wv': 64.0,
     'L0_attn_Wo': 64.0,
     'L0_ffn_s_gate': 3.853,
     'L0_ffn_s_up': 4.879,
     'L2_attn_dt_bias': 8.0,
     'L2_ffn_wq': 8.0,
     'L2_ffn_wk': 8.0,
     'L2_ffn_wg': 8.0,
     'L2_ffn_w1': 8.0,
     'L2_ffn_w3': 8.0,
     'L2_ffn_w2': 8.0}
    for name, (base, spread) in spreads.items():
        noise = np.random.default_rng([zlib.crc32(name.encode()), seed]).standard_normal(out[name].shape)
        drawn = base * np.exp(spread * noise) if base else spread * noise
        out[name] = jnp.asarray(drawn.astype(out[name].dtype))
    for name, factor in factors.items():
        out[name] = (out[name] * factor).astype(out[name].dtype)
    return out
```

```python
from contextlib import ExitStack

import concourse.bass as bass
import numpy as np
from concourse import mybir

F32 = mybir.dt.float32
I32 = mybir.dt.int32
ALU = mybir.AluOpType
ACT = mybir.ActivationFunctionType
AX = mybir.AxisListType

P = 128
T = 1024
D = 256
NT = T // P
KD = D // P
HALF = 512
NH = T // HALF
LN_EPS = 1e-5
MASKED = -1e30
STAGES = ("l0f", "l0a", "l0f", "l1f", "l1a", "l1f", "l2f", "l2a", "l2f", "l3f", "l3a", "l3f")


class Core:

    def __init__(self, nc, dram):
        self.nc, self.dram = nc, dram
        self.n = 0


class Stage:

    def __init__(self, core):
        self.nc = core.nc
        core.n += 1
        self.tag = f"_{core.n}"
        self.stack = ExitStack()
        self.sems = []

    def sb(self, name, shape, dt=F32):
        return self.stack.enter_context(self.nc.sbuf_tensor(name + self.tag, shape, dt))

    def ps(self, name, shape):
        return self.stack.enter_context(self.nc.psum_tensor(name + self.tag, shape, F32))

    def sem(self, name):
        s = self.nc.alloc_semaphore(name + self.tag)
        self.sems.append(s)
        return s

    def block(self):
        return self.nc.Block()

    def close(self):
        numbers = sorted(s.num for s in self.sems)
        while numbers:
            last = first = numbers[0]
            while last in numbers:
                numbers.remove(last)
                last += 1
            self.nc.all_engine_barrier(sems_to_clear=range(first, last))
        for s in self.sems:
            self.nc.release_semaphore(s)
        self.stack.close()


def chain(engine, semaphore, start=0):
    count = [start]

    def link(instruction):
        count[0] += 1
        instruction.then_inc(semaphore, 1)
        engine.wait_ge(semaphore, count[0])

    return link


def load_residual(core):
    nc, s = core.nc, Stage(core)
    loaded = s.sem("x_loaded")
    const_loaded = s.sem("ident_loaded")
    with s.block() as block:
        @block.sync
        def _(sp):
            sp.dma_start(core.x[:], core.dram["x"].rearrange("(t p) d -> p t d", p=P)).then_inc(loaded, 16)
            sp.wait_ge(loaded, 16)

        @block.scalar
        def _(act):
            act.dma_start(core.ident[:], core.dram["ident"]).then_inc(const_loaded, 16)
            act.wait_ge(const_loaded, 16)
    s.close()


def store_residual(core):
    nc, s = core.nc, Stage(core)
    stored = s.sem("out_stored")
    with s.block() as block:
        @block.sync
        def _(sp):
            sp.dma_start(core.dram["out"].rearrange("(t p) d -> p t d", p=P), core.x[:]).then_inc(stored, 16)
            sp.wait_ge(stored, 16)
    s.close()


def layernorm(core, weight=None, source=None, keep=True, transpose=True):
    nc, s = core.nc, Stage(core)
    x, xn, xnT, ident = core.x, core.xn, core.xnT, core.ident
    stats = s.sb("stats", [P, NT, 6])
    mv = s.sb("mean_var", [P, NT, 2])
    std = s.sb("std", [P, NT])
    rstd = s.sb("rstd", [P, NT])
    psT = s.ps("psT", [P, KD, NH, HALF])
    dve_step = s.sem("dve_step")
    var_ready = s.sem("var_ready")
    std_ready = s.sem("std_ready")
    rows_ready = s.sem("rows_ready")
    bank_ready = s.sem("bank_ready")
    rms = weight is not None
    if rms:
        sq = s.sb("squares", [P, D])
        h = s.sb("h", [P, NT, D])
        ms = s.sb("mean_square", [P, NT])
        wcol = s.sb("wcol", [P, KD])
        w_loaded = s.sem("w_loaded")
        ms_ready = s.sem("ms_ready")
        act_step = s.sem("act_step")
        rms_ready = s.sem("rms_std_ready")
    rows = h if rms else xn
    base = xn if source is None else source
    with s.block() as block:
        @block.sync
        def _(sp):
            if rms:
                sp.dma_start(wcol[:], core.dram[weight]).then_inc(w_loaded, 16)

        @block.vector
        def _(dve):
            link = chain(dve, dve_step)
            if source is None:
                for t in range(NT):
                    last = nc.vector.bn_stats(stats[:, t, :], x[:, t, :])
                link(last)
                for t in range(NT):
                    last = nc.vector.bn_aggr(mv[:, t, :], stats[:, t, :])
                last.then_inc(var_ready, 1)
                dve.wait_ge(std_ready, 1)
                link(nc.vector.reciprocal(rstd[:], std[:]))
                for t in range(NT):
                    last = nc.vector.tensor_scalar(xn[:, t, :], x[:, t, :], mv[:, t, 0:1], rstd[:, t:t + 1],
                                                   ALU.subtract, ALU.mult)
                    if not rms:
                        last.then_inc(rows_ready, 1)
                if rms:
                    last.then_inc(ms_ready, 1)
            if rms:
                dve.wait_ge(rms_ready, 1)
                link(nc.vector.reciprocal(rstd[:], std[:]))
                for t in range(NT):
                    nc.vector.tensor_scalar(h[:, t, :], base[:, t, :], rstd[:, t:t + 1], None,
                                            ALU.mult).then_inc(rows_ready, 1)

        @block.scalar
        def _(act):
            if source is None:
                act.wait_ge(var_ready, 1)
                nc.scalar.activation(std[:], mv[:, :, 1], ACT.Sqrt, bias=core.eps[:, 0:1]).then_inc(std_ready, 1)
            if rms:
                if source is None:
                    act.wait_ge(ms_ready, 1)
                link = chain(act, act_step)
                for t in range(NT):
                    last = nc.scalar.activation(sq[:], base[:, t, :], ACT.Square, accum_out=ms[:, t:t + 1])
                    link(last)
                nc.scalar.activation(std[:], ms[:], ACT.Sqrt, bias=core.eps[:, 0:1],
                                     scale=1.0 / D).then_inc(rms_ready, 1)
                act.wait_ge(w_loaded, 16)
            for k in range(KD):
                for half in range(NH):
                    act.wait_ge(bank_ready, k * NH + half + 1)
                    nc.scalar.activation(xnT[:, k, half * HALF:(half + 1) * HALF], psT[:, k, half, :], ACT.Copy,
                                         scale=wcol[:, k:k + 1] if rms else 1.0)

        @block.tensor
        def _(pe):
            for k in range(KD):
                for t in range(NT):
                    if k == 0:
                        pe.wait_ge(rows_ready, t + 1)
                    last = nc.tensor.transpose(psT[:, k, t // 4, (t % 4) * P:(t % 4 + 1) * P],
                                               rows[:, t, k * P:(k + 1) * P], ident[:])
                    if t % 4 == 3:
                        last.then_inc(bank_ready, 1)
    s.close()


def route(core, router, experts, top, gain, rest=0, rest_gain=0.0):
    nc, s = core.nc, Stage(core)
    xnT, ident = core.xnT, core.ident
    wr = s.sb("w_router", [P, KD, experts])
    lg = s.sb("logits", [P, NT, experts])
    top8 = s.sb("top8", [P, NT, 8])
    key8 = s.sb("key8", [P, NT, 8])
    cut = s.sb("cut", [P, NT, experts])
    kept = s.sb("kept", [P, NT, experts])
    ex = s.sb("exps", [P, NT, experts])
    den = s.sb("den", [P, NT])
    rden = s.sb("rden", [P, NT])
    gT = s.sb("gatesT", [32, T])
    restrow = s.sb("rest_rows", [max(rest, 1), T])
    psL = s.ps("psL", [P, NT, 64])
    psG = s.ps("psG", [P, NH, HALF])
    w_loaded, logits, rel, exps, gates, gT_ps, gT_sb, stored = (s.sem(n) for n in (
        "w_loaded", "logits_ready", "shifted_ready", "exps_ready", "gates_ready", "gatesT_psum", "gatesT_sbuf",
        "gates_stored"))
    dve_step, rest_set, rest_stored = s.sem("dve_step"), s.sem("rest_set"), s.sem("rest_stored")
    rows = core.gates
    with s.block() as block:
        @block.sync
        def _(sp):
            sp.dma_start(wr[:], core.dram[router]).then_inc(w_loaded, 16)
            if rest:
                sp.wait_ge(rest_set, 1)
                sp.dma_start(rows[experts:experts + rest, :], restrow[:]).then_inc(rest_stored, 16)
                sp.wait_ge(rest_stored, 16)
            sp.wait_ge(gT_sb, NH)
            sp.dma_start(rows[0:experts, :], gT[0:experts, :]).then_inc(stored, 16)
            sp.wait_ge(stored, 16)

        @block.tensor
        def _(pe):
            pe.wait_ge(w_loaded, 16)
            for t in range(NT):
                for k in range(KD):
                    last = nc.tensor.matmul(psL[:, t, 0:experts], xnT[:, k, t * P:(t + 1) * P], wr[:, k, :],
                                            start=k == 0, stop=k == KD - 1)
            last.then_inc(logits, 1)
            pe.wait_ge(gates, 1)
            for t in range(NT):
                last = nc.tensor.transpose(psG[0:experts, t // 4, (t % 4) * P:(t % 4 + 1) * P], ex[:, t, :],
                                           ident[:])
                if t % 4 == 3:
                    last.then_inc(gT_ps, 1)

        @block.vector
        def _(dve):
            link = chain(dve, dve_step)
            if rest:
                nc.vector.memset(restrow[:], rest_gain).then_inc(rest_set, 1)
            dve.wait_ge(logits, 1)
            link(nc.vector.tensor_copy(lg[:], psL[:, :, 0:experts]))
            for t in range(NT):
                last = nc.vector.max(top8[:, t, :], lg[:, t, :])
            link(last)
            nc.vector.tensor_tensor(lg[:], lg[:], top8[:, :, 0:1].to_broadcast([P, NT, experts]),
                                    ALU.subtract).then_inc(rel, 1)
            link(nc.vector.memset(key8[:], -3e38))
            link(nc.vector.tensor_tensor(key8[:, :, 0:top], top8[:, :, 0:top],
                                         top8[:, :, 0:1].to_broadcast([P, NT, top]), ALU.subtract))
            dve.wait_ge(rel, 1)
            for t in range(NT):
                last = nc.vector.match_replace(cut[:, t, :], key8[:, t, :], lg[:, t, :], 1.0)
            link(last)
            link(nc.vector.tensor_scalar(kept[:], cut[:], 1.0, None, ALU.is_equal))
            dve.wait_ge(exps, 1)
            link(nc.vector.tensor_tensor(kept[:], kept[:], ex[:], ALU.mult))
            link(nc.vector.tensor_reduce(den[:], kept[:], AX.X, ALU.add))
            link(nc.vector.reciprocal(rden[:], den[:]))
            link(nc.vector.tensor_scalar(rden[:], rden[:], gain, None, ALU.mult))
            nc.vector.tensor_tensor(ex[:], kept[:], rden[:].unsqueeze(2).to_broadcast([P, NT, experts]),
                                    ALU.mult).then_inc(gates, 1)

        @block.scalar
        def _(act):
            act.wait_ge(rel, 1)
            nc.scalar.activation(ex[:], lg[:], ACT.Exp).then_inc(exps, 1)
            for half in range(NH):
                act.wait_ge(gT_ps, half + 1)
                nc.scalar.activation(gT[0:experts, half * HALF:(half + 1) * HALF], psG[0:experts, half, :],
                                     ACT.Copy).then_inc(gT_sb, 1)
    s.close()


def gated_ffn(core, weights, chunks, gates_per_pair):
    nc, s = core.nc, Stage(core)
    x, xnT = core.x, core.xnT
    quant = gates_per_pair == 0
    iters = chunks // 2
    W = 3 * D
    slots = chunks if quant else 2
    wt = s.sb("weights", [P, slots, W])
    act_s = s.sb("silu", [P, 2, HALF])
    hid = s.sb("hidden", [P, 2, HALF])
    zero = s.sb("zeros", [1, HALF])
    if quant:
        raw = s.sb("raw_weights", [P, slots, W], I32)
        sgu = s.sb("scales_gate_up", [P, 2, chunks])
        sdn = s.sb("scales_down", [P, HALF])
        scaled = s.sb("scaled", [P, 4, HALF])
    else:
        gate = s.sb("gates", [P, 2, T])
        prod = s.sb("prod", [P, 2, HALF])
    psU = s.ps("psUp", [P, 2, 2, HALF])
    psD = s.ps("psDown", [P, 4, HALF])
    w_loaded = [s.sem(f"w_loaded{j}") for j in range(slots)]
    g_loaded = [s.sem(f"gate_loaded{j}") for j in range(2)]
    scales_loaded, scales2_loaded = s.sem("scales_loaded"), s.sem("scales2_loaded")
    w_ready, zero_set = s.sem("w_ready"), s.sem("zero_set")
    up_done, silu_done, prod_done, hid_done, down_done = (s.sem(n) for n in (
        "up_done", "silu_done", "prod_done", "hid_done", "down_done"))
    dve_step = s.sem("dve_step")

    def loop(engine, body):
        body(0, True, False)
        if quant:
            for i in range(1, iters - 1):
                body(i, False, False)
        else:
            with engine.Fori(1, iters - 1) as i:
                body(i, False, False)
        body(iters - 1, False, True)

    with s.block() as block:
        @block.sync
        def _(sp):
            if quant:
                for c in range(chunks):
                    sp.dma_start(raw[:, c, :], core.dram[weights][c]).then_inc(w_loaded[c], 16)
                    if c == 0:
                        sp.dma_start(sgu[:], core.dram["l0_scales"]).then_inc(scales_loaded, 16)
                sp.dma_start(sdn[:], core.dram["l0_scale_down"]).then_inc(scales2_loaded, 16)
                return

            def body(i, first, last):
                for j in range(2):
                    if not first:
                        sp.wait_ge(down_done, 4 * i + 2 * j - 2)
                    sp.dma_start(wt[:, j, :], core.dram[weights][2 * i + j]).then_inc(w_loaded[j], 16)
                    if not first:
                        sp.wait_ge(hid_done, 4 * i + 2 * j - 2)
                    row = i if gates_per_pair == 1 else 2 * i + j
                    sp.dma_start(gate[:, j, :],
                                 core.gates[bass.ds(row, 1), :].to_broadcast([P, T])).then_inc(g_loaded[j], 16)
            loop(sp, body)

        @block.gpsimd
        def _(pool):
            if quant:
                for c in range(chunks):
                    pool.wait_ge(w_loaded[c], 16)
                    nc.gpsimd.tensor_scalar(wt[:, c, :], raw[:, c, :], -128.0, None, ALU.add).then_inc(w_ready, 1)

        @block.tensor
        def _(pe):
            pe.wait_ge(zero_set, 1)
            for b in range(4):
                nc.tensor.matmul(psD[:, b, :], zero[:, 0:P], zero[:], start=True, stop=False)

            def up(i, u, first):
                j, half = u // 2, u % 2
                if quant:
                    if half == 0:
                        pe.wait_ge(w_ready, 2 * i + j + 1)
                elif half == 0:
                    pe.wait_ge(w_loaded[j], 16 * i + 16)
                if not (first and u < 2):
                    pe.wait_ge(hid_done, 4 * i + u - 1)
                slot = 2 * i + j if quant else j
                for g in range(2):
                    for k in range(KD):
                        last = nc.tensor.matmul(
                            psU[:, u % 2, g, :], wt[:, slot, g * D + k * P:g * D + (k + 1) * P],
                            xnT[:, k, half * HALF:(half + 1) * HALF], start=k == 0, stop=k == KD - 1)
                last.then_inc(up_done, 1)

            def down(i, u, closing=False):
                j, half = u // 2, u % 2
                pe.wait_ge(hid_done, 4 * i + u + 1)
                slot = 2 * i + j if quant else j
                for q in range(4):
                    t = half * 4 + q
                    last = nc.tensor.matmul(
                        psD[:, t // 2, (t % 2) * D:(t % 2 + 1) * D], hid[:, u % 2, q * P:(q + 1) * P],
                        wt[:, slot, 2 * D:3 * D], start=False, stop=closing and q % 2 == 1)
                last.then_inc(down_done, 1)

            def body(i, first, last):
                for u in range(4):
                    up(i, u, first)
                    if u:
                        down(i, u - 1, last and u == 3)
                    elif not first:
                        down(i - 1, 3)
                if last:
                    down(i, 3, True)
            loop(pe, body)

        @block.scalar
        def _(act):
            if quant:
                act.wait_ge(scales_loaded, 16)

            def body(i, first, last):
                for u in range(4):
                    act.wait_ge(up_done, 4 * i + u + 1)
                    if not (first and u < 2):
                        act.wait_ge(hid_done, 4 * i + u - 1)
                    c = 2 * i + u // 2
                    nc.scalar.activation(act_s[:, u % 2, :], psU[:, u % 2, 0, :], ACT.Silu,
                                         scale=sgu[:, 0, c:c + 1] if quant else 1.0).then_inc(silu_done, 1)
            loop(act, body)

        @block.vector
        def _(dve):
            nc.vector.memset(zero[:], 0.0).then_inc(zero_set, 1)
            if quant:
                dve.wait_ge(scales_loaded, 16)

            def body(i, first, last):
                for u in range(4):
                    j, half = u // 2, u % 2
                    dve.wait_ge(silu_done, 4 * i + u + 1)
                    if not (first and u < 2):
                        dve.wait_ge(down_done, 4 * i + u - 1)
                    if quant:
                        c = 2 * i + j
                        nc.vector.scalar_tensor_tensor(hid[:, u % 2, :], psU[:, u % 2, 1, :], sgu[:, 1, c:c + 1],
                                                       act_s[:, u % 2, :], ALU.mult, ALU.mult).then_inc(hid_done, 1)
                        continue
                    nc.vector.tensor_tensor(prod[:, u % 2, :], psU[:, u % 2, 1, :], act_s[:, u % 2, :],
                                            ALU.mult).then_inc(prod_done, 1)
                    if half == 0:
                        dve.wait_ge(g_loaded[j], 16 * i + 16)
                    dve.wait_ge(prod_done, 4 * i + u + 1)
                    nc.vector.tensor_tensor(hid[:, u % 2, :], prod[:, u % 2, :],
                                            gate[:, j, half * HALF:(half + 1) * HALF],
                                            ALU.mult).then_inc(hid_done, 1)
            loop(dve, body)
            dve.wait_ge(down_done, 4 * iters)
            if quant:
                dve.wait_ge(scales2_loaded, 16)
            xb = x[:, :, :].rearrange("p (b t) d -> p b (t d)", b=4)
            link = chain(dve, dve_step)
            if quant:
                for b in range(4):
                    last = nc.vector.tensor_tensor(scaled[:, b, :], psD[:, b, :], sdn[:], ALU.mult)
                link(last)
            for b in range(4):
                nc.vector.scalar_tensor_tensor(xb[:, b, :], scaled[:, b, :] if quant else psD[:, b, :], 0.5,
                                               xb[:, b, :], ALU.mult, ALU.add)
    s.close()


def l3_attention(core):
    nc, s = core.nc, Stage(core)
    x, xn, xnT = core.x, core.xn, core.xnT
    R = 32
    mats = s.sb("abc_transposed", [R, 3, R])
    rcol = s.sb("r", [P, 1])
    mask = s.sb("mask", [P, KD, D])
    uw = s.sb("uw", [R, 2, D])
    att = s.sb("att", [P, KD, D])
    xatt = s.sb("xatt", [R, D])
    add = s.sb("add", [P, NT, D])
    psU = s.ps("psUW", [R, 2, D])
    psS = s.ps("psS", [P, KD, D])
    psZ = s.ps("psZ", [P, NT, D])
    psA = s.ps("psA", [R, HALF])
    loads = [s.sem(n) for n in ("mats_loaded", "r_loaded", "mask_loaded")]
    uw_ps, uw_sb, scores, relus, att_ready, z_ps, xatt_sb, ax_ps, dve_step = (s.sem(n) for n in (
        "uw_psum", "uw_sbuf", "scores_ready", "relu_ready", "att_ready", "zatt_ready", "xatt_sbuf", "ax_psum",
        "dve_step"))
    with s.block() as block:
        @block.sync
        def _(sp):
            for sb, name, sem in zip((mats, rcol, mask), ("l3_abc", "l3_r", "l3_mask"), loads):
                sp.dma_start(sb[:], core.dram[name]).then_inc(sem, 16)

        @block.tensor
        def _(pe):
            pe.wait_ge(loads[0], 16)
            for m in range(2):
                last = nc.tensor.matmul(psU[:, m, :], mats[:, 1 + m, :], xn[0:R, 0, :], start=True, stop=True)
            last.then_inc(uw_ps, 1)
            pe.wait_ge(uw_sb, 1)
            for k in range(KD):
                last = nc.tensor.matmul(psS[:, k, :], uw[:, 0, k * P:(k + 1) * P], uw[:, 1, :], start=True,
                                        stop=True)
            last.then_inc(scores, 1)
            pe.wait_ge(att_ready, 1)
            for t in range(NT):
                for k in range(KD):
                    last = nc.tensor.matmul(psZ[:, t, :], xnT[:, k, t * P:(t + 1) * P], att[:, k, :],
                                            start=k == 0, stop=k == KD - 1)
                last.then_inc(z_ps, 1)
            pe.wait_ge(xatt_sb, 1)
            nc.tensor.matmul(psA[:, 0:D], mats[:, 0, :], xatt[:], start=True, stop=True).then_inc(ax_ps, 1)

        @block.scalar
        def _(act):
            act.wait_ge(uw_ps, 1)
            nc.scalar.activation(uw[:], psU[:], ACT.Copy).then_inc(uw_sb, 1)
            act.wait_ge(scores, 1)
            nc.scalar.activation(att[:], psS[:], ACT.Relu).then_inc(relus, 1)
            act.wait_ge(z_ps, 2)
            nc.scalar.activation(xatt[:], psZ[0:R, 0, :], ACT.Copy).then_inc(xatt_sb, 1)

        @block.vector
        def _(dve):
            link = chain(dve, dve_step)
            dve.wait_ge(loads[2], 16)
            dve.wait_ge(relus, 1)
            nc.vector.tensor_tensor(att[:], att[:], mask[:], ALU.mult).then_inc(att_ready, 1)
            dve.wait_ge(loads[1], 16)
            dve.wait_ge(xatt_sb, 1)
            for t in range(NT):
                dve.wait_ge(z_ps, t // 2 * 2 + 2)
                last = nc.vector.scalar_tensor_tensor(add[:, t, :], psZ[:, t, :], rcol[:, 0:1], xn[:, t, :],
                                                      ALU.mult, ALU.add)
            link(last)
            dve.wait_ge(ax_ps, 1)
            link(nc.vector.tensor_tensor(add[0:R, 0, :], psA[:, 0:D], xn[0:R, 0, :], ALU.add))
            nc.vector.tensor_tensor(x[:], x[:], add[:], ALU.add)
    s.close()


def l1_scan(core):
    nc, s = core.nc, Stage(core)
    x, xnT, ident = core.x, core.xnT, core.ident
    N = 16
    wdt = s.sb("w_dt", [P, KD, D])
    wbc = s.sb("w_bc", [P, KD, 2 * N])
    wout = s.sb("w_out", [P, KD, D])
    dtb = s.sb("b_dt", [P, KD])
    bcb = s.sb("b_bc", [2 * N, 1])
    outb = s.sb("b_out", [P, D])
    alog = s.sb("a_log", [P, KD, N])
    nega = s.sb("neg_a", [P, KD, N])
    acol = s.sb("a_column", [P, 2, KD])
    za = s.sb("z_abs", [P, KD, T])
    zr = s.sb("z_relu", [P, KD, T])
    dt = s.sb("dt", [P, KD, T])
    dtx = s.sb("dtx", [P, KD, T])
    bcT = s.sb("bcT", [2 * N, T])
    bcast = s.sb("bc_broadcast", [P, 2, 2, T])
    da = s.sb("decay", [P, 2, T])
    dbx = s.sb("dbx", [P, 2, T])
    hs = s.sb("states", [P, 2, T])
    hc = s.sb("states_c", [P, 2, T])
    yT = s.sb("yT", [P, KD, T])
    zero = s.sb("zeros", [1, HALF])
    psP = s.ps("psP", [P, 4, HALF])
    psY = s.ps("psY", [P, KD, NH, HALF])
    outs = zr[:, :, :].rearrange("p k (t d) -> p (k t) d", d=D)
    biased = s.sem("biased")
    names = ("l1_wdt", "l1_wbc", "l1_wout", "l1_bdt", "l1_bbc", "l1_bout", "l1_alog")
    loads = {n: s.sem(n + "_loaded") for n in names}
    zero_set, dt_ps, dt_free, abs_done, relu_done, exp_done, ln_done, dt_done, dtx_done = (s.sem(n) for n in (
        "zero_set", "dt_psum", "dt_psum_read", "abs_done", "relu_done", "exp_done", "ln_done", "dt_done",
        "dtx_done"))
    bc_ps, bc_sb, bc_stored, aexp, nega_done = (s.sem(n) for n in (
        "bc_psum", "bc_sbuf", "bc_stored", "a_exp_done", "neg_a_done"))
    b_loaded = [s.sem(f"b_row_loaded{j}") for j in range(2)]
    c_loaded = [s.sem(f"c_row_loaded{j}") for j in range(2)]
    col_done, da_done, dbx_done, scan_done, hc_done, y_added, y_sb, out_ps = (s.sem(n) for n in (
        "a_column_done", "decay_done", "dbx_done", "scan_done", "hc_done", "y_added", "yT_sbuf", "out_psum"))

    def loop(engine, body):
        body(0, True, False)
        with engine.Fori(1, N // 2 - 1) as i:
            body(i, False, False)
        body(N // 2 - 1, False, True)

    with s.block() as block:
        @block.sync
        def _(sp):
            for sb, n in zip((wdt, wbc, wout, dtb, bcb, outb, alog), names):
                sp.dma_start(sb[:], core.dram[n]).then_inc(loads[n], 16)
            sp.wait_ge(bc_sb, NH)
            sp.dma_start(core.bc_rows, bcT[:]).then_inc(bc_stored, 16)
            sp.wait_ge(bc_stored, 16)

            def body(i, first, last):
                for j in range(2):
                    if not first:
                        sp.wait_ge(dbx_done, 4 * i + 2 * j - 2)
                    sp.dma_start(bcast[:, j, 0, :],
                                 core.bc_rows[bass.ds(2 * i + j, 1), :].to_broadcast([P, T])).then_inc(b_loaded[j], 16)
                    if not first:
                        sp.wait_ge(hc_done, 4 * i + 2 * j - 2)
                    sp.dma_start(bcast[:, j, 1, :],
                                 core.bc_rows[bass.ds(N + 2 * i + j, 1), :].to_broadcast([P, T])).then_inc(c_loaded[j], 16)
            loop(sp, body)

        @block.tensor
        def _(pe):
            pe.wait_ge(loads["l1_wbc"], 16)
            for half in range(NH):
                for k in range(KD):
                    last = nc.tensor.matmul(psP[0:2 * N, half, :], wbc[:, k, :],
                                            xnT[:, k, half * HALF:(half + 1) * HALF], start=k == 0, stop=k == KD - 1)
                last.then_inc(bc_ps, 1)
            pe.wait_ge(loads["l1_wdt"], 16)
            for c in range(KD):
                for half in range(NH):
                    b = 2 + half
                    if c:
                        pe.wait_ge(dt_free, 2 * half + 2)
                    for k in range(KD):
                        last = nc.tensor.matmul(psP[:, b, :], wdt[:, k, c * P:(c + 1) * P],
                                                xnT[:, k, half * HALF:(half + 1) * HALF],
                                                start=k == 0, stop=k == KD - 1)
                    last.then_inc(dt_ps, 1)
            pe.wait_ge(zero_set, 1)
            for c in range(KD):
                for half in range(NH):
                    nc.tensor.matmul(psY[:, c, half, :], zero[:, 0:P], zero[:], start=True, stop=False)

            def body(i, first, last):
                for u in range(4):
                    pe.wait_ge(hc_done, 4 * i + u + 1)
                    for half in range(NH):
                        add = nc.tensor.matmul(psY[:, u % 2, half, :], ident[:],
                                               hc[:, u % 2, half * HALF:(half + 1) * HALF],
                                               start=False, stop=last and u >= 2)
                    add.then_inc(y_added, 1)
            loop(pe, body)
            pe.wait_ge(y_sb, KD * NH)
            pe.wait_ge(loads["l1_wout"], 16)
            for t in range(NT):
                for k in range(KD):
                    last = nc.tensor.matmul(psP[:, t // 2, (t % 2) * D:(t % 2 + 1) * D], yT[:, k, t * P:(t + 1) * P],
                                            wout[:, k, :], start=k == 0, stop=k == KD - 1)
                last.then_inc(out_ps, 1)

        @block.scalar
        def _(act):
            act.wait_ge(loads["l1_bbc"], 16)
            for half in range(NH):
                act.wait_ge(bc_ps, half + 1)
                nc.scalar.activation(bcT[:, half * HALF:(half + 1) * HALF], psP[0:2 * N, half, :], ACT.Identity,
                                     bias=bcb[:, 0:1]).then_inc(bc_sb, 1)
            act.wait_ge(loads["l1_bdt"], 16)
            for c in range(KD):
                for half in range(NH):
                    act.wait_ge(dt_ps, 2 * c + half + 1)
                    to = slice(half * HALF, (half + 1) * HALF)
                    nc.scalar.activation(za[:, c, to], psP[:, 2 + half, :], ACT.Abs, bias=dtb[:, c:c + 1]).then_inc(abs_done, 1)
                    nc.scalar.activation(zr[:, c, to], psP[:, 2 + half, :], ACT.Relu, bias=dtb[:, c:c + 1]).then_inc(dt_free, 2)
            act.wait_ge(loads["l1_alog"], 16)
            nc.scalar.activation(nega[:], alog[:], ACT.Exp).then_inc(aexp, 1)
            act.wait_ge(abs_done, 4)
            act.wait_ge(dt_free, 8)
            nc.scalar.activation(dtx[:], za[:], ACT.Exp, scale=-1.0).then_inc(exp_done, 1)
            act.wait_ge(exp_done, 1)
            nc.scalar.activation(za[:], dtx[:], ACT.Ln, bias=1.0).then_inc(ln_done, 1)

            def body(i, first, last):
                for u in range(4):
                    j, c = u // 2, u % 2
                    if c == 0:
                        act.wait_ge(col_done, 2 * i + j + 1)
                    if not (first and u < 2):
                        act.wait_ge(scan_done, 4 * i + u - 1)
                    elif u == 0:
                        act.wait_ge(dt_done, 1)
                    nc.scalar.activation(da[:, c, :], dt[:, c, :], ACT.Exp,
                                         scale=acol[:, j, c:c + 1]).then_inc(da_done, 1)
            loop(act, body)
            act.wait_ge(y_added, 2 * N)
            for c in range(KD):
                for half in range(NH):
                    nc.scalar.activation(yT[:, c, half * HALF:(half + 1) * HALF], psY[:, c, half, :],
                                         ACT.Copy).then_inc(y_sb, 1)

        @block.gpsimd
        def _(pool):
            pool.wait_ge(dtx_done, 1)

            def body(i, first, last):
                for u in range(4):
                    j, c = u // 2, u % 2
                    if c == 0:
                        pool.wait_ge(b_loaded[j], 16 * i + 16)
                    if not (first and u < 2):
                        pool.wait_ge(scan_done, 4 * i + u - 1)
                    nc.gpsimd.tensor_tensor(dbx[:, c, :], dtx[:, c, :], bcast[:, j, 0, :],
                                            ALU.mult).then_inc(dbx_done, 1)
            loop(pool, body)

        @block.vector
        def _(dve):
            nc.vector.memset(zero[:], 0.0).then_inc(zero_set, 1)
            dve.wait_ge(aexp, 1)
            nc.vector.tensor_scalar(nega[:], nega[:], -1.0, None, ALU.mult).then_inc(nega_done, 1)
            dve.wait_ge(ln_done, 1)
            nc.vector.tensor_tensor(dt[:], za[:], zr[:], ALU.add).then_inc(dt_done, 1)
            dve.wait_ge(dt_done, 1)
            nc.vector.tensor_tensor(dtx[:], dt[:], xnT[:], ALU.mult).then_inc(dtx_done, 1)
            dve.wait_ge(nega_done, 1)

            def body(i, first, last):
                for u in range(4):
                    j, c = u // 2, u % 2
                    if c == 0:
                        if not first:
                            dve.wait_ge(da_done, 4 * i + 2 * j - 2)
                        nc.vector.tensor_copy(acol[:, j, :], nega[:, :, bass.ds(2 * i + j, 1)].rearrange(
                            "p k o -> p (k o)")).then_inc(col_done, 1)
                    dve.wait_ge(da_done, 4 * i + u + 1)
                    dve.wait_ge(dbx_done, 4 * i + u + 1)
                    nc.vector.tensor_tensor_scan(hs[:, c, :], da[:, c, :], dbx[:, c, :], 0.0, ALU.mult,
                                                 ALU.add).then_inc(scan_done, 1)
                    dve.wait_ge(scan_done, 4 * i + u + 1)
                    if c == 0:
                        dve.wait_ge(c_loaded[j], 16 * i + 16)
                    if not (first and u < 2):
                        dve.wait_ge(y_added, 4 * i + u - 1)
                    nc.vector.tensor_tensor(hc[:, c, :], hs[:, c, :], bcast[:, j, 1, :], ALU.mult).then_inc(hc_done, 1)
            loop(dve, body)
            dve.wait_ge(loads["l1_bout"], 16)
            for t in range(NT):
                dve.wait_ge(out_ps, t // 2 * 2 + 2)
                nc.vector.tensor_tensor(outs[:, t, :], psP[:, t // 2, (t % 2) * D:(t % 2 + 1) * D],
                                        outb[:], ALU.add).then_inc(biased, 1)
            dve.wait_ge(biased, NT)
            nc.vector.tensor_tensor(x[:], x[:], outs, ALU.add)
    s.close()


class GroupAttention:

    UNITS = 4 * NT

    def __init__(self, s, nc, ident, rows, dv, mask, fix_first=None):
        self.nc, self.ident, self.rows, self.dv, self.mask, self.fix_first = nc, ident, rows, dv, mask, fix_first
        self.qT = s.sb("qT", [P, 2, T])
        self.kT = s.sb("kT", [P, T])
        self.v = s.sb("v_group", [P, NT, dv])
        self.o = s.sb("o_group", [P, NT, 4 * dv])
        self.p = s.sb("probs", [P, 2, T])
        self.pT = s.sb("probsT", [P, 2, NT, P])
        self.negmax = s.sb("neg_max", [P, self.UNITS])
        self.rowsum = s.sb("row_sum", [P, self.UNITS])
        self.rinv = s.sb("row_inverse", [P, self.UNITS])
        self.psS = s.ps("psS", [P, 2, 2, HALF])
        self.psT = s.ps("psT", [P, 2, HALF])
        self.psO = s.ps("psO", [P, 2, HALF])
        self.scored, self.masked, self.maxed, self.exped = (s.sem(n) for n in (
            "scores_done", "mask_done", "max_done", "exp_done"))
        self.turned = [s.sem(f"transposed{b}") for b in range(2)]
        self.emptied = [s.sem(f"transposed_copied{b}") for b in range(2)]
        self.valued, self.inverted, self.normed = s.sem("pv_done"), s.sem("inverse_done"), s.sem("o_done")
        self.units = []
        chunk = 0
        for n in range(self.UNITS):
            blocks = n % NT + 1
            k = -(-blocks // 4)
            self.units.append((blocks, list(range(chunk, chunk + k))))
            chunk += k
        self.per_bank = chunk // 2
        assert chunk % 2 == 0

    def pe(self, pe, g, before):
        nc = self.nc

        def scores(n):
            before(n)
            if n >= 2:
                pe.wait_ge(self.exped, self.UNITS * g + n - 1)
            head, qt, (blocks, _) = n // NT, n % NT, self.units[n]
            at = slice(64 * (head % 2), 64 * (head % 2) + self.rows)
            for b in range(-(-blocks // 4)):
                w = min(blocks * P - b * HALF, HALF)
                last = nc.tensor.matmul(self.psS[:, n % 2, b, 0:w], self.qT[at, head // 2, qt * P:(qt + 1) * P],
                                        self.kT[at, b * HALF:b * HALF + w], start=True, stop=True)
            last.then_inc(self.scored, 1)

        def turn(n):
            pe.wait_ge(self.exped, self.UNITS * g + n + 1)
            blocks, chunks = self.units[n]
            for j, c in enumerate(chunks):
                if c >= 2:
                    pe.wait_ge(self.emptied[c % 2], self.per_bank * g + c // 2)
                for b in range(4 * j, min(blocks, 4 * j + 4)):
                    last = nc.tensor.transpose(self.psT[:, c % 2, (b % 4) * P:(b % 4 + 1) * P],
                                               self.p[:, n % 2, b * P:(b + 1) * P], self.ident[:])
                last.then_inc(self.turned[c % 2], 1)

        def values(n):
            blocks, chunks = self.units[n]
            for c in chunks:
                pe.wait_ge(self.emptied[c % 2], self.per_bank * g + c // 2 + 1)
            if n >= 2:
                pe.wait_ge(self.normed, self.UNITS * g + n - 1)
            for b in range(blocks):
                last = nc.tensor.matmul(self.psO[:, n % 2, 0:self.dv], self.pT[:, n % 2, b, :], self.v[:, b, :],
                                        start=b == 0, stop=b == blocks - 1)
            last.then_inc(self.valued, 1)

        scores(0)
        for n in range(self.UNITS):
            if n + 1 < self.UNITS:
                scores(n + 1)
            if n:
                values(n - 1)
            turn(n)
        values(self.UNITS - 1)

    def act(self, act, g):
        nc = self.nc

        def exp(n):
            act.wait_ge(self.maxed, self.UNITS * g + n + 1)
            w = self.units[n][0] * P
            scores = self.psS[:, n % 2, :, :].rearrange("p b w -> p (b w)")
            nc.scalar.activation(self.p[:, n % 2, 0:w], scores[:, 0:w], ACT.Exp, bias=self.negmax[:, n:n + 1],
                                 accum_out=self.rowsum[:, n:n + 1]).then_inc(self.exped, 1)

        exp(0)
        for n in range(self.UNITS):
            if n + 1 < self.UNITS:
                exp(n + 1)
            self.empty(act, g, n, 0, lambda out, in_: nc.scalar.activation(out, in_, ACT.Copy))

    def empty(self, engine, g, n, bank, copy):
        blocks, chunks = self.units[n]
        for j, c in enumerate(chunks):
            if c % 2 == bank:
                engine.wait_ge(self.turned[bank], self.per_bank * g + c // 2 + 1)
                if n >= 2:
                    engine.wait_ge(self.valued, self.UNITS * g + n - 1)
                b, e = 4 * j, min(blocks, 4 * j + 4)
                copy(self.pT[:, n % 2, b:e, :].rearrange("p b w -> p (b w)"),
                     self.psT[:, bank, 0:(e - b) * P]).then_inc(self.emptied[bank], 1)

    def dve(self, dve, g):
        nc = self.nc

        def maximum(n):
            dve.wait_ge(self.scored, self.UNITS * g + n + 1)
            w = self.units[n][0] * P
            scores = self.psS[:, n % 2, :, :].rearrange("p b w -> p (b w)")
            nc.vector.tensor_tensor(scores[:, w - P:w], scores[:, w - P:w], self.mask[:],
                                    ALU.add).then_inc(self.masked, 1)
            dve.wait_ge(self.masked, self.UNITS * g + n + 1)
            nc.vector.tensor_reduce(self.negmax[:, n:n + 1], scores[:, 0:w], AX.X, ALU.max,
                                    negate=True).then_inc(self.maxed, 1)

        def norm(n):
            dve.wait_ge(self.valued, self.UNITS * g + n + 1)
            head, qt = n // NT, n % NT
            nc.vector.reciprocal(self.rinv[:, n:n + 1], self.rowsum[:, n:n + 1]).then_inc(self.inverted, 1)
            dve.wait_ge(self.inverted, self.UNITS * g + n + 1)
            out = self.o[:, qt, head * self.dv:(head + 1) * self.dv]
            if self.fix_first is not None and qt == 0:
                nc.vector.tensor_scalar(out, self.psO[:, n % 2, 0:self.dv], self.rinv[:, n:n + 1],
                                        self.fix_first, ALU.mult, ALU.mult).then_inc(self.normed, 1)
            else:
                nc.vector.tensor_scalar(out, self.psO[:, n % 2, 0:self.dv], self.rinv[:, n:n + 1], None,
                                        ALU.mult).then_inc(self.normed, 1)

        maximum(0)
        for n in range(self.UNITS):
            if n + 1 < self.UNITS:
                maximum(n + 1)
            self.empty(dve, g, n, 1, lambda out, in_: nc.vector.tensor_copy(out, in_))
            if n:
                norm(n - 1)
        norm(self.UNITS - 1)


def l2_attention(core):
    nc, s = core.nc, Stage(core)
    x, xn, hT, acc, ident = core.x, core.xn, core.xnT, core.acc, core.ident
    G, DV = 8, 64
    WP = KD * (2 * D + 2 * P)
    att_mask = s.sb("causal_mask", [P, P])
    att = GroupAttention(s, nc, ident, DV, DV, att_mask)
    rope = s.sb("rope", [P, 4, T])
    wv = s.sb("w_v", [P, KD, G * DV])
    wp = s.sb("w_group", [P, WP])
    wo = s.sb("w_o_group", [P, KD, D])
    v_all = s.sb("v_all", [P, NT, G * DV])
    oT = s.sb("oT", [P, KD, T])
    rot = s.sb("rotated", [P, 2, 2, HALF])
    psS, UNITS = att.psS, att.UNITS
    mask_loaded, rope_loaded, wv_loaded, wp_loaded, wo_loaded = (s.sem(n) for n in (
        "mask_loaded", "rope_loaded", "wv_loaded", "w_group_loaded", "w_o_loaded"))
    v_ps, v_sb, v_group, proj, rotated, roped, proj_used, free = (s.sem(n) for n in (
        "v_psum", "v_sbuf", "v_group_ready", "projected", "rotated", "roped", "w_group_used", "banks_free"))
    oT_ps, oT_sb, wo_ps, acc_step = s.sem("oT_psum"), s.sem("oT_sbuf"), s.sem("wo_psum"), s.sem("acc_step")

    def parts(u):
        which, half = u // 2, u % 2
        if which == 0:
            return half, KD * 2 * D, P, 0, 2
        return half, (which - 1) * P, D, 0, 0

    with s.block() as block:
        @block.sync
        def _(sp):
            sp.dma_start(wv[:], core.dram["l2_wv"]).then_inc(wv_loaded, 16)
            sp.dma_start(rope[:], core.dram["l2_rope"]).then_inc(rope_loaded, 16)
            sp.dma_start(att_mask[:], core.dram["l2_mask"]).then_inc(mask_loaded, 16)
            sp.dma_start(wp[:], core.dram["l2_wgroup"][0]).then_inc(wp_loaded, 16)
            sp.dma_start(wo[:], core.dram["l2_wo"][0]).then_inc(wo_loaded, 16)
            with sp.Fori(0, G - 1) as g:
                sp.wait_ge(proj_used, g + 1)
                sp.dma_start(wp[:], core.dram["l2_wgroup"][g + 1]).then_inc(wp_loaded, 16)
                sp.wait_ge(wo_ps, 4 * g + 4)
                sp.dma_start(wo[:], core.dram["l2_wo"][g + 1]).then_inc(wo_loaded, 16)

        @block.gpsimd
        def _(pool):
            pool.wait_ge(v_sb, NT)
            nc.gpsimd.tensor_copy(att.v[:], v_all[:, :, 0:DV]).then_inc(v_group, 1)
            with pool.Fori(0, G - 1) as g:
                pool.wait_ge(att.valued, UNITS * g + UNITS)
                nc.gpsimd.tensor_copy(att.v[:], v_all[:, :, bass.ds((g + 1) * DV, DV)]).then_inc(v_group, 1)

        @block.tensor
        def _(pe):
            pe.wait_ge(wv_loaded, 16)
            for t in range(NT):
                if t >= 4:
                    pe.wait_ge(v_sb, t - 3)
                for k in range(KD):
                    last = nc.tensor.matmul(psS[:, t % 4 // 2, t % 2, :], hT[:, k, t * P:(t + 1) * P], wv[:, k, :],
                                            start=k == 0, stop=k == KD - 1)
                last.then_inc(v_ps, 1)
            pe.wait_ge(v_sb, NT)
            with pe.Fori(0, G) as g:
                pe.wait_ge(wp_loaded, 16 * g + 16)
                pe.wait_ge(free, g + 1)
                for u in range(6):
                    half, at, step, _, _ = parts(u)
                    if u >= 2:
                        pe.wait_ge(roped, 6 * g + u - 1)
                    for r in range(2):
                        for k in range(KD):
                            w = at + (r * KD + k) * step
                            last = nc.tensor.matmul(psS[:, u % 2, r, :], wp[:, w:w + P],
                                                    hT[:, k, half * HALF:(half + 1) * HALF],
                                                    start=k == 0, stop=k == KD - 1)
                    last.then_inc(proj, 1)

                def before(n):
                    if n == 0:
                        pe.wait_ge(roped, 6 * g + 5)
                        pe.wait_ge(v_group, g + 1)
                    if n == 1:
                        pe.wait_ge(roped, 6 * g + 6)
                att.pe(pe, g, before)
                pe.wait_ge(att.normed, UNITS * g + UNITS)
                for k in range(KD):
                    for half in range(NH):
                        for q in range(4):
                            last = nc.tensor.transpose(psS[:, k, half, q * P:(q + 1) * P],
                                                       att.o[:, half * 4 + q, k * P:(k + 1) * P], ident[:])
                        last.then_inc(oT_ps, 1)
                pe.wait_ge(oT_sb, 4 * g + 4)
                pe.wait_ge(wo_loaded, 16 * g + 16)
                for b in range(4):
                    for t in (2 * b, 2 * b + 1):
                        for k in range(KD):
                            last = nc.tensor.matmul(psS[:, b // 2, b % 2, (t % 2) * D:(t % 2 + 1) * D],
                                                    oT[:, k, t * P:(t + 1) * P], wo[:, k, :],
                                                    start=k == 0, stop=k == KD - 1)
                    last.then_inc(wo_ps, 1)

        @block.scalar
        def _(act):
            for t in range(NT):
                act.wait_ge(v_ps, t + 1)
                nc.scalar.activation(v_all[:, t, :], psS[:, t % 4 // 2, t % 2, :], ACT.Copy).then_inc(v_sb, 1)
            with act.Fori(0, G) as g:
                att.act(act, g)
                for k in range(KD):
                    for half in range(NH):
                        act.wait_ge(oT_ps, 4 * g + 2 * k + half + 1)
                        nc.scalar.activation(oT[:, k, half * HALF:(half + 1) * HALF], psS[:, k, half, :],
                                             ACT.Copy).then_inc(oT_sb, 1)

        @block.vector
        def _(dve):
            nc.vector.tensor_copy(acc[:], xn[:]).then_inc(free, 1)
            dve.wait_ge(rope_loaded, 16)
            dve.wait_ge(mask_loaded, 16)
            accb = acc[:, :, :].rearrange("p (b t) d -> p b (t d)", b=4)
            with dve.Fori(0, G) as g:
                for u in range(6):
                    half, _, _, _, table = parts(u)
                    to = slice(half * HALF, (half + 1) * HALF)
                    dve.wait_ge(proj, 6 * g + u + 1)
                    if u == 5:
                        dve.sem_inc(proj_used, 1)
                    for r in range(2):
                        last = nc.vector.tensor_tensor(rot[:, u % 2, r, :], psS[:, u % 2, r, :],
                                                       rope[:, table + r, to], ALU.mult)
                    last.then_inc(rotated, 1)
                    dve.wait_ge(rotated, 6 * g + u + 1)
                    out = att.kT[:, to] if u < 2 else att.qT[:, u // 2 - 1, to]
                    nc.vector.tensor_tensor(out, rot[:, u % 2, 0, :], rot[:, u % 2, 1, :],
                                            ALU.add).then_inc(roped, 1)
                att.dve(dve, g)
                for b in range(4):
                    dve.wait_ge(wo_ps, 4 * g + b + 1)
                    last = nc.vector.tensor_tensor(accb[:, b, :], psS[:, b // 2, b % 2, :], accb[:, b, :], ALU.add)
                last.then_inc(free, 1)
            dve.wait_ge(free, G + 1)
            nc.vector.scalar_tensor_tensor(x[:].rearrange("p t d -> p (t d)"), acc[:].rearrange("p t d -> p (t d)"),
                                           0.5, x[:].rearrange("p t d -> p (t d)"), ALU.mult, ALU.add)
    s.close()


def l0_attention(core):
    nc, s = core.nc, Stage(core)
    x, xnT, ident = core.x, core.xnT, core.ident
    G, NB, W, H = 4, 8, 4, 16
    HN = H * NB
    KV = G * NB
    att_mask = s.sb("causal_mask", [P, P])
    seen = s.sb("sees_a_key", [P, 1])
    att = GroupAttention(s, nc, ident, NB * W + 1, NB, att_mask, seen[:, 0:1])
    wq = s.sb("w_q", [P, KD, HN])
    wk = s.sb("w_k", [P, KD, KV])
    wv = s.sb("w_v", [P, KD, KV])
    wo = s.sb("w_o", [P, D])
    emb = s.sb("v_embeddings", [P, 2, HN])
    tau = s.sb("tau", [P, 1])
    itau = s.sb("inverse_tau", [P, 1])
    qT = s.sb("q_tanh", [HN, T])
    kT = s.sb("k_tanh", [KV, T])
    pad = s.sb("pad", [P, W])
    irow = s.sb("inverse_position", [1, T])
    v_all = s.sb("v_all", [P, NT, KV])
    o_all = s.sb("o_all", [P, NT, HN])
    o_neg = s.sb("one_minus_o", [P, NT, HN])
    oT = s.sb("oT", [HN, T])
    psS, UNITS = att.psS, att.UNITS
    names = ("l0_wq", "l0_wk", "l0_wv", "l0_wo", "l0_emb", "l0_tau", "l0_mask", "l0_seen", "l0_inverse")
    ld = {n: s.sem(n + "_loaded") for n in names}
    j_loaded = [s.sem(f"key_positions_loaded{i}") for i in range(2)]
    i_loaded = [s.sem(f"query_rows_loaded{i}") for i in range(4)]
    itau_ready, irow_ready, pad_ready, v_zero = (s.sem(n) for n in (
        "itau_ready", "irow_ready", "pad_ready", "v_zeroed"))
    q_ps, q_tanh, q_scaled, k_ps, k_tanh, v_ps, v_sb = (s.sem(n) for n in (
        "q_psum", "q_tanh_done", "q_scaled", "k_psum", "k_tanh_done", "v_psum", "v_sbuf"))
    q_stored = [s.sem(f"q_step_stored{w}") for w in range(W)]
    k_stored = [s.sem(f"k_step_stored{w}") for w in range(W)]
    q_pad = [s.sem(f"q_pad_stored{w}") for w in range(W - 1)]
    k_pad = [s.sem(f"k_pad_stored{w}") for w in range(W - 1)]
    q_loaded = [s.sem(f"q_loaded{i}") for i in range(4)]
    k_loaded = [s.sem(f"k_loaded{i}") for i in range(2)]
    v_group, o_kept, mixed, oT_ps, oT_sb, out_ps = (s.sem(n) for n in (
        "v_group_ready", "o_kept", "mixed", "oT_psum", "oT_sbuf", "out_psum"))
    q_rows, k_rows = core.q_steps, core.k_steps

    with s.block() as block:
        @block.sync
        def _(sp):
            for sb, n in zip((wq, wk, wv, wo, emb, tau, att_mask, seen, irow), names):
                sp.dma_start(sb[:], core.dram[n]).then_inc(ld[n], 16)
            for i in range(2):
                sp.dma_start(att.kT[64 * i + 32:64 * i + 33, :], core.dram["l0_positions"]).then_inc(j_loaded[i], 16)
            sp.wait_ge(pad_ready, 1)
            for w in range(W - 1):
                sp.dma_start(q_rows[w, :, 0:W - 1 - w], pad[:, 0:W - 1 - w],
                             allow_slow_non_contiguous=True).then_inc(q_pad[w], 16)
                sp.dma_start(k_rows[w, :, 0:W - 1 - w], pad[0:KV, 0:W - 1 - w],
                             allow_slow_non_contiguous=True).then_inc(k_pad[w], 16)
            sp.wait_ge(irow_ready, 1)
            for i in range(4):
                sp.dma_start(att.qT[64 * (i % 2) + 32:64 * (i % 2) + 33, i // 2, :], irow[:]).then_inc(i_loaded[i], 16)
            sp.wait_ge(k_tanh, NH)
            for w in range(W):
                late = W - 1 - w
                sp.dma_start(k_rows[w, :, late:T], kT[:, 0:T - late]).then_inc(k_stored[w], 16)
            sp.wait_ge(q_scaled, 1)
            for w in range(W):
                late = W - 1 - w
                sp.dma_start(q_rows[w, :, late:T], qT[:, 0:T - late]).then_inc(q_stored[w], 16)
            for w in range(W):
                sp.wait_ge(q_stored[w], 16)
                sp.wait_ge(k_stored[w], 16)
            for w in range(W - 1):
                sp.wait_ge(q_pad[w], 16)
                sp.wait_ge(k_pad[w], 16)

            def load(g):
                for i in range(2):
                    sp.dma_start(att.kT[64 * i:64 * i + 32, :],
                                 k_rows[:, bass.ds(g * NB, NB), :]).then_inc(k_loaded[i], 16)
                for i in range(4):
                    sp.dma_start(att.qT[64 * (i % 2):64 * (i % 2) + 32, i // 2, :],
                                 q_rows[:, bass.ds((4 * g + i) * NB, NB), :]).then_inc(q_loaded[i], 16)
            load(0)
            with sp.Fori(1, G) as g:
                sp.wait_ge(att.scored, UNITS * g)
                load(g)

        @block.gpsimd
        def _(pool):
            nc.gpsimd.memset(pad[:], 0.0).then_inc(pad_ready, 1)
            nc.gpsimd.memset(v_all[:], 0.0).then_inc(v_zero, 1)
            pool.wait_ge(v_sb, NT)
            nc.gpsimd.tensor_copy(att.v[:], v_all[:, :, 0:NB]).then_inc(v_group, 1)
            with pool.Fori(0, G - 1) as g:
                pool.wait_ge(att.valued, UNITS * g + UNITS)
                nc.gpsimd.tensor_copy(att.v[:], v_all[:, :, bass.ds((g + 1) * NB, NB)]).then_inc(v_group, 1)

        @block.tensor
        def _(pe):
            pe.wait_ge(ld["l0_wk"], 16)
            for half in range(NH):
                for k in range(KD):
                    last = nc.tensor.matmul(psS[0:KV, 0, half, :], wk[:, k, :],
                                            xnT[:, k, half * HALF:(half + 1) * HALF], start=k == 0, stop=k == KD - 1)
                last.then_inc(k_ps, 1)
            pe.wait_ge(ld["l0_wq"], 16)
            for half in range(NH):
                for k in range(KD):
                    last = nc.tensor.matmul(psS[:, 1, half, :], wq[:, k, :],
                                            xnT[:, k, half * HALF:(half + 1) * HALF], start=k == 0, stop=k == KD - 1)
                last.then_inc(q_ps, 1)
            pe.wait_ge(ld["l0_wv"], 16)
            for t in range(NT):
                rows = P if t < NT - 1 else P - 1
                for k in range(KD):
                    last = nc.tensor.matmul(att.psO[0:rows, 0, t * KV:(t + 1) * KV],
                                            xnT[:, k, t * P + 1:t * P + 1 + rows], wv[:, k, :],
                                            start=k == 0, stop=k == KD - 1)
            last.then_inc(v_ps, 1)
            for i in range(4):
                pe.wait_ge(i_loaded[i], 16)
            for i in range(2):
                pe.wait_ge(j_loaded[i], 16)
            with pe.Fori(0, G) as g:
                def before(n):
                    if n == 0:
                        pe.wait_ge(v_group, g + 1)
                        for i in range(2):
                            pe.wait_ge(k_loaded[i], 16 * g + 16)
                    if n % NT == 0:
                        pe.wait_ge(q_loaded[n // NT], 16 * g + 16)
                att.pe(pe, g, before)
            pe.wait_ge(mixed, 3)
            for t in range(NT):
                last = nc.tensor.transpose(psS[:, 0, t // 4, (t % 4) * P:(t % 4 + 1) * P], o_all[:, t, :], ident[:])
                if t % 4 == 3:
                    last.then_inc(oT_ps, 1)
            pe.wait_ge(oT_sb, NH)
            pe.wait_ge(ld["l0_wo"], 16)
            for b in range(4):
                for t in (2 * b, 2 * b + 1):
                    last = nc.tensor.matmul(psS[:, b // 2, b % 2, (t % 2) * D:(t % 2 + 1) * D],
                                            oT[:, t * P:(t + 1) * P], wo[:], start=True, stop=True)
                last.then_inc(out_ps, 1)

        @block.scalar
        def _(act):
            act.wait_ge(itau_ready, 1)
            for half in range(NH):
                act.wait_ge(k_ps, half + 1)
                nc.scalar.activation(kT[:, half * HALF:(half + 1) * HALF], psS[0:KV, 0, half, :], ACT.Tanh,
                                     scale=itau[0:KV, 0:1]).then_inc(k_tanh, 1)
            for half in range(NH):
                act.wait_ge(q_ps, half + 1)
                nc.scalar.activation(qT[:, half * HALF:(half + 1) * HALF], psS[:, 1, half, :], ACT.Tanh,
                                     scale=itau[:, 0:1]).then_inc(q_tanh, 1)
            act.wait_ge(v_ps, 1)
            act.wait_ge(v_zero, 1)
            for t in range(NT):
                rows = P if t < NT - 1 else P - 1
                nc.scalar.activation(v_all[0:rows, t, :], att.psO[0:rows, 0, t * KV:(t + 1) * KV], ACT.Sigmoid,
                                     scale=itau[0:rows, 0:1]).then_inc(v_sb, 1)
            with act.Fori(0, G) as g:
                att.act(act, g)
            for half in range(NH):
                act.wait_ge(oT_ps, half + 1)
                nc.scalar.activation(oT[:, half * HALF:(half + 1) * HALF], psS[:, 0, half, :],
                                     ACT.Copy).then_inc(oT_sb, 1)

        @block.vector
        def _(dve):
            dve.wait_ge(ld["l0_tau"], 16)
            nc.vector.reciprocal(itau[:], tau[:]).then_inc(itau_ready, 1)
            dve.wait_ge(ld["l0_inverse"], 16)
            dve.wait_ge(itau_ready, 1)
            nc.vector.tensor_scalar(irow[:], irow[:], itau[0:1, 0:1], None, ALU.mult).then_inc(irow_ready, 1)
            dve.wait_ge(q_tanh, NH)
            nc.vector.tensor_scalar(qT[:], qT[:], itau[:, 0:1], float((NB * W) ** -0.5), ALU.mult,
                                    ALU.mult).then_inc(q_scaled, 1)
            dve.wait_ge(ld["l0_mask"], 16)
            dve.wait_ge(ld["l0_seen"], 16)
            with dve.Fori(0, G) as g:
                att.dve(dve, g)
                dve.wait_ge(att.normed, UNITS * g + UNITS)
                nc.vector.tensor_copy(o_all[:, :, bass.ds(g * 4 * NB, 4 * NB)], att.o[:]).then_inc(o_kept, 1)
            dve.wait_ge(o_kept, G)
            dve.wait_ge(ld["l0_emb"], 16)
            nc.vector.tensor_scalar(o_neg[:], o_all[:], -1.0, 1.0, ALU.mult, ALU.add).then_inc(mixed, 1)
            dve.wait_ge(mixed, 1)
            nc.vector.tensor_tensor(o_neg[:], o_neg[:], emb[:, 0:1, :].to_broadcast([P, NT, HN]), ALU.mult)
            nc.vector.tensor_tensor(o_all[:], o_all[:], emb[:, 1:2, :].to_broadcast([P, NT, HN]),
                                    ALU.mult).then_inc(mixed, 1)
            dve.wait_ge(mixed, 2)
            nc.vector.tensor_tensor(o_all[:], o_all[:], o_neg[:], ALU.add).then_inc(mixed, 1)
            xb = x[:, :, :].rearrange("p (b t) d -> p b (t d)", b=4)
            for b in range(4):
                dve.wait_ge(out_ps, b + 1)
                nc.vector.tensor_tensor(xb[:, b, :], psS[:, b // 2, b % 2, :], xb[:, b, :], ALU.add)
    s.close()


class Delta:

    H, DK, DV = 6, 32, 64
    QK = 2 * H * DK
    V = H * DV
    CH = QK + V
    CT = CH // P

    def __init__(self, core):
        self.memory = s = Stage(core)
        H = self.H
        self.nat = s.sb("qkv", [P, NT, self.CH])
        self.beta = s.sb("beta", [P, NT, H])
        self.g = s.sb("log_decay", [P, NT, H])
        self.eg = s.sb("decay_from_start", [P, NT, H])
        self.ek = s.sb("decay_to_end", [P, NT, H])
        self.ec = s.sb("decay_of_chunk", [P, NT, H])
        self.tri = s.sb("triangles", [P, 3, P])
        self.o = s.sb("o", [P, NT, self.V])


def l2_delta_inputs(core, d):
    nc, s = core.nc, Stage(core)
    xnT, ident = core.xnT, core.ident
    H, DK, CT = d.H, d.DK, d.CT
    K = 4
    w = s.sb("w_qkv", [P, KD, d.CH])
    wc = s.sb("w_conv", [P, CT, K])
    wba = s.sb("w_beta_decay", [P, KD, 2 * H])
    bias = s.sb("dt_bias", [P, H])
    alog = s.sb("a_log", [P, H])
    na = s.sb("neg_a", [P, H])
    raw = s.sb("raw", [P, 2, K - 1 + T])
    cv = s.sb("conv", [P, 2, T])
    act_out = s.sb("conv_silu", [P, 2, T])
    z = s.sb("z", [P, NT, H])
    za = s.sb("z_abs", [P, NT, H])
    zl = s.sb("z_log", [P, NT, H])
    sq = s.sb("squares", [P, NT, d.QK])
    ss = s.sb("norms", [P, NT, 2 * H])
    eps = s.sb("eps", [P, 1])
    ones = s.sb("ones", [P, P])
    ps = s.ps("ps", [P, 4, HALF])
    psT = s.ps("psT", [P, 2, HALF])
    psG = s.ps("psG", [P, NT, 4 * H])
    psC = s.ps("psC", [P, 3, NT * H])
    names = ("l2_wqkv", "l2_wconv", "l2_wba", "l2_dt_bias", "l2_alog", "l2_tri")
    ld = {n: s.sem(n + "_loaded") for n in names}
    pad_set, const_set, proj, raw_done, conv_step, conv_done, silu_done, turned, nat_done = (s.sem(n) for n in (
        "pad_set", "const_set", "projected", "raw_done", "conv_step", "conv_done", "silu_done", "transposed",
        "qkv_done"))
    ba_ps, beta_done, z_done, zabs_done, zexp_done, zln_done, a_exp, g_step, g_done = (s.sem(n) for n in (
        "ba_psum", "beta_done", "z_done", "z_abs_done", "z_exp_done", "z_ln_done", "a_exp_done", "g_step",
        "g_done"))
    cum_ps, ss_done, sqrt_done, norm_step = (s.sem(n) for n in (
        "cumulated", "squares_summed", "sqrt_done", "norm_step"))
    with s.block() as block:
        @block.sync
        def _(sp):
            for sb, n in zip((w, wc, wba, bias, alog, d.tri), names):
                sp.dma_start(sb[:], core.dram[n]).then_inc(ld[n], 16)

        @block.gpsimd
        def _(pool):
            nc.gpsimd.memset(raw[:, 0, 0:K - 1], 0.0)
            nc.gpsimd.memset(raw[:, 1, 0:K - 1], 0.0).then_inc(pad_set, 1)
            nc.gpsimd.memset(eps[:], 1e-6)
            nc.gpsimd.memset(ones[:], 1.0).then_inc(const_set, 1)

        @block.tensor
        def _(pe):
            pe.wait_ge(ld["l2_wqkv"], 16)

            def project(c):
                for half in range(NH):
                    if c >= 2:
                        pe.wait_ge(raw_done, 2 * c + half - 3)
                    for k in range(KD):
                        last = nc.tensor.matmul(ps[:, c % 2 * 2 + half, :], w[:, k, c * P:(c + 1) * P],
                                                xnT[:, k, half * HALF:(half + 1) * HALF],
                                                start=k == 0, stop=k == KD - 1)
                    last.then_inc(proj, 1)

            def turn(c):
                pe.wait_ge(silu_done, c + 1)
                for half in range(NH):
                    if c >= 1:
                        pe.wait_ge(nat_done, 2 * c + half - 1)
                    for q in range(4):
                        t = half * 4 + q
                        last = nc.tensor.transpose(psT[:, half, q * P:(q + 1) * P],
                                                   act_out[:, c % 2, t * P:(t + 1) * P], ident[:])
                    last.then_inc(turned, 1)

            project(0)
            pe.wait_ge(ld["l2_wba"], 16)
            for t in range(NT):
                for k in range(KD):
                    last = nc.tensor.matmul(psG[:, t, 0:2 * H], xnT[:, k, t * P:(t + 1) * P], wba[:, k, :],
                                            start=k == 0, stop=k == KD - 1)
            last.then_inc(ba_ps, 1)
            project(1)
            for c in range(CT):
                if c + 2 < CT:
                    project(c + 2)
                turn(c)
            pe.wait_ge(g_done, 1)
            pe.wait_ge(ld["l2_tri"], 16)
            pe.wait_ge(const_set, 1)
            gf = d.g[:].rearrange("p t h -> p (t h)")
            for m, lhsT in enumerate((d.tri[:, 0, :], d.tri[:, 1, :], ones[:])):
                last = nc.tensor.matmul(psC[:, m, :], lhsT, gf, start=True, stop=True)
            last.then_inc(cum_ps, 1)

        @block.scalar
        def _(act):
            def evacuate(c):
                if c >= 2:
                    act.wait_ge(conv_done, c - 1)
                for half in range(NH):
                    act.wait_ge(proj, 2 * c + half + 1)
                    nc.scalar.activation(raw[:, c % 2, K - 1 + half * HALF:K - 1 + (half + 1) * HALF],
                                         ps[:, c % 2 * 2 + half, :], ACT.Copy).then_inc(raw_done, 1)

            act.wait_ge(ba_ps, 1)
            nc.scalar.activation(d.beta[:], psG[:, :, 0:H], ACT.Sigmoid).then_inc(beta_done, 1)
            evacuate(0)
            for c in range(CT):
                if c + 1 < CT:
                    evacuate(c + 1)
                act.wait_ge(conv_done, c + 1)
                if c >= 2:
                    act.wait_ge(turned, 2 * c - 2)
                nc.scalar.activation(act_out[:, c % 2, :], cv[:, c % 2, :], ACT.Silu).then_inc(silu_done, 1)
            act.wait_ge(z_done, 1)
            nc.scalar.activation(za[:], z[:], ACT.Abs).then_inc(zabs_done, 1)
            act.wait_ge(zabs_done, 1)
            nc.scalar.activation(zl[:], za[:], ACT.Exp, scale=-1.0).then_inc(zexp_done, 1)
            act.wait_ge(zexp_done, 1)
            nc.scalar.activation(za[:], zl[:], ACT.Ln, bias=1.0).then_inc(zln_done, 1)
            act.wait_ge(ld["l2_alog"], 16)
            nc.scalar.activation(na[:], alog[:], ACT.Exp).then_inc(a_exp, 1)
            act.wait_ge(cum_ps, 1)
            for m, out in enumerate((d.eg, d.ek, d.ec)):
                nc.scalar.activation(out[:].rearrange("p t h -> p (t h)"), psC[:, m, :], ACT.Exp)
            act.wait_ge(ss_done, 1)
            act.wait_ge(const_set, 1)
            nc.scalar.activation(ss[:], ss[:], ACT.Sqrt, bias=eps[:, 0:1]).then_inc(sqrt_done, 1)

        @block.vector
        def _(dve):
            link = chain(dve, conv_step)
            dve.wait_ge(ld["l2_wconv"], 16)
            dve.wait_ge(pad_set, 1)

            def convolve(c):
                dve.wait_ge(raw_done, 2 * c + 2)
                if c >= 2:
                    dve.wait_ge(silu_done, c - 1)
                out, b = cv[:, c % 2, :], c % 2
                link(nc.vector.tensor_scalar(out, raw[:, b, K - 1:K - 1 + T], wc[:, c, K - 1:K], None, ALU.mult))
                for k in range(K - 1):
                    last = nc.vector.scalar_tensor_tensor(out, raw[:, b, k:k + T], wc[:, c, k:k + 1], out,
                                                          ALU.mult, ALU.add)
                    if k < K - 2:
                        link(last)
                last.then_inc(conv_done, 1)

            def keep(c):
                for half in range(NH):
                    dve.wait_ge(turned, 2 * c + half + 1)
                    nc.vector.tensor_copy(d.nat[:, half * 4:half * 4 + 4, c * P:(c + 1) * P],
                                          psT[:, half, :].rearrange("p (t w) -> p t w", t=4)).then_inc(nat_done, 1)

            dve.wait_ge(ba_ps, 1)
            dve.wait_ge(beta_done, 1)
            dve.wait_ge(ld["l2_dt_bias"], 16)
            nc.vector.tensor_tensor(z[:], psG[:, :, H:2 * H], bias[:].unsqueeze(1).to_broadcast([P, NT, H]),
                                    ALU.add).then_inc(z_done, 1)
            convolve(0)
            for c in range(CT):
                if c + 1 < CT:
                    convolve(c + 1)
                keep(c)
            step = chain(dve, g_step)
            dve.wait_ge(zln_done, 1)
            dve.wait_ge(z_done, 1)
            step(nc.vector.tensor_scalar(z[:], z[:], 0.0, None, ALU.max))
            step(nc.vector.tensor_tensor(za[:], za[:], z[:], ALU.add))
            dve.wait_ge(a_exp, 1)
            step(nc.vector.tensor_scalar(na[:], na[:], -1.0, None, ALU.mult))
            nc.vector.tensor_tensor(d.g[:], za[:], na[:].unsqueeze(1).to_broadcast([P, NT, H]),
                                    ALU.mult).then_inc(g_done, 1)
            norm = chain(dve, norm_step)
            dve.wait_ge(nat_done, 2 * CT)
            qk = d.nat[:, :, 0:d.QK]
            norm(nc.vector.tensor_tensor(sq[:], qk, qk, ALU.mult))
            nc.vector.tensor_reduce(ss[:], sq[:].rearrange("p t (h k) -> p t h k", k=DK), AX.X,
                                    ALU.add).then_inc(ss_done, 1)
            dve.wait_ge(sqrt_done, 1)
            norm(nc.vector.reciprocal(ss[:], ss[:]))
            norm(nc.vector.tensor_scalar(ss[:, :, 0:H], ss[:, :, 0:H], float(DK) ** -0.5, None, ALU.mult))
            qk4 = qk.rearrange("p t (h k) -> p t h k", k=DK)
            nc.vector.tensor_tensor(qk4, qk4, ss[:].unsqueeze(3).to_broadcast([P, NT, 2 * H, DK]), ALU.mult)
    s.close()


def l2_delta_chunks(core, d):
    nc, s = core.nc, Stage(core)
    ident = core.ident
    H, DK, DV, QK = d.H, d.DK, d.DV, d.QK
    HK = H * DK
    LEVELS = 6
    B = 3
    masks = s.sb("level_masks", [P, LEVELS + 1, P])
    sg = s.sb("staged", [P, 2, 4, HK])
    kd = s.sb("k_to_end", [P, 2, HK])
    st = s.sb("staged_T", [DK, H, 8, P])
    lg = s.sb("summed_g", [P, B, 4, P])
    bm = s.sb("beta_mask", [P, B, 4, P])
    ed = s.sb("decays", [P, B, 2, HALF])
    em = s.sb("decays_masked", [P, B, 2, HALF])
    L = s.sb("L", [P, B, 4, P])
    AT = s.sb("AT", [P, B, 4, P])
    t0 = s.sb("joined0", [P, B, 4, P])
    X = s.sb("X", [P, B, 4, P])
    Y = s.sb("Y", [P, B, 4, P])
    ml = s.sb("L_level", [P, B, 4, P])
    bs = s.sb("B_level", [P, B, 4, P])
    S = s.sb("state", [DK, H, DV])
    Sd = s.sb("state_decayed", [DK, H, DV])
    vd = s.sb("v_less", [P, H, DV])
    R = s.sb("R", [P, H, DV])
    U = s.sb("u", [P, H, DV])
    ps = s.ps("ps", [P, 8, HALF])
    flat = lambda ap: ap.rearrange("p s n -> p (s n)")
    four = lambda ap: ap.unsqueeze(1).to_broadcast([P, 4, P])
    (masks_loaded, staged, copied, bmask, summed, turned, st_done, d_ps, d_exp, masked, kq_ps, la_done, t0_done,
     x0_done, y0_ps, y0_done, ml_done, b_ps, b_sb, yx_ps, yx_done, p1_ps, vd_done, r_done, u_ps, u_sb, o_ps, o_sb,
     sd_ps, s_done, sd_done) = (s.sem(n) for n in (
         "masks_loaded", "staged", "qk_copied", "beta_mask_done", "g_summed", "staged_turned", "staged_T_done",
         "decay_logs", "decays_done", "decays_masked", "kk_qk_psum", "l_a_done", "joined0_done", "x0_done",
         "y0_psum", "y0_done", "l_level_done", "b_psum", "b_sbuf", "yx_psum", "yx_done", "p1_psum", "v_less_done",
         "r_done", "u_psum", "u_sbuf", "o_psum", "o_sbuf", "s_psum", "s_done", "s_decayed"))

    def systems(b):
        return [(b, h) for h in range(4)] if b < 2 else [(e, h) for e in range(2) for h in (4, 5)]

    def place(e, h):
        return (e, h) if h < 4 else (2, 2 * e + h - 4)

    def kqT(e, which, h):
        return st[:, h, e * 4 + which, :]

    with s.block() as block:
        @block.sync
        def _(sp):
            sp.dma_start(masks[:], core.dram["l2_levels"]).then_inc(masks_loaded, 16)

        @block.gpsimd
        def _(pool):
            pool.wait_ge(masks_loaded, 16)
            with pool.Fori(0, NT // 2) as i:
                two = bass.ds(2 * i, 2)
                nc.gpsimd.tensor_copy(sg[:, :, 2:4, :].rearrange("p e a n -> p e (a n)"),
                                      d.nat[:, two, 0:QK]).then_inc(copied, 1)
                for b in range(B):
                    if b < 2:
                        beta = d.beta[:, bass.ds(2 * i + b, 1), 0:4].rearrange("p a h -> p (a h)").unsqueeze(2)
                        nc.gpsimd.tensor_tensor(bm[:, b, :, :], four(d.tri[:, 2, :]), beta.to_broadcast([P, 4, P]),
                                                ALU.mult).then_inc(bmask, 1)
                    else:
                        for e in range(2):
                            beta = d.beta[:, bass.ds(2 * i + e, 1), 4:6].rearrange("p a h -> p (a h)").unsqueeze(2)
                            nc.gpsimd.tensor_tensor(bm[:, b, 2 * e:2 * e + 2, :],
                                                    d.tri[:, 2, :].unsqueeze(1).to_broadcast([P, 2, P]),
                                                    beta.to_broadcast([P, 2, P]), ALU.mult).then_inc(bmask, 1)
                pool.wait_ge(bmask, 4 * i + 4)
                for b in range(B):
                    pool.wait_ge(d_exp, B * i + b + 1)
                    nc.gpsimd.tensor_tensor(em[:, b, 0, :], ed[:, b, 0, :], flat(bm[:, b, :, :]), ALU.mult)
                    nc.gpsimd.tensor_tensor(em[:, b, 1, :].rearrange("p (s n) -> p s n", s=4),
                                            ed[:, b, 1, :].rearrange("p (s n) -> p s n", s=4),
                                            four(d.tri[:, 0, :]), ALU.mult).then_inc(masked, 1)
                for k in range(LEVELS):
                    for b in range(B):
                        if k == 0:
                            pool.wait_ge(la_done, B * i + b + 1)
                        else:
                            pool.wait_ge(b_ps, B * LEVELS * i + B * (k - 1) + b + 1)
                        nc.gpsimd.tensor_tensor(ml[:, b, :, :], L[:, b, :, :], four(masks[:, k + 1, :]),
                                                ALU.mult).then_inc(ml_done, 1)

        @block.tensor
        def _(pe):
            with pe.Fori(0, NT // 2) as i:
                pe.wait_ge(staged, i + 1)
                pe.wait_ge(copied, i + 1)
                for h in range(H):
                    if h >= 2:
                        pe.wait_ge(st_done, H * i + h - 1)
                    for e in range(2):
                        for a in range(4):
                            last = nc.tensor.transpose(ps[0:DK, 2 * (h % 2) + e, a * P:(a + 1) * P],
                                                       sg[:, e, a, h * DK:(h + 1) * DK], ident[:])
                    last.then_inc(turned, 1)
                pe.wait_ge(summed, i + 1)
                for b in range(B):
                    if b < 2:
                        pe.wait_ge(st_done, H * i + H - 1 + b)
                    else:
                        pe.wait_ge(s_done, 2 * i + 1)
                    for j in range(4):
                        nc.tensor.matmul(ps[:, 2 * b, j * P:(j + 1) * P], lg[:, b, j, :], d.tri[:, 1, :],
                                         start=True, stop=True)
                    nc.tensor.matmul(ps[:, 2 * b + 1, :], d.tri[:, 1, :], flat(lg[:, b, :, :]), start=True,
                                     stop=True).then_inc(d_ps, 1)
                pe.wait_ge(st_done, H * i + H)
                for b in range(B):
                    pe.wait_ge(d_exp, B * i + b + 1)
                    for j, (e, h) in enumerate(systems(b)):
                        to = slice(j * P, (j + 1) * P)
                        nc.tensor.matmul(ps[:, 2 * b, to], kqT(e, 3, h), kqT(e, 3, h), start=True, stop=True)
                        last = nc.tensor.matmul(ps[:, 2 * b + 1, to], kqT(e, 3, h), kqT(e, 2, h), start=True,
                                                stop=True)
                    last.then_inc(kq_ps, 1)
                for b in range(B):
                    pe.wait_ge(x0_done, B * i + b + 1)
                    for j in range(4):
                        last = nc.tensor.transpose(ps[:, 2 * b, j * P:(j + 1) * P], X[:, b, j, :], ident[:])
                    last.then_inc(y0_ps, 1)
                for k in range(LEVELS):
                    for b in range(B):
                        pe.wait_ge(ml_done, B * LEVELS * i + B * k + b + 1)
                        if k == 0:
                            pe.wait_ge(y0_done, B * i + b + 1)
                        else:
                            pe.wait_ge(yx_done, B * LEVELS * i + B * (k - 1) + b + 1)
                        for j in range(4):
                            last = nc.tensor.matmul(ps[:, 2 * b, j * P:(j + 1) * P], ml[:, b, j, :], Y[:, b, j, :],
                                                    start=True, stop=True)
                        last.then_inc(b_ps, 1)
                    for b in range(B):
                        pe.wait_ge(b_sb, B * LEVELS * i + B * k + b + 1)
                        for j in range(4):
                            to = slice(j * P, (j + 1) * P)
                            last = nc.tensor.matmul(ps[:, 2 * b, to], X[:, b, j, :], bs[:, b, j, :], start=True,
                                                    stop=True)
                            if k < LEVELS - 1:
                                last = nc.tensor.matmul(ps[:, 2 * b + 1, to], bs[:, b, j, :], X[:, b, j, :],
                                                        start=True, stop=True)
                        last.then_inc(yx_ps, 1)
                for e in range(2):
                    pe.wait_ge(s_done, 2 * i + e + 1)
                    for h in range(H):
                        last = nc.tensor.matmul(ps[:, 6, h * DV:(h + 1) * DV], kqT(e, 1, h),
                                                S[:, h, :], start=True, stop=True)
                    last.then_inc(p1_ps, 1)
                    pe.wait_ge(r_done, 2 * i + e + 1)
                    if e == 0:
                        pe.wait_ge(yx_done, B * LEVELS * i + B * LEVELS)
                    for h in range(H):
                        b, j = place(e, h)
                        last = nc.tensor.matmul(ps[:, 7, h * DV:(h + 1) * DV], Y[:, b, j, :], R[:, h, :],
                                                start=True, stop=True)
                    last.then_inc(u_ps, 1)
                    pe.wait_ge(u_sb, 2 * i + e + 1)
                    if e == 1:
                        pe.wait_ge(o_sb, 2 * i + 1)
                    for h in range(H):
                        b, j = place(e, h)
                        to = slice(h * DV, (h + 1) * DV)
                        nc.tensor.matmul(ps[:, 4, to], kqT(e, 0, h), S[:, h, :],
                                         start=True, stop=False)
                        last = nc.tensor.matmul(ps[:, 4, to], AT[:, b, j, :], U[:, h, :], start=False, stop=True)
                    last.then_inc(o_ps, 1)
                    for h in range(H):
                        last = nc.tensor.matmul(ps[0:DK, 5, h * DV:(h + 1) * DV],
                                                kd[:, e, h * DK:(h + 1) * DK], U[:, h, :], start=True, stop=True)
                    last.then_inc(sd_ps, 1)

        @block.scalar
        def _(act):
            with act.Fori(0, NT // 2) as i:
                for h in range(H):
                    act.wait_ge(turned, H * i + h + 1)
                    nc.scalar.activation(st[:, h, :, :].rearrange("p a n -> p (a n)"),
                                         ps[0:DK, 2 * (h % 2):2 * (h % 2) + 2, :].rearrange("p b n -> p (b n)"),
                                         ACT.Copy).then_inc(st_done, 1)
                for b in range(B):
                    act.wait_ge(d_ps, B * i + b + 1)
                    nc.scalar.activation(ed[:, b, :, :], ps[:, 2 * b:2 * b + 2, :], ACT.Exp).then_inc(d_exp, 1)
                for b in range(B):
                    act.wait_ge(y0_ps, B * i + b + 1)
                    nc.scalar.activation(flat(Y[:, b, :, :]), ps[:, 2 * b, :], ACT.Copy).then_inc(y0_done, 1)
                for k in range(LEVELS):
                    for b in range(B):
                        act.wait_ge(b_ps, B * LEVELS * i + B * k + b + 1)
                        nc.scalar.activation(flat(bs[:, b, :, :]), ps[:, 2 * b, :], ACT.Copy).then_inc(b_sb, 1)
                for e in range(2):
                    act.wait_ge(u_ps, 2 * i + e + 1)
                    nc.scalar.activation(U[:].rearrange("p h n -> p (h n)"), ps[:, 7, 0:H * DV],
                                         ACT.Copy).then_inc(u_sb, 1)
                    act.wait_ge(o_ps, 2 * i + e + 1)
                    nc.scalar.activation(d.o[:, bass.ds(2 * i + e, 1), :].rearrange("p a n -> p (a n)"),
                                         ps[:, 4, 0:H * DV], ACT.Copy).then_inc(o_sb, 1)

        @block.vector
        def _(dve):
            nc.vector.memset(S[:], 0.0).then_inc(s_done, 1)
            dve.wait_ge(masks_loaded, 16)
            with dve.Fori(0, NT // 2) as i:
                def heads(ap, e, lo, hi):
                    return ap[:, bass.ds(2 * i + e, 1), lo:hi].rearrange("p a h -> p (a h)")

                for e in range(2):
                    q3, k3 = (heads(d.nat, e, lo, lo + HK).rearrange("p (h n) -> p h n", n=DK) for lo in (0, HK))
                    g3, k_end = (heads(ap, e, 0, H).unsqueeze(2).to_broadcast([P, H, DK]) for ap in (d.eg, d.ek))
                    for out, a, decay in ((sg[:, e, 0, :], q3, g3), (sg[:, e, 1, :], k3, g3), (kd[:, e, :], k3, k_end)):
                        last = nc.vector.tensor_tensor(out.rearrange("p (h n) -> p h n", n=DK), a, decay, ALU.mult)
                last.then_inc(staged, 1)
                for b in range(B):
                    if b < 2:
                        last = nc.vector.tensor_tensor(lg[:, b, :, :], four(d.tri[:, 0, :]),
                                                       heads(d.g, b, 0, 4).unsqueeze(2).to_broadcast([P, 4, P]),
                                                       ALU.mult)
                    else:
                        for e in range(2):
                            last = nc.vector.tensor_tensor(
                                lg[:, b, 2 * e:2 * e + 2, :], d.tri[:, 0, :].unsqueeze(1).to_broadcast([P, 2, P]),
                                heads(d.g, e, 4, 6).unsqueeze(2).to_broadcast([P, 2, P]), ALU.mult)
                last.then_inc(summed, 1)
                for b in range(B):
                    dve.wait_ge(masked, B * i + b + 1)
                    dve.wait_ge(kq_ps, B * i + b + 1)
                    nc.vector.tensor_tensor(flat(L[:, b, :, :]), ps[:, 2 * b, :], em[:, b, 0, :], ALU.mult)
                    nc.vector.tensor_tensor(flat(AT[:, b, :, :]), ps[:, 2 * b + 1, :], em[:, b, 1, :],
                                            ALU.mult).then_inc(la_done, 1)
                    dve.wait_ge(la_done, B * i + b + 1)
                    nc.vector.tensor_tensor(t0[:, b, :, :], L[:, b, :, :], four(masks[:, 0, :]),
                                            ALU.mult).then_inc(t0_done, 1)
                    dve.wait_ge(t0_done, B * i + b + 1)
                    nc.vector.tensor_tensor(X[:, b, :, :], four(ident[:]), t0[:, b, :, :],
                                            ALU.subtract).then_inc(x0_done, 1)
                for k in range(LEVELS):
                    for b in range(B):
                        dve.wait_ge(yx_ps, B * LEVELS * i + B * k + b + 1)
                        last = nc.vector.tensor_tensor(flat(Y[:, b, :, :]), flat(Y[:, b, :, :]), ps[:, 2 * b, :],
                                                       ALU.subtract)
                        if k < LEVELS - 1:
                            last = nc.vector.tensor_tensor(flat(X[:, b, :, :]), flat(X[:, b, :, :]),
                                                           ps[:, 2 * b + 1, :], ALU.subtract)
                        last.then_inc(yx_done, 1)
                for e in range(2):
                    dve.wait_ge(s_done, 2 * i + e + 1)
                    nc.vector.tensor_tensor(
                        Sd[:], S[:],
                        d.ec[0:DK, bass.ds(2 * i + e, 1), :].rearrange("p a h -> p (a h)").unsqueeze(2)
                        .to_broadcast([DK, H, DV]), ALU.mult).then_inc(sd_done, 1)
                    dve.wait_ge(p1_ps, 2 * i + e + 1)
                    nc.vector.tensor_tensor(vd[:].rearrange("p h n -> p (h n)"), heads(d.nat, e, QK, QK + H * DV),
                                            ps[:, 6, 0:H * DV], ALU.subtract).then_inc(vd_done, 1)
                    dve.wait_ge(vd_done, 2 * i + e + 1)
                    nc.vector.tensor_tensor(R[:], vd[:], heads(d.beta, e, 0, H).unsqueeze(2).to_broadcast([P, H, DV]),
                                            ALU.mult).then_inc(r_done, 1)
                    dve.wait_ge(sd_done, 2 * i + e + 1)
                    dve.wait_ge(sd_ps, 2 * i + e + 1)
                    if e == 1:
                        dve.wait_ge(o_sb, 2 * i + 2)
                    nc.vector.tensor_tensor(S[:].rearrange("p h n -> p (h n)"),
                                            Sd[:].rearrange("p h n -> p (h n)"), ps[0:DK, 5, 0:H * DV],
                                            ALU.add).then_inc(s_done, 1)
    s.close()


def l2_delta_output(core, d):
    nc, s = core.nc, Stage(core)
    x, xnT, ident = core.x, core.xnT, core.ident
    H, DV, V = d.H, d.DV, d.V
    VT = V // P
    wg = s.sb("w_gate", [P, KD, V])
    wo = s.sb("w_out", [P, VT, D])
    nw = s.sb("norm_w", [P, V])
    gate = s.sb("gate", [P, NT, V])
    sq = s.sb("squares", [P, NT, V])
    ms = s.sb("mean_square", [P, NT, H])
    oT = s.sb("oT", [P, VT, T])
    ps = s.ps("ps", [P, 4, HALF])
    psT = s.ps("psT", [P, 4, HALF])
    ld = {n: s.sem(n + "_loaded") for n in ("l2_wg", "l2_norm_w", "l2_dwo")}
    gate_ps, gate_sb, step, ms_done, sqrt_done, gated, turned, oT_sb, out_ps = (s.sem(n) for n in (
        "gate_psum", "gate_sbuf", "dve_step", "ms_done", "sqrt_done", "gated", "transposed", "oT_sbuf", "out_psum"))
    with s.block() as block:
        @block.sync
        def _(sp):
            for sb, n in zip((wg, nw, wo), ld):
                sp.dma_start(sb[:], core.dram[n]).then_inc(ld[n], 16)

        @block.tensor
        def _(pe):
            pe.wait_ge(ld["l2_wg"], 16)
            for t in range(NT):
                if t >= 4:
                    pe.wait_ge(gate_sb, t - 3)
                for k in range(KD):
                    last = nc.tensor.matmul(ps[:, t % 4, 0:V], xnT[:, k, t * P:(t + 1) * P], wg[:, k, :],
                                            start=k == 0, stop=k == KD - 1)
                last.then_inc(gate_ps, 1)
            for c in range(VT):
                for half in range(NH):
                    n = 2 * c + half
                    if n >= 4:
                        pe.wait_ge(oT_sb, n - 3)
                    for q in range(4):
                        t = half * 4 + q
                        if c == 0:
                            pe.wait_ge(gated, t + 1)
                        last = nc.tensor.transpose(psT[:, n % 4, q * P:(q + 1) * P], d.o[:, t, c * P:(c + 1) * P],
                                                   ident[:])
                    last.then_inc(turned, 1)
            pe.wait_ge(oT_sb, 2 * VT)
            pe.wait_ge(ld["l2_dwo"], 16)
            for b in range(4):
                for t in (2 * b, 2 * b + 1):
                    for c in range(VT):
                        last = nc.tensor.matmul(ps[:, b, (t % 2) * D:(t % 2 + 1) * D], oT[:, c, t * P:(t + 1) * P],
                                                wo[:, c, :], start=c == 0, stop=c == VT - 1)
                last.then_inc(out_ps, 1)

        @block.scalar
        def _(act):
            for t in range(NT):
                act.wait_ge(gate_ps, t + 1)
                nc.scalar.activation(gate[:, t, :], ps[:, t % 4, 0:V], ACT.Silu).then_inc(gate_sb, 1)
            act.wait_ge(ms_done, 1)
            nc.scalar.activation(ms[:], ms[:], ACT.Sqrt, bias=core.eps[:, 0:1], scale=1.0 / DV).then_inc(sqrt_done, 1)
            for n in range(2 * VT):
                act.wait_ge(turned, n + 1)
                nc.scalar.activation(oT[:, n // 2, n % 2 * HALF:(n % 2 + 1) * HALF], psT[:, n % 4, :],
                                     ACT.Copy).then_inc(oT_sb, 1)

        @block.vector
        def _(dve):
            link = chain(dve, step)
            link(nc.vector.tensor_tensor(sq[:], d.o[:], d.o[:], ALU.mult))
            nc.vector.tensor_reduce(ms[:], sq[:].rearrange("p t (h n) -> p t h n", n=DV), AX.X,
                                    ALU.add).then_inc(ms_done, 1)
            dve.wait_ge(ld["l2_norm_w"], 16)
            dve.wait_ge(gate_sb, NT)
            link(nc.vector.tensor_tensor(gate[:], gate[:], nw[:].unsqueeze(1).to_broadcast([P, NT, V]), ALU.mult))
            dve.wait_ge(sqrt_done, 1)
            link(nc.vector.reciprocal(ms[:], ms[:]))
            o4 = d.o[:].rearrange("p t (h n) -> p t h n", n=DV)
            link(nc.vector.tensor_tensor(o4, o4, ms[:].unsqueeze(3).to_broadcast([P, NT, H, DV]), ALU.mult))
            for t in range(NT):
                nc.vector.tensor_tensor(d.o[:, t, :], d.o[:, t, :], gate[:, t, :], ALU.mult).then_inc(gated, 1)
            xb = x[:, :, :].rearrange("p (b t) d -> p b (t d)", b=4)
            for b in range(4):
                dve.wait_ge(out_ps, b + 1)
                nc.vector.tensor_tensor(xb[:, b, :], ps[:, b, :], xb[:, b, :], ALU.add)
    s.close()


def l2_delta(core):
    d = Delta(core)
    l2_delta_inputs(core, d)
    l2_delta_chunks(core, d)
    l2_delta_output(core, d)
    d.memory.close()


def program(nc, dram, stages=STAGES):
    core = Core(nc, dram)
    with ExitStack() as stack:
        def sb(name, shape):
            return stack.enter_context(nc.sbuf_tensor(name, shape, F32))

        core.x = sb("x_residual", [P, NT, D])
        core.xn = sb("xn", [P, NT, D])
        core.acc = sb("acc", [P, NT, D])
        core.xnT = sb("xnT", [P, KD, T])
        core.ident = sb("ident", [P, P])
        core.eps = sb("eps", [P, 1])
        core.gates = nc.dram_tensor("gate_rows", (20, T), F32, kind="Internal").ap()
        core.q_steps = nc.dram_tensor("q_steps", (4, P, T), F32, kind="Internal").ap()
        core.k_steps = nc.dram_tensor("k_steps", (4, 32, T), F32, kind="Internal").ap()
        core.bc_rows = nc.dram_tensor("bc_rows", (32, T), F32, kind="Internal").ap()
        nc.vector.memset(core.eps[:], LN_EPS)
        load_residual(core)
        for stage in stages:
            if stage == "l0f":
                layernorm(core)
                gated_ffn(core, "l0_ffn", 6, 0)
            if stage == "l1f":
                layernorm(core)
                route(core, "l1_router", 16, 4, 0.8, 4, 0.2)
                gated_ffn(core, "l1_ffn", 20, 2)
            if stage == "l3f":
                layernorm(core)
                route(core, "l3_router", 8, 2, 1.0)
                gated_ffn(core, "l3_ffn", 16, 1)
            if stage == "l0a":
                layernorm(core)
                l0_attention(core)
            if stage == "l1a":
                layernorm(core)
                l1_scan(core)
            if stage == "l2f":
                layernorm(core, "l2_ln_w")
                l2_attention(core)
                layernorm(core, "l2_ff_ln_w", core.acc)
                route(core, "l2_router", 16, 4, 1.0)
                gated_ffn(core, "l2_ffn", 32, 1)
            if stage == "l2a":
                layernorm(core)
                l2_delta(core)
            if stage == "l3a":
                layernorm(core)
                l3_attention(core)
        store_residual(core)


def by_partition(w):
    return np.ascontiguousarray(w.reshape(-1, P, w.shape[1]).transpose(1, 0, 2))


def ffn_chunks(w1, w3, w2):
    chunks = w1.shape[1] // P
    up = [w.reshape(KD, P, chunks, P).transpose(2, 1, 0, 3).reshape(chunks, P, D) for w in (w1, w3)]
    return np.ascontiguousarray(np.concatenate([*up, w2.reshape(chunks, P, D)], axis=2))


def side_by_side(w):
    return w.transpose(1, 0, 2).reshape(w.shape[1], -1)


def rotation_tables():
    half = 32
    inv = np.float32(1.0) / np.float32(150000.0) ** (np.arange(half, dtype=np.float32) / np.float32(half))
    ang = (np.arange(T, dtype=np.float32)[:, None] * inv).T
    cos, sin = np.cos(ang), np.sin(ang)
    c = np.concatenate([cos, cos] * 2)
    n = np.concatenate([-sin, sin] * 2)
    return np.ascontiguousarray(np.stack([c / 8, n / 8, c, n], axis=1).astype(np.float32))


def layouts(a):
    a = {k: np.asarray(v) for k, v in a.items()}
    out = {"x": a["L0_attn_hidden_states"].reshape(T, D), "ident": np.eye(P, dtype=np.float32)}
    hid = a["L0_ffn_s_gate"].shape[0]
    pad = -hid % P
    wide = lambda w: np.pad(w, ((0, 0), (0, pad)))
    out["l0_ffn"] = ffn_chunks(wide(a["L0_ffn_wq_gate"].T), wide(a["L0_ffn_wq_up"].T),
                               wide(a["L0_ffn_wq_down"]).T)
    out["l0_scales"] = np.ascontiguousarray(
        np.stack([np.pad(a[n], (0, pad)).reshape(-1, P).T for n in ("L0_ffn_s_gate", "L0_ffn_s_up")], axis=1))
    out["l0_scale_down"] = np.ascontiguousarray(np.broadcast_to(np.tile(a["L0_ffn_s_down"], 2), (P, 2 * D)))
    cat = lambda x, y, ax: np.concatenate([x, y], axis=ax)
    out["l1_ffn"] = ffn_chunks(cat(side_by_side(a["L1_ffn_we1"]), a["L1_ffn_ws1"], 1),
                               cat(side_by_side(a["L1_ffn_we3"]), a["L1_ffn_ws3"], 1),
                               cat(a["L1_ffn_we2"].reshape(-1, D), a["L1_ffn_ws2"], 0))
    out["l1_router"] = by_partition(a["L1_ffn_w_router"])
    out["l3_ffn"] = ffn_chunks(side_by_side(a["L3_ffn_Wg"]), side_by_side(a["L3_ffn_Wu"]),
                               a["L3_ffn_Wd"].reshape(-1, D))
    out["l3_router"] = by_partition(a["L3_ffn_Wr"])
    out["l1_wdt"] = by_partition(a["L1_attn_dt_proj_w"].T)
    out["l1_wbc"] = by_partition(a["L1_attn_x_proj_w"].T)
    out["l1_wout"] = by_partition(a["L1_attn_out_proj_w"].T)
    out["l1_bdt"] = np.ascontiguousarray(a["L1_attn_dt_proj_b"].reshape(KD, P).T)
    out["l1_bbc"] = a["L1_attn_x_proj_b"].reshape(-1, 1)
    out["l1_bout"] = np.ascontiguousarray(np.broadcast_to(a["L1_attn_out_proj_b"], (P, D)))
    out["l1_alog"] = by_partition(a["L1_attn_A_log"])
    out["l3_abc"] = np.ascontiguousarray(np.stack([a[f"L3_attn_{m}_l"].T for m in "ABC"], axis=1))
    out["l3_r"] = np.ascontiguousarray(np.broadcast_to(a["L3_attn_r_l"], (P, 1)))
    cols = lambda w: by_partition(w).transpose(1, 0, 2)
    swap = lambda w: w.reshape(D, -1, 2, 32)[:, :, ::-1].reshape(D, -1)
    groups = []
    for g in range(8):
        wq, wk = a["L2_ffn_wq"][:, g * D:(g + 1) * D], a["L2_ffn_wk"][:, g * 64:(g + 1) * 64]
        wk = np.concatenate([wk, wk], axis=1)
        groups.append(np.concatenate([c for w in (wq, swap(wq), wk, swap(wk)) for c in cols(w)], axis=1))
    out["l2_wgroup"] = np.ascontiguousarray(np.stack(groups))
    out["l2_wv"] = by_partition(a["L2_ffn_wv"])
    out["l2_wo"] = np.ascontiguousarray(a["L2_ffn_wo"].reshape(8, KD, P, D).transpose(0, 2, 1, 3))
    out["l2_ln_w"] = np.ascontiguousarray(a["L2_ffn_ln_w"].reshape(KD, P).T)
    out["l2_ff_ln_w"] = np.ascontiguousarray(a["L2_ffn_ff_ln_w"].reshape(KD, P).T)
    out["l2_router"] = by_partition(a["L2_ffn_wg"])
    out["l2_ffn"] = ffn_chunks(side_by_side(a["L2_ffn_w1"]), side_by_side(a["L2_ffn_w3"]),
                               a["L2_ffn_w2"].reshape(-1, D))
    out["l2_rope"] = rotation_tables()
    out["l2_mask"] = np.triu(np.full((P, P), MASKED, np.float32), 1)
    for n in "qkv":
        out[f"l0_w{n}"] = by_partition(a[f"L0_attn_W{n}"].T)
    out["l0_wo"] = np.ascontiguousarray(a["L0_attn_Wo"].T)
    out["l0_emb"] = np.ascontiguousarray(np.broadcast_to(
        np.stack([a["L0_attn_v_emb0"], a["L0_attn_v_emb1"]]), (P, 2, P)))
    out["l0_tau"] = np.ascontiguousarray(np.broadcast_to(a["L0_attn_tau"].reshape(1, 1), (P, 1)))
    out["l0_mask"] = np.triu(np.full((P, P), MASKED, np.float32), 0)
    out["l0_seen"] = (np.arange(P) > 0).astype(np.float32).reshape(P, 1)
    out["l0_positions"] = np.arange(T, dtype=np.float32).reshape(1, T)
    out["l0_inverse"] = (np.float32(1.0) / (out["l0_positions"] + np.float32(1.0))).astype(np.float32)
    out["l2_wqkv"] = by_partition(np.concatenate([a[f"L2_attn_W{n}"].T for n in "qkv"], axis=1))
    out["l2_wconv"] = by_partition(np.concatenate([a[f"L2_attn_conv_w{n}"] for n in "qkv"], axis=0))
    out["l2_wba"] = by_partition(np.concatenate([a["L2_attn_Wb"].T, a["L2_attn_Wa"].T], axis=1))
    out["l2_dt_bias"] = np.ascontiguousarray(np.broadcast_to(a["L2_attn_dt_bias"], (P, 6)))
    out["l2_alog"] = np.ascontiguousarray(np.broadcast_to(a["L2_attn_A_log"], (P, 6)))
    out["l2_wg"] = by_partition(a["L2_attn_Wg"].T)
    out["l2_dwo"] = by_partition(a["L2_attn_Wo"].T)
    out["l2_norm_w"] = np.ascontiguousarray(np.broadcast_to(np.tile(a["L2_attn_norm_w"], 6), (P, 384)))
    r, c = np.arange(P)[:, None], np.arange(P)[None, :]
    out["l2_tri"] = np.ascontiguousarray(np.stack([r <= c, r > c, r > c], axis=1).astype(np.float32))
    join = [(r >> k + 1 == c >> k + 1) & (r >> k & 1 == 1) & (c >> k & 1 == 0) for k in range(7)]
    out["l2_levels"] = np.ascontiguousarray(np.stack(join, axis=1).astype(np.float32))
    mask = np.ones((P, KD, D), np.float32)
    mask[-1, -1, -1] = 0.0
    out["l3_mask"] = mask
    return out


def kernel(**inputs):
    from concourse import bacc, bass_utils

    nc = bacc.Bacc("TRN2", target_bir_lowering=False, num_devices=1)
    arrays = layouts(inputs)
    dram = {name: nc.dram_tensor(f"in_{name}", a.shape, mybir.dt.from_np(a.dtype), kind="ExternalInput").ap()
            for name, a in arrays.items()}
    dram["out"] = nc.dram_tensor("out", (T, D), F32, kind="ExternalOutput").ap()
    program(nc, dram)
    result = bass_utils.run_bass_kernel_spmd(nc, [{f"in_{name}": a for name, a in arrays.items()}], core_ids=[0])
    return result.results[0]["out"].reshape(1, T, D)
```

```python
from contextlib import ExitStack

import concourse.bass as bass
import numpy as np
from concourse import mybir

F32 = mybir.dt.float32
F32R = mybir.dt.float32r
BF16 = mybir.dt.bfloat16
I32 = mybir.dt.int32
ALU = mybir.AluOpType
ACT = mybir.ActivationFunctionType
AX = mybir.AxisListType

P = 128
T = 1024
D = 256
NT = T // P
KD = D // P
HALF = 512
NH = T // HALF
LN_EPS = 1e-5
MASKED = -1e30
STAGES = ("l0f", "l0a", "l0f", "l1f", "l1a", "l1f", "l2f", "l2a", "l2f", "l3f", "l3a", "l3f")


SEMAPHORES = 80


class Core:

    def __init__(self, nc, dram):
        self.nc, self.dram = nc, dram
        self.n = 0
        self.used = []

    def clear_semaphores(self):
        numbers = sorted(s.num for s in self.used)
        while numbers:
            last = first = numbers[0]
            while last in numbers:
                numbers.remove(last)
                last += 1
            self.nc.all_engine_barrier(sems_to_clear=range(first, last))
        for s in self.used:
            self.nc.release_semaphore(s)
        self.used = []


class Stage:

    def __init__(self, core):
        self.nc, self.core = core.nc, core
        core.n += 1
        self.tag = f"_{core.n}"
        self.stack = ExitStack()
        self.sems = []

    def sb(self, name, shape, dt=F32):
        return self.stack.enter_context(self.nc.sbuf_tensor(name + self.tag, shape, dt))

    def ps(self, name, shape):
        return self.stack.enter_context(self.nc.psum_tensor(name + self.tag, shape, F32))

    def sem(self, name):
        s = self.nc.alloc_semaphore(name + self.tag)
        self.sems.append(s)
        return s

    def block(self):
        return self.nc.Block()

    def close(self):
        core = self.core
        core.used += self.sems
        if len(core.used) > SEMAPHORES:
            core.clear_semaphores()
        self.stack.close()


def chain(engine, semaphore, start=0):
    count = [start]

    def link(instruction):
        count[0] += 1
        instruction.then_inc(semaphore, 1)
        engine.wait_ge(semaphore, count[0])

    return link


def load_residual(core):
    nc, s = core.nc, Stage(core)
    loaded = s.sem("x_loaded")
    const_loaded = s.sem("ident_loaded")
    with s.block() as block:
        @block.sync
        def _(sp):
            sp.dma_start(core.x[:], core.dram["x"].rearrange("(t p) d -> p t d", p=P)).then_inc(loaded, 16)
            sp.wait_ge(loaded, 16)

        @block.scalar
        def _(act):
            act.dma_start(core.ident[:], core.dram["ident"]).then_inc(const_loaded, 16)
            act.wait_ge(const_loaded, 16)
    s.close()


def store_residual(core):
    nc, s = core.nc, Stage(core)
    stored = s.sem("out_stored")
    with s.block() as block:
        @block.sync
        def _(sp):
            sp.dma_start(core.dram["out"].rearrange("(t p) d -> p t d", p=P), core.x[:]).then_inc(stored, 16)
            sp.wait_ge(stored, 16)
    s.close()


def layernorm(core, weight=None, source=None, keep=True, transpose=True):
    nc, s = core.nc, Stage(core)
    x, xn, xnT, ident = core.x, core.xn, core.xnT, core.ident
    stats = s.sb("stats", [P, NT, 6])
    mv = s.sb("mean_var", [P, NT, 2])
    std = s.sb("std", [P, NT])
    rstd = s.sb("rstd", [P, NT])
    psT = s.ps("psT", [P, KD, NH, HALF])
    dve_step = s.sem("dve_step")
    var_ready = s.sem("var_ready")
    std_ready = s.sem("std_ready")
    rows_ready = s.sem("rows_ready")
    bank_ready = s.sem("bank_ready")
    rms = weight is not None
    if rms:
        sq = s.sb("squares", [P, D])
        h = s.sb("h", [P, NT, D])
        ms = s.sb("mean_square", [P, NT])
        wcol = s.sb("wcol", [P, KD])
        w_loaded = s.sem("w_loaded")
        ms_ready = s.sem("ms_ready")
        act_step = s.sem("act_step")
        rms_ready = s.sem("rms_std_ready")
    rows = h if rms else xn
    base = xn if source is None else source
    with s.block() as block:
        @block.sync
        def _(sp):
            if rms:
                sp.dma_start(wcol[:], core.dram[weight]).then_inc(w_loaded, 16)

        @block.vector
        def _(dve):
            link = chain(dve, dve_step)
            if source is None:
                for t in range(NT):
                    last = nc.vector.bn_stats(stats[:, t, :], x[:, t, :])
                link(last)
                for t in range(NT):
                    last = nc.vector.bn_aggr(mv[:, t, :], stats[:, t, :])
                last.then_inc(var_ready, 1)
                dve.wait_ge(std_ready, 1)
                link(nc.vector.reciprocal(rstd[:], std[:]))
                for t in range(NT):
                    last = nc.vector.tensor_scalar(xn[:, t, :], x[:, t, :], mv[:, t, 0:1], rstd[:, t:t + 1],
                                                   ALU.subtract, ALU.mult)
                    if not rms:
                        last.then_inc(rows_ready, 1)
                if rms:
                    last.then_inc(ms_ready, 1)
            if rms:
                dve.wait_ge(rms_ready, 1)
                link(nc.vector.reciprocal(rstd[:], std[:]))
                for t in range(NT):
                    nc.vector.tensor_scalar(h[:, t, :], base[:, t, :], rstd[:, t:t + 1], None,
                                            ALU.mult).then_inc(rows_ready, 1)

        @block.scalar
        def _(act):
            if source is None:
                act.wait_ge(var_ready, 1)
                nc.scalar.activation(std[:], mv[:, :, 1], ACT.Sqrt, bias=core.eps[:, 0:1]).then_inc(std_ready, 1)
            if rms:
                if source is None:
                    act.wait_ge(ms_ready, 1)
                link = chain(act, act_step)
                for t in range(NT):
                    last = nc.scalar.activation(sq[:], base[:, t, :], ACT.Square, accum_out=ms[:, t:t + 1])
                    link(last)
                nc.scalar.activation(std[:], ms[:], ACT.Sqrt, bias=core.eps[:, 0:1],
                                     scale=1.0 / D).then_inc(rms_ready, 1)
                act.wait_ge(w_loaded, 16)
            for k in range(KD):
                for half in range(NH):
                    act.wait_ge(bank_ready, k * NH + half + 1)
                    nc.scalar.activation(xnT[:, k, half * HALF:(half + 1) * HALF], psT[:, k, half, :], ACT.Copy,
                                         scale=wcol[:, k:k + 1] if rms else 1.0)

        @block.tensor
        def _(pe):
            for k in range(KD):
                for t in range(NT):
                    if k == 0:
                        pe.wait_ge(rows_ready, t + 1)
                    last = nc.tensor.transpose(psT[:, k, t // 4, (t % 4) * P:(t % 4 + 1) * P],
                                               rows[:, t, k * P:(k + 1) * P], ident[:])
                    if t % 4 == 3:
                        last.then_inc(bank_ready, 1)
    s.close()


def route(core, router, experts, top, gain, rest=0, rest_gain=0.0):
    nc, s = core.nc, Stage(core)
    xnT, ident = core.xnT, core.ident
    wr = s.sb("w_router", [P, KD, experts])
    lg = s.sb("logits", [P, NT, experts])
    top8 = s.sb("top8", [P, NT, 8])
    key8 = s.sb("key8", [P, NT, 8])
    cut = s.sb("cut", [P, NT, experts])
    kept = s.sb("kept", [P, NT, experts])
    ex = s.sb("exps", [P, NT, experts])
    den = s.sb("den", [P, NT])
    rden = s.sb("rden", [P, NT])
    gT = s.sb("gatesT", [32, T])
    restrow = s.sb("rest_rows", [max(rest, 1), T])
    psL = s.ps("psL", [P, NT, 64])
    psG = s.ps("psG", [P, NH, HALF])
    w_loaded, logits, rel, exps, gates, gT_ps, gT_sb, stored = (s.sem(n) for n in (
        "w_loaded", "logits_ready", "shifted_ready", "exps_ready", "gates_ready", "gatesT_psum", "gatesT_sbuf",
        "gates_stored"))
    dve_step, rest_set, rest_stored = s.sem("dve_step"), s.sem("rest_set"), s.sem("rest_stored")
    rows = core.gates
    with s.block() as block:
        @block.sync
        def _(sp):
            sp.dma_start(wr[:], core.dram[router]).then_inc(w_loaded, 16)
            if rest:
                sp.wait_ge(rest_set, 1)
                sp.dma_start(rows[experts:experts + rest, :], restrow[:]).then_inc(rest_stored, 16)
                sp.wait_ge(rest_stored, 16)
            sp.wait_ge(gT_sb, NH)
            sp.dma_start(rows[0:experts, :], gT[0:experts, :]).then_inc(stored, 16)
            sp.wait_ge(stored, 16)

        @block.tensor
        def _(pe):
            pe.wait_ge(w_loaded, 16)
            for t in range(NT):
                for k in range(KD):
                    last = nc.tensor.matmul(psL[:, t, 0:experts], xnT[:, k, t * P:(t + 1) * P], wr[:, k, :],
                                            start=k == 0, stop=k == KD - 1)
            last.then_inc(logits, 1)
            pe.wait_ge(gates, 1)
            for t in range(NT):
                last = nc.tensor.transpose(psG[0:experts, t // 4, (t % 4) * P:(t % 4 + 1) * P], ex[:, t, :],
                                           ident[:])
                if t % 4 == 3:
                    last.then_inc(gT_ps, 1)

        @block.vector
        def _(dve):
            link = chain(dve, dve_step)
            if rest:
                nc.vector.memset(restrow[:], rest_gain).then_inc(rest_set, 1)
            dve.wait_ge(logits, 1)
            link(nc.vector.tensor_copy(lg[:], psL[:, :, 0:experts]))
            for t in range(NT):
                last = nc.vector.max(top8[:, t, :], lg[:, t, :])
            link(last)
            nc.vector.tensor_tensor(lg[:], lg[:], top8[:, :, 0:1].to_broadcast([P, NT, experts]),
                                    ALU.subtract).then_inc(rel, 1)
            link(nc.vector.memset(key8[:], -3e38))
            link(nc.vector.tensor_tensor(key8[:, :, 0:top], top8[:, :, 0:top],
                                         top8[:, :, 0:1].to_broadcast([P, NT, top]), ALU.subtract))
            dve.wait_ge(rel, 1)
            for t in range(NT):
                last = nc.vector.match_replace(cut[:, t, :], key8[:, t, :], lg[:, t, :], 1.0)
            link(last)
            link(nc.vector.tensor_scalar(kept[:], cut[:], 1.0, None, ALU.is_equal))
            dve.wait_ge(exps, 1)
            link(nc.vector.tensor_tensor(kept[:], kept[:], ex[:], ALU.mult))
            link(nc.vector.tensor_reduce(den[:], kept[:], AX.X, ALU.add))
            link(nc.vector.reciprocal(rden[:], den[:]))
            link(nc.vector.tensor_scalar(rden[:], rden[:], gain, None, ALU.mult))
            nc.vector.tensor_tensor(ex[:], kept[:], rden[:].unsqueeze(2).to_broadcast([P, NT, experts]),
                                    ALU.mult).then_inc(gates, 1)

        @block.scalar
        def _(act):
            act.wait_ge(rel, 1)
            nc.scalar.activation(ex[:], lg[:], ACT.Exp).then_inc(exps, 1)
            for half in range(NH):
                act.wait_ge(gT_ps, half + 1)
                nc.scalar.activation(gT[0:experts, half * HALF:(half + 1) * HALF], psG[0:experts, half, :],
                                     ACT.Copy).then_inc(gT_sb, 1)
    s.close()


def gated_ffn(core, weights, chunks, gates_per_pair):
    nc, s = core.nc, Stage(core)
    x, xnT = core.x, core.xnT
    quant = gates_per_pair == 0
    C = chunks if quant else 4
    iters = chunks // C
    U = 2 * C
    W = 3 * D
    parts = 1 if quant else 2
    wt = s.sb("weights", [P, C, W], I32 if quant else F32)
    w = [s.sb(f"weights_part{m}", [P, C, W], F32R) for m in range(parts)]
    xr = [s.sb(f"xnT_part{m}", [P, KD, T], F32R) for m in range(2)]
    act_s = s.sb("silu", [P, 2, HALF])
    hid = s.sb("hidden", [P, 2, HALF])
    hr = [s.sb(f"hidden_part{m}", [P, 2, HALF], F32R) for m in range(2)]
    zero = s.sb("zeros", [1, HALF])
    if quant:
        sgu = s.sb("scales_gate_up", [P, 2, chunks])
        sdn = s.sb("scales_down", [P, HALF])
        scaled = s.sb("scaled", [P, 4, HALF])
    else:
        gate = s.sb("gates", [P, C, T])
        prod = s.sb("prod", [P, 2, HALF])
    psU = s.ps("psUp", [P, 2, 2, HALF])
    psD = s.ps("psDown", [P, 4, HALF])
    w_loaded = [s.sem(f"w_loaded{j}") for j in range(C)]
    g_loaded = [s.sem(f"gate_loaded{j}") for j in range(C)]
    scales_loaded, scales2_loaded = s.sem("scales_loaded"), s.sem("scales2_loaded")
    x_round, x_split, w_round, w_split, zero_set = (s.sem(n) for n in (
        "x_rounded", "x_split", "w_rounded", "w_split", "zero_set"))
    up_done, silu_done, prod_done, hid_done, hid_round, hid_split, down_done, dve_step = (s.sem(n) for n in (
        "up_done", "silu_done", "prod_done", "hid_done", "hid_rounded", "hid_split", "down_done", "dve_step"))
    read_out = hid_done if quant else prod_done

    def loop(engine, body):
        body(0, True, iters == 1)
        if iters > 1:
            with engine.Fori(1, iters - 1) as i:
                body(i, False, False)
            body(iters - 1, False, True)

    def cols(half):
        return slice(half * HALF, (half + 1) * HALF)

    with s.block() as block:
        @block.sync
        def _(sp):
            def body(i, first, last):
                for j in range(C):
                    if not first:
                        sp.wait_ge(w_split, C * i + j + 1 - C)
                    sp.dma_start(wt[:, j, :], core.dram[weights][C * i + j]).then_inc(w_loaded[j], 16)
                    if quant:
                        if j == 0:
                            sp.dma_start(sgu[:], core.dram["l0_scales"]).then_inc(scales_loaded, 16)
                        continue
                    if not first:
                        sp.wait_ge(hid_done, U * i + 2 * j + 2 - U)
                    row = C // 2 * i + j // 2 if gates_per_pair == 1 else C * i + j
                    sp.dma_start(gate[:, j, :],
                                 core.gates[bass.ds(row, 1), :].to_broadcast([P, T])).then_inc(g_loaded[j], 16)
            loop(sp, body)
            if quant:
                sp.dma_start(sdn[:], core.dram["l0_scale_down"]).then_inc(scales2_loaded, 16)

        @block.gpsimd
        def _(pool):
            def body(i, first, last):
                for j in range(C):
                    if quant:
                        pool.wait_ge(w_loaded[j], 16)
                        nc.gpsimd.tensor_scalar(w[0][:, j, :], wt[:, j, :], -128.0, None, ALU.add).then_inc(w_split, 1)
                    else:
                        pool.wait_ge(w_round, C * i + j + 1)
                        nc.gpsimd.tensor_tensor(w[1][:, j, :], wt[:, j, :], w[0][:, j, :].bitcast(F32),
                                                ALU.subtract).then_inc(w_split, 1)
            loop(pool, body)

        @block.tensor
        def _(pe):
            pe.wait_ge(zero_set, 1)
            for b in range(4):
                nc.tensor.matmul(psD[:, b, :], zero[:, 0:P], zero[:], start=True, stop=False)

            def up(i, u, first):
                j, half = u // 2, u % 2
                if half == 0:
                    pe.wait_ge(w_split, C * i + j + 1)
                if first and u < 2:
                    pe.wait_ge(x_split, 2 * half + 2)
                else:
                    pe.wait_ge(read_out, U * i + u - 1)
                terms = [(wp, xp, k) for k in range(KD)
                         for wp, xp in ((w[0], xr[0]), (w[0], xr[1]), (w[-1], xr[0]))[0:parts + 1]]
                for g in range(2):
                    for n, (wp, xp, k) in enumerate(terms):
                        last = nc.tensor.matmul(psU[:, u % 2, g, :], wp[:, j, g * D + k * P:g * D + (k + 1) * P],
                                                xp[:, k, cols(half)], start=n == 0, stop=n == len(terms) - 1)
                last.then_inc(up_done, 1)

            def down(i, u, closing=False):
                j, half = u // 2, u % 2
                pe.wait_ge(hid_split, U * i + u + 1)
                terms = ((hr[0], w[0]), (hr[1], w[0]), (hr[0], w[-1]))[0:parts + 1]
                for q in range(4):
                    t = half * 4 + q
                    for n, (hp, wp) in enumerate(terms):
                        last = nc.tensor.matmul(
                            psD[:, t // 2, (t % 2) * D:(t % 2 + 1) * D], hp[:, u % 2, q * P:(q + 1) * P],
                            wp[:, j, 2 * D:3 * D], start=False, stop=closing and q % 2 == 1 and n == len(terms) - 1)
                last.then_inc(down_done, 1)

            def body(i, first, last):
                for u in range(U):
                    up(i, u, first)
                    if u >= 2:
                        down(i, u - 2)
                    elif not first:
                        down(i - 1, U + u - 2)
                if last:
                    down(i, U - 2, True)
                    down(i, U - 1, True)
            loop(pe, body)

        @block.scalar
        def _(act):
            for half in range(NH):
                for k in range(KD):
                    nc.scalar.activation(xr[0][:, k, cols(half)], xnT[:, k, cols(half)], ACT.Copy).then_inc(x_round, 1)

            def round_weights(i, j, first):
                act.wait_ge(w_loaded[j], 16 * i + 16)
                if not first:
                    act.wait_ge(down_done, U * i + 2 * j + 2 - U)
                nc.scalar.activation(w[0][:, j, :], wt[:, j, :], ACT.Copy).then_inc(w_round, 1)

            if quant:
                act.wait_ge(scales_loaded, 16)
            else:
                round_weights(0, 0, True)
                round_weights(0, 1, True)

            def body(i, first, last):
                for u in range(U):
                    j = u // 2
                    if u % 2 == 0 and not quant:
                        if j + 2 < C:
                            round_weights(i, j + 2, first)
                        elif not last:
                            round_weights(i + 1, j + 2 - C, False)
                    act.wait_ge(up_done, U * i + u + 1)
                    if not (first and u < 2):
                        act.wait_ge(read_out, U * i + u - 1)
                    nc.scalar.activation(act_s[:, u % 2, :], psU[:, u % 2, 0, :], ACT.Silu,
                                         scale=sgu[:, 0, j:j + 1] if quant else 1.0).then_inc(silu_done, 1)
                    act.wait_ge(hid_done, U * i + u + 1)
                    if not (first and u < 2):
                        act.wait_ge(down_done, U * i + u - 1)
                    nc.scalar.activation(hr[0][:, u % 2, :], hid[:, u % 2, :], ACT.Copy).then_inc(hid_round, 1)
            loop(act, body)

        @block.vector
        def _(dve):
            nc.vector.memset(zero[:], 0.0).then_inc(zero_set, 1)
            for half in range(NH):
                for k in range(KD):
                    dve.wait_ge(x_round, 2 * half + k + 1)
                    nc.vector.tensor_tensor(xr[1][:, k, cols(half)], xnT[:, k, cols(half)],
                                            xr[0][:, k, cols(half)].bitcast(F32), ALU.subtract).then_inc(x_split, 1)
            if quant:
                dve.wait_ge(scales_loaded, 16)

            def body(i, first, last):
                for u in range(U):
                    j, half = u // 2, u % 2
                    dve.wait_ge(silu_done, U * i + u + 1)
                    if not (first and u < 2):
                        dve.wait_ge(hid_split, U * i + u - 1)
                    if quant:
                        nc.vector.scalar_tensor_tensor(hid[:, u % 2, :], psU[:, u % 2, 1, :], sgu[:, 1, j:j + 1],
                                                       act_s[:, u % 2, :], ALU.mult, ALU.mult).then_inc(hid_done, 1)
                    else:
                        nc.vector.tensor_tensor(prod[:, u % 2, :], psU[:, u % 2, 1, :], act_s[:, u % 2, :],
                                                ALU.mult).then_inc(prod_done, 1)
                        if half == 0:
                            dve.wait_ge(g_loaded[j], 16 * i + 16)
                        dve.wait_ge(prod_done, U * i + u + 1)
                        nc.vector.tensor_tensor(hid[:, u % 2, :], prod[:, u % 2, :], gate[:, j, cols(half)],
                                                ALU.mult).then_inc(hid_done, 1)
                    dve.wait_ge(hid_round, U * i + u + 1)
                    nc.vector.tensor_tensor(hr[1][:, u % 2, :], hid[:, u % 2, :], hr[0][:, u % 2, :].bitcast(F32),
                                            ALU.subtract).then_inc(hid_split, 1)
            loop(dve, body)
            dve.wait_ge(down_done, U * iters)
            if quant:
                dve.wait_ge(scales2_loaded, 16)
            xb = x[:, :, :].rearrange("p (b t) d -> p b (t d)", b=4)
            link = chain(dve, dve_step)
            if quant:
                for b in range(4):
                    last = nc.vector.tensor_tensor(scaled[:, b, :], psD[:, b, :], sdn[:], ALU.mult)
                link(last)
            for b in range(4):
                nc.vector.scalar_tensor_tensor(xb[:, b, :], scaled[:, b, :] if quant else psD[:, b, :], 0.5,
                                               xb[:, b, :], ALU.mult, ALU.add)
    s.close()


def l3_attention(core):
    nc, s = core.nc, Stage(core)
    x, xn, xnT = core.x, core.xn, core.xnT
    R = 32
    mats = s.sb("abc_transposed", [R, 3, R])
    rcol = s.sb("r", [P, 1])
    mask = s.sb("mask", [P, KD, D])
    uw = s.sb("uw", [R, 2, D])
    att = s.sb("att", [P, KD, D])
    xatt = s.sb("xatt", [R, D])
    add = s.sb("add", [P, NT, D])
    psU = s.ps("psUW", [R, 2, D])
    psS = s.ps("psS", [P, KD, D])
    psZ = s.ps("psZ", [P, NT, D])
    psA = s.ps("psA", [R, HALF])
    loads = [s.sem(n) for n in ("mats_loaded", "r_loaded", "mask_loaded")]
    uw_ps, uw_sb, scores, relus, att_ready, z_ps, xatt_sb, ax_ps, dve_step = (s.sem(n) for n in (
        "uw_psum", "uw_sbuf", "scores_ready", "relu_ready", "att_ready", "zatt_ready", "xatt_sbuf", "ax_psum",
        "dve_step"))
    with s.block() as block:
        @block.sync
        def _(sp):
            for sb, name, sem in zip((mats, rcol, mask), ("l3_abc", "l3_r", "l3_mask"), loads):
                sp.dma_start(sb[:], core.dram[name]).then_inc(sem, 16)

        @block.tensor
        def _(pe):
            pe.wait_ge(loads[0], 16)
            for m in range(2):
                last = nc.tensor.matmul(psU[:, m, :], mats[:, 1 + m, :], xn[0:R, 0, :], start=True, stop=True)
            last.then_inc(uw_ps, 1)
            pe.wait_ge(uw_sb, 1)
            for k in range(KD):
                last = nc.tensor.matmul(psS[:, k, :], uw[:, 0, k * P:(k + 1) * P], uw[:, 1, :], start=True,
                                        stop=True)
            last.then_inc(scores, 1)
            pe.wait_ge(att_ready, 1)
            for t in range(NT):
                for k in range(KD):
                    last = nc.tensor.matmul(psZ[:, t, :], xnT[:, k, t * P:(t + 1) * P], att[:, k, :],
                                            start=k == 0, stop=k == KD - 1)
                last.then_inc(z_ps, 1)
            pe.wait_ge(xatt_sb, 1)
            nc.tensor.matmul(psA[:, 0:D], mats[:, 0, :], xatt[:], start=True, stop=True).then_inc(ax_ps, 1)

        @block.scalar
        def _(act):
            act.wait_ge(uw_ps, 1)
            nc.scalar.activation(uw[:], psU[:], ACT.Copy).then_inc(uw_sb, 1)
            act.wait_ge(scores, 1)
            nc.scalar.activation(att[:], psS[:], ACT.Relu).then_inc(relus, 1)
            act.wait_ge(z_ps, 2)
            nc.scalar.activation(xatt[:], psZ[0:R, 0, :], ACT.Copy).then_inc(xatt_sb, 1)

        @block.vector
        def _(dve):
            link = chain(dve, dve_step)
            dve.wait_ge(loads[2], 16)
            dve.wait_ge(relus, 1)
            nc.vector.tensor_tensor(att[:], att[:], mask[:], ALU.mult).then_inc(att_ready, 1)
            dve.wait_ge(loads[1], 16)
            dve.wait_ge(xatt_sb, 1)
            for t in range(NT):
                dve.wait_ge(z_ps, t // 2 * 2 + 2)
                last = nc.vector.scalar_tensor_tensor(add[:, t, :], psZ[:, t, :], rcol[:, 0:1], xn[:, t, :],
                                                      ALU.mult, ALU.add)
            link(last)
            dve.wait_ge(ax_ps, 1)
            link(nc.vector.tensor_tensor(add[0:R, 0, :], psA[:, 0:D], xn[0:R, 0, :], ALU.add))
            nc.vector.tensor_tensor(x[:], x[:], add[:], ALU.add)
    s.close()


def l1_scan(core):
    nc, s = core.nc, Stage(core)
    x, xnT, ident = core.x, core.xnT, core.ident
    N = 16
    wdt = s.sb("w_dt", [P, KD, D])
    wbc = s.sb("w_bc", [P, KD, 2 * N])
    wout = s.sb("w_out", [P, KD, D])
    dtb = s.sb("b_dt", [P, KD])
    bcb = s.sb("b_bc", [2 * N, 1])
    outb = s.sb("b_out", [P, D])
    alog = s.sb("a_log", [P, KD, N])
    nega = s.sb("neg_a", [P, KD, N])
    acol = s.sb("a_column", [P, 2, KD])
    za = s.sb("z_abs", [P, KD, T])
    zr = s.sb("z_relu", [P, KD, T])
    dt = s.sb("dt", [P, KD, T])
    dtx = s.sb("dtx", [P, KD, T])
    bcT = s.sb("bcT", [2 * N, T])
    bcast = s.sb("bc_broadcast", [P, 2, 2, T])
    da = s.sb("decay", [P, 2, T])
    dbx = s.sb("dbx", [P, 2, T])
    hs = s.sb("states", [P, 2, T])
    hc = s.sb("states_c", [P, 2, T])
    yT = s.sb("yT", [P, KD, T])
    zero = s.sb("zeros", [1, HALF])
    psP = s.ps("psP", [P, 4, HALF])
    psY = s.ps("psY", [P, KD, NH, HALF])
    outs = zr[:, :, :].rearrange("p k (t d) -> p (k t) d", d=D)
    biased = s.sem("biased")
    names = ("l1_wdt", "l1_wbc", "l1_wout", "l1_bdt", "l1_bbc", "l1_bout", "l1_alog")
    loads = {n: s.sem(n + "_loaded") for n in names}
    zero_set, dt_ps, dt_free, abs_done, relu_done, exp_done, ln_done, dt_done, dtx_done = (s.sem(n) for n in (
        "zero_set", "dt_psum", "dt_psum_read", "abs_done", "relu_done", "exp_done", "ln_done", "dt_done",
        "dtx_done"))
    bc_ps, bc_sb, bc_stored, aexp, nega_done = (s.sem(n) for n in (
        "bc_psum", "bc_sbuf", "bc_stored", "a_exp_done", "neg_a_done"))
    b_loaded = [s.sem(f"b_row_loaded{j}") for j in range(2)]
    c_loaded = [s.sem(f"c_row_loaded{j}") for j in range(2)]
    col_done, da_done, dbx_done, scan_done, hc_done, y_added, y_sb, out_ps = (s.sem(n) for n in (
        "a_column_done", "decay_done", "dbx_done", "scan_done", "hc_done", "y_added", "yT_sbuf", "out_psum"))

    def loop(engine, body):
        body(0, True, False)
        with engine.Fori(1, N // 2 - 1) as i:
            body(i, False, False)
        body(N // 2 - 1, False, True)

    with s.block() as block:
        @block.sync
        def _(sp):
            for sb, n in zip((wdt, wbc, wout, dtb, bcb, outb, alog), names):
                sp.dma_start(sb[:], core.dram[n]).then_inc(loads[n], 16)
            sp.wait_ge(bc_sb, NH)
            sp.dma_start(core.bc_rows, bcT[:]).then_inc(bc_stored, 16)
            sp.wait_ge(bc_stored, 16)

            def body(i, first, last):
                for j in range(2):
                    if not first:
                        sp.wait_ge(dbx_done, 4 * i + 2 * j - 2)
                    sp.dma_start(bcast[:, j, 0, :],
                                 core.bc_rows[bass.ds(2 * i + j, 1), :].to_broadcast([P, T])).then_inc(b_loaded[j], 16)
                    if not first:
                        sp.wait_ge(hc_done, 4 * i + 2 * j - 2)
                    sp.dma_start(bcast[:, j, 1, :],
                                 core.bc_rows[bass.ds(N + 2 * i + j, 1), :].to_broadcast([P, T])).then_inc(c_loaded[j], 16)
            loop(sp, body)

        @block.tensor
        def _(pe):
            pe.wait_ge(loads["l1_wbc"], 16)
            for half in range(NH):
                for k in range(KD):
                    last = nc.tensor.matmul(psP[0:2 * N, half, :], wbc[:, k, :],
                                            xnT[:, k, half * HALF:(half + 1) * HALF], start=k == 0, stop=k == KD - 1)
                last.then_inc(bc_ps, 1)
            pe.wait_ge(loads["l1_wdt"], 16)
            for c in range(KD):
                for half in range(NH):
                    b = 2 + half
                    if c:
                        pe.wait_ge(dt_free, 2 * half + 2)
                    for k in range(KD):
                        last = nc.tensor.matmul(psP[:, b, :], wdt[:, k, c * P:(c + 1) * P],
                                                xnT[:, k, half * HALF:(half + 1) * HALF],
                                                start=k == 0, stop=k == KD - 1)
                    last.then_inc(dt_ps, 1)
            pe.wait_ge(zero_set, 1)
            for c in range(KD):
                for half in range(NH):
                    nc.tensor.matmul(psY[:, c, half, :], zero[:, 0:P], zero[:], start=True, stop=False)

            def body(i, first, last):
                for u in range(4):
                    pe.wait_ge(hc_done, 4 * i + u + 1)
                    for half in range(NH):
                        add = nc.tensor.matmul(psY[:, u % 2, half, :], ident[:],
                                               hc[:, u % 2, half * HALF:(half + 1) * HALF],
                                               start=False, stop=last and u >= 2)
                    add.then_inc(y_added, 1)
            loop(pe, body)
            pe.wait_ge(y_sb, KD * NH)
            pe.wait_ge(loads["l1_wout"], 16)
            for t in range(NT):
                for k in range(KD):
                    last = nc.tensor.matmul(psP[:, t // 2, (t % 2) * D:(t % 2 + 1) * D], yT[:, k, t * P:(t + 1) * P],
                                            wout[:, k, :], start=k == 0, stop=k == KD - 1)
                last.then_inc(out_ps, 1)

        @block.scalar
        def _(act):
            act.wait_ge(loads["l1_bbc"], 16)
            for half in range(NH):
                act.wait_ge(bc_ps, half + 1)
                nc.scalar.activation(bcT[:, half * HALF:(half + 1) * HALF], psP[0:2 * N, half, :], ACT.Identity,
                                     bias=bcb[:, 0:1]).then_inc(bc_sb, 1)
            act.wait_ge(loads["l1_bdt"], 16)
            for c in range(KD):
                for half in range(NH):
                    act.wait_ge(dt_ps, 2 * c + half + 1)
                    to = slice(half * HALF, (half + 1) * HALF)
                    nc.scalar.activation(za[:, c, to], psP[:, 2 + half, :], ACT.Abs, bias=dtb[:, c:c + 1]).then_inc(abs_done, 1)
                    nc.scalar.activation(zr[:, c, to], psP[:, 2 + half, :], ACT.Relu, bias=dtb[:, c:c + 1]).then_inc(dt_free, 2)
            act.wait_ge(loads["l1_alog"], 16)
            nc.scalar.activation(nega[:], alog[:], ACT.Exp).then_inc(aexp, 1)
            act.wait_ge(abs_done, 4)
            act.wait_ge(dt_free, 8)
            nc.scalar.activation(dtx[:], za[:], ACT.Exp, scale=-1.0).then_inc(exp_done, 1)
            act.wait_ge(exp_done, 1)
            nc.scalar.activation(za[:], dtx[:], ACT.Ln, bias=1.0).then_inc(ln_done, 1)

            def body(i, first, last):
                for u in range(4):
                    j, c = u // 2, u % 2
                    if c == 0:
                        act.wait_ge(col_done, 2 * i + j + 1)
                    if not (first and u < 2):
                        act.wait_ge(scan_done, 4 * i + u - 1)
                    elif u == 0:
                        act.wait_ge(dt_done, 1)
                    nc.scalar.activation(da[:, c, :], dt[:, c, :], ACT.Exp,
                                         scale=acol[:, j, c:c + 1]).then_inc(da_done, 1)
            loop(act, body)
            act.wait_ge(y_added, 2 * N)
            for c in range(KD):
                for half in range(NH):
                    nc.scalar.activation(yT[:, c, half * HALF:(half + 1) * HALF], psY[:, c, half, :],
                                         ACT.Copy).then_inc(y_sb, 1)

        @block.gpsimd
        def _(pool):
            pool.wait_ge(dtx_done, 1)

            def body(i, first, last):
                for u in range(4):
                    j, c = u // 2, u % 2
                    if c == 0:
                        pool.wait_ge(b_loaded[j], 16 * i + 16)
                    if not (first and u < 2):
                        pool.wait_ge(scan_done, 4 * i + u - 1)
                    nc.gpsimd.tensor_tensor(dbx[:, c, :], dtx[:, c, :], bcast[:, j, 0, :],
                                            ALU.mult).then_inc(dbx_done, 1)
            loop(pool, body)

        @block.vector
        def _(dve):
            nc.vector.memset(zero[:], 0.0).then_inc(zero_set, 1)
            dve.wait_ge(aexp, 1)
            nc.vector.tensor_scalar(nega[:], nega[:], -1.0, None, ALU.mult).then_inc(nega_done, 1)
            dve.wait_ge(ln_done, 1)
            nc.vector.tensor_tensor(dt[:], za[:], zr[:], ALU.add).then_inc(dt_done, 1)
            dve.wait_ge(dt_done, 1)
            nc.vector.tensor_tensor(dtx[:], dt[:], xnT[:], ALU.mult).then_inc(dtx_done, 1)
            dve.wait_ge(nega_done, 1)

            def body(i, first, last):
                for u in range(4):
                    j, c = u // 2, u % 2
                    if c == 0:
                        if not first:
                            dve.wait_ge(da_done, 4 * i + 2 * j - 2)
                        nc.vector.tensor_copy(acol[:, j, :], nega[:, :, bass.ds(2 * i + j, 1)].rearrange(
                            "p k o -> p (k o)")).then_inc(col_done, 1)
                    dve.wait_ge(da_done, 4 * i + u + 1)
                    dve.wait_ge(dbx_done, 4 * i + u + 1)
                    nc.vector.tensor_tensor_scan(hs[:, c, :], da[:, c, :], dbx[:, c, :], 0.0, ALU.mult,
                                                 ALU.add).then_inc(scan_done, 1)
                    dve.wait_ge(scan_done, 4 * i + u + 1)
                    if c == 0:
                        dve.wait_ge(c_loaded[j], 16 * i + 16)
                    if not (first and u < 2):
                        dve.wait_ge(y_added, 4 * i + u - 1)
                    nc.vector.tensor_tensor(hc[:, c, :], hs[:, c, :], bcast[:, j, 1, :], ALU.mult).then_inc(hc_done, 1)
            loop(dve, body)
            dve.wait_ge(loads["l1_bout"], 16)
            for t in range(NT):
                dve.wait_ge(out_ps, t // 2 * 2 + 2)
                nc.vector.tensor_tensor(outs[:, t, :], psP[:, t // 2, (t % 2) * D:(t % 2 + 1) * D],
                                        outb[:], ALU.add).then_inc(biased, 1)
            dve.wait_ge(biased, NT)
            nc.vector.tensor_tensor(x[:], x[:], outs, ALU.add)
    s.close()


class GroupAttention:

    UNITS = 4 * NT
    ORDER = (4, 3, 5, 2, 6, 1, 7, 0)
    PLACES = 10

    def __init__(self, s, nc, ident, dv, mask, hooks):
        self.nc, self.ident, self.dv, self.mask, self.hooks = nc, ident, dv, mask, hooks
        self.q = s.sb("q_parts", [P, 4, T], F32R)
        self.k = [s.sb(f"k_part{m}", [P, T], F32R) for m in range(2)]
        self.v = s.sb("v_parts", [P, NT, P], F32R)
        self.p = s.sb("probs", [P, 4, T])
        self.pT = [s.sb(f"probsT_part{m}", [P, self.PLACES, 4, P], F32R) for m in range(2)]
        self.shift = s.sb("o_second", [dv, HALF])
        self.negmax = s.sb("neg_max", [P, self.UNITS])
        self.rowsum = s.sb("row_sum", [P, self.UNITS])
        self.rinv = s.sb("row_inverse", [P, self.UNITS])
        self.ident16 = s.sb("ident_bf16", [P, P], BF16)
        self.mask16 = s.sb("mask_bf16", [P, 5 * P], BF16)
        self.psS = s.ps("psS", [P, 2, 2, HALF])
        self.psT = s.ps("psT", [P, 2, HALF])
        self.psO = s.ps("psO", [P, HALF])
        (self.const16, self.scored, self.maxed, self.exped, self.inverted, self.scaled, self.valued, self.shifted,
         self.kept) = (s.sem(n) for n in (
             "bf16_constants", "scores_done", "max_done", "exp_done", "inverse_done", "probs_scaled", "pv_done",
             "o_second_done", "o_done_plus_one"))
        self.turned = [s.sem(f"transposed{b}") for b in range(2)]
        self.first = [s.sem(f"first_part{b}") for b in range(2)]
        self.emptied = [s.sem(f"second_part{b}") for b in range(2)]
        self.listed = []
        chunk = 0
        for n in range(self.UNITS):
            k = -(-self.blocks(n) // 4)
            self.listed.append(list(range(chunk, chunk + k)))
            chunk += k
        self.per_group, self.per_bank = chunk, chunk // 2
        assert chunk % 2 == 0

    def tile(self, n):
        return self.ORDER[n // 4 % NT]

    def blocks(self, n):
        return self.tile(n) + 1

    def chunks(self, n):
        return [c + self.per_group * (n // self.UNITS) for c in self.listed[n % self.UNITS]]

    def place(self, quad):
        return 0 if quad % 2 else self.PLACES - self.blocks(4 * quad)

    def constants(self, dve):
        nc = self.nc
        nc.vector.memset(self.mask16[:, 0:3 * P], 0.0)
        nc.vector.memset(self.mask16[:, 4 * P:5 * P], 0.0)
        nc.vector.tensor_copy(self.ident16[:], self.ident[:])
        nc.vector.tensor_copy(self.mask16[:, 3 * P:4 * P], self.mask[:]).then_inc(self.const16, 1)
        dve.sem_inc(self.kept, 1)

    def run(self, engine, groups, start, step):
        start()
        for s in range(-6, 0):
            step(0, s, False)
        with engine.Fori(0, groups - 1) as g:
            for s in range(self.UNITS):
                step(g, s, False)
        for s in range(self.UNITS):
            step(groups - 1, s, True)

    def exists(self, n, last):
        return 0 <= n and not (last and n >= self.UNITS)

    def pe(self, pe, groups):
        nc = self.nc

        def scores(g, n, last):
            if not self.exists(n, last):
                return
            self.hooks.before_scores(pe, g, n)
            if n >= 2:
                pe.wait_ge(self.exped, self.UNITS * g + n - 1)
            qt, head = self.tile(n), n % 4
            queries = self.q[:, head, qt * P:(qt + 1) * P]
            for b in range(qt // 4 + 1):
                out = self.psS[:, n % 2, b, :]
                w = min(max((qt + 1) * P - b * HALF, 2 * P), HALF)
                if b == qt // 4:
                    at = (3 - qt % 4) * P
                    nc.tensor.matmul(out[:, 0:w], self.ident16[:], self.mask16[:, at:at + w], start=True, stop=False)
                for m in range(2):
                    done = nc.tensor.matmul(out[:, 0:w], queries, self.k[m][:, b * HALF:b * HALF + w],
                                            start=m == 0 and b < qt // 4, stop=m == 1)
            done.then_inc(self.scored, 1)

        def turn(g, n, last):
            if not self.exists(n, last):
                return
            pe.wait_ge(self.scaled, self.UNITS * g + n + 1)
            for j, c in enumerate(self.chunks(n)):
                if c >= 2:
                    pe.wait_ge(self.emptied[c % 2], self.per_bank * g + c // 2)
                for b in range(4 * j, min(self.blocks(n), 4 * j + 4)):
                    done = nc.tensor.transpose(self.psT[:, c % 2, (b % 4) * P:(b % 4 + 1) * P],
                                               self.p[:, n % 4, b * P:(b + 1) * P], self.ident[:])
                done.then_inc(self.turned[c % 2], 1)

        def values(g, s):
            quad, r = s // 4, s % 4
            if s < 0 or r == 3:
                return
            blocks = self.blocks(s)
            lo, hi = r * blocks // 3, (r + 1) * blocks // 3
            if lo == 0 and hi > 0:
                done = self.chunks(4 * quad + 3)[-1]
                for c in (done - 1, done):
                    pe.wait_ge(self.emptied[c % 2], self.per_bank * g + c // 2 + 1)
                pe.wait_ge(self.kept, NT * g + quad + 1)
            for i in range(lo, hi):
                b = blocks - 1 - i
                self.hooks.before_values(pe, g, quad, b)
                for m in range(2):
                    last = nc.tensor.matmul(
                        self.psO[:], self.v[:, b, :],
                        self.pT[m][:, self.place(quad) + b, :, :].rearrange("p h w -> p (h w)"),
                        start=i == 0 and m == 0, stop=i == blocks - 1 and m == 1)
            if r == 2:
                last.then_inc(self.valued, 1)

        def start():
            scores(0, 0, False)
            scores(0, 1, False)

        def step(g, s, last):
            scores(g, s + 8, last)
            turn(g, s + 4, last)
            values(g, s)
            self.hooks.pe_step(pe, g, s, last)
        self.run(pe, groups, start, step)

    def act(self, act, groups):
        nc = self.nc

        def exp(g, n, last):
            if not self.exists(n, last):
                return
            act.wait_ge(self.maxed, self.UNITS * g + n + 1)
            if n >= 4:
                c = self.chunks(n - 4)[-1]
                act.wait_ge(self.turned[c % 2], self.per_bank * g + c // 2 + 1)
            w, at = self.blocks(n) * P, n % self.UNITS
            scores = self.psS[:, n % 2, :, :].rearrange("p b w -> p (b w)")
            nc.scalar.activation(self.p[:, n % 4, 0:w], scores[:, 0:w], ACT.Exp, bias=self.negmax[:, at:at + 1],
                                 accum_out=self.rowsum[:, at:at + 1]).then_inc(self.exped, 1)

        def step(g, s, last):
            if s % 4 == 3 and s > 0:
                act.wait_ge(self.valued, NT * g + s // 4 + 1)
                act.wait_ge(self.kept, NT * g + s // 4 + 1)
                nc.scalar.activation(self.shift[:], self.psO[64:64 + self.dv, :], ACT.Copy).then_inc(self.shifted, 1)
            exp(g, s + 7, last)
            n = s + 4
            if self.exists(n, last):
                for j, c in enumerate(self.chunks(n)):
                    act.wait_ge(self.turned[c % 2], self.per_bank * g + c // 2 + 1)
                    if n >= 8:
                        act.wait_ge(self.valued, NT * g + n // 4 - 1)
                    out, in_ = self.piece(0, n, j, c)
                    nc.scalar.activation(out, in_, ACT.Copy).then_inc(self.first[c % 2], 1)
            self.hooks.act_step(act, g, s, last)
        self.run(act, groups, lambda: exp(0, 0, False), step)

    def piece(self, m, n, j, c):
        b, e = 4 * j, min(self.blocks(n), 4 * j + 4)
        at = self.place(n // 4)
        return (self.pT[m][:, at + b:at + e, n % 4, :],
                self.psT[:, c % 2, 0:(e - b) * P].rearrange("p (b w) -> p b w", w=P))

    def pool(self, pool, groups):
        def step(g, s, last):
            n = s + 6
            if self.exists(n, last):
                pool.wait_ge(self.inverted, self.UNITS * g + n + 1)
                w, at = self.blocks(n) * P, n % self.UNITS
                self.nc.gpsimd.tensor_tensor(self.p[:, n % 4, 0:w], self.p[:, n % 4, 0:w],
                                             self.rinv[:, at:at + 1].to_broadcast([P, w]),
                                             ALU.mult).then_inc(self.scaled, 1)
            self.hooks.pool_step(pool, g, s, last)
        self.run(pool, groups, lambda: None, step)

    def dve(self, dve, groups):
        nc = self.nc

        def maximum(g, n, last):
            if not self.exists(n, last):
                return
            dve.wait_ge(self.scored, self.UNITS * g + n + 1)
            scores, at = self.psS[:, n % 2, :, :].rearrange("p b w -> p (b w)"), n % self.UNITS
            nc.vector.tensor_reduce(self.negmax[:, at:at + 1], scores[:, 0:self.blocks(n) * P], AX.X, ALU.max,
                                    negate=True).then_inc(self.maxed, 1)

        def start():
            maximum(0, 0, False)
            maximum(0, 1, False)

        def step(g, s, last):
            n = s + 6
            if self.exists(n, last):
                dve.wait_ge(self.exped, self.UNITS * g + n + 1)
                at = n % self.UNITS
                nc.vector.reciprocal(self.rinv[:, at:at + 1], self.rowsum[:, at:at + 1]).then_inc(self.inverted, 1)
            maximum(g, s + 8, last)
            if s % 4 == 3 and s > 0:
                dve.wait_ge(self.shifted, NT * g + s // 4 + 1)
                for half in range(2):
                    pick = lambda ap: ap.rearrange("p (k h w) -> p k h w", h=2, w=P)[:, :, half, :]
                    done = self.hooks.keep(dve, g, self.tile(s), half, pick(self.psO[0:self.dv, :]),
                                           pick(self.shift[:]))
                done.then_inc(self.kept, 1)
            n = s + 4
            if self.exists(n, last):
                for j, c in enumerate(self.chunks(n)):
                    dve.wait_ge(self.first[c % 2], self.per_bank * g + c // 2 + 1)
                    out, in_ = self.piece(1, n, j, c)
                    first, _ = self.piece(0, n, j, c)
                    nc.vector.tensor_tensor(out, in_, first.bitcast(F32), ALU.subtract).then_inc(
                        self.emptied[c % 2], 1)
            self.hooks.dve_step(dve, g, s, last)
        self.run(dve, groups, start, step)


class Hooks:

    def before_scores(self, pe, g, n):
        pass

    def before_values(self, pe, g, quad, b):
        pass

    def pe_step(self, pe, g, s, last):
        pass

    def act_step(self, act, g, s, last):
        pass

    def pool_step(self, pool, g, s, last):
        pass

    def dve_step(self, dve, g, s, last):
        pass


class Splits(Hooks):

    PIECES = ((None, 1), (0, 1), (1, 1), (None, 0), (0, 0), (1, 0))
    ROUND_AT = {20: 0, 21: 1, 22: 2, 23: 3, 24: 4, 25: 5}
    SPLIT_AT = {21: 0, 22: 1, 23: 2, 25: 4, 26: 5}

    def setup(self, s, nc, att, v_all, dv):
        self.nc, self.att, self.v_all, self.dv = nc, att, v_all, dv
        self.rounded, self.split, self.part_split, self.k_split, self.v_round, self.v_split = (s.sem(n) for n in (
            "pieces_rounded", "pieces_split", "even_head_split", "first_keys_split", "v_rounded", "v_split"))

    def before_scores(self, pe, g, n):
        to, n = g + n // 32, n % 32
        if n == 0:
            pe.wait_ge(self.k_split, to + 1)
        if n in (0, 2, 4, 6):
            pe.wait_ge(self.split, 5 * to + 2 + n // 2)

    def before_values(self, pe, g, quad, b):
        if quad == 0 and b == self.att.blocks(0) - 1:
            pe.wait_ge(self.v_split, 2 * g + 1)
        if quad == 0 and b == 0:
            pe.wait_ge(self.v_split, 2 * g + 2)

    def split_order(self, i):
        return i + 1 if i < 3 else i

    def pool_split(self, pool, to, i, before):
        pool.wait_ge(self.rounded, 6 * to + i + 1)
        before()
        self.split_piece(pool, to, i).then_inc(self.split, 1)
        pool.wait_ge(self.split, 5 * to + self.split_order(i))

    def round_values(self, to, blocks):
        self.nc.gpsimd.tensor_copy(self.att.v[:, blocks, 0:self.dv],
                                   self.v_all[:, blocks, bass.ds(to * self.dv, self.dv)]).then_inc(self.v_round, 1)

    def split_values(self, dve, to, part, blocks):
        dve.wait_ge(self.v_round, 2 * to + part + 1)
        self.nc.vector.tensor_tensor(self.att.v[:, blocks, 64:64 + self.dv],
                                     self.v_all[:, blocks, bass.ds(to * self.dv, self.dv)],
                                     self.att.v[:, blocks, 0:self.dv].bitcast(F32),
                                     ALU.subtract).then_inc(self.v_split, 1)

    def split_first_keys(self, dve, to):
        dve.wait_ge(self.rounded, 6 * to + 4)
        self.split_piece(dve, to, 3).then_inc(self.k_split, 1)

    def act_start(self, act):
        self.whole_ready(act, 0)
        for i in range(6):
            self.round_piece(0, i).then_inc(self.rounded, 1)

    def pool_start(self, pool):
        self.round_values(0, slice(1, NT))
        self.round_values(0, slice(0, 1))
        for i in (0, 1, 2, 4, 5):
            self.pool_split(pool, 0, i, lambda: pool.wait_ge(self.v_round, 2))

    def dve_start(self, dve):
        self.split_values(dve, 0, 0, slice(1, NT))
        self.split_values(dve, 0, 1, slice(0, 1))
        self.split_first_keys(dve, 0)

    def act_step(self, act, g, s, last):
        if last or s not in self.ROUND_AT:
            return
        i = self.ROUND_AT[s]
        if i == 0:
            self.whole_ready(act, g + 1)
        act.wait_ge(self.att.scored, 32 * g + (28 if i < 3 else 32))
        self.round_piece(g + 1, i).then_inc(self.rounded, 1)

    def pool_step(self, pool, g, s, last):
        if last:
            return
        if s in self.SPLIT_AT:
            self.pool_split(pool, g + 1, self.SPLIT_AT[s], lambda: pool.wait_ge(self.att.scaled, 32 * g + s + 7))
        if s == 28:
            pool.wait_ge(self.att.valued, NT * g + 7)
            self.round_values(g + 1, slice(1, NT))
        if s == 31:
            pool.wait_ge(self.att.valued, NT * g + 8)
            self.round_values(g + 1, slice(0, 1))

    def dve_step(self, dve, g, s, last):
        if last:
            return
        if s == 23:
            self.split_first_keys(dve, g + 1)
        if s == 29:
            self.split_values(dve, g + 1, 0, slice(1, NT))
        if s == 31:
            self.split_values(dve, g + 1, 1, slice(0, 1))


class L2Hooks(Splits):

    PROJECT = (1, 2, 3, 5, 6, 7, 9, 10, 11, 13, 14, 15)
    OUTPUT = (4, 8, 12, 16, 20, 24, 28, 31)
    JOBS = sorted([(s, "project", j) for j, s in enumerate(PROJECT)] + [(s, "output", q) for q, s in enumerate(OUTPUT)])
    ADD_AT = dict(zip([s + 1 for s in PROJECT[1::2]], range(6)))

    def __init__(self, core, s):
        nc = core.nc
        self.core, self.hT, self.acc = core, core.xnT, core.acc
        self.rope = s.sb("rope", [P, 2, T])
        self.wp = s.sb("w_group", [P, KD * (2 * D + 2 * P)])
        self.wo = s.sb("w_o_group", [P, KD, D])
        self.oT = s.sb("oT", [P, KD, P])
        self.rot = s.sb("rotated", [P, 2, 2, HALF])
        self.whole = s.sb("qk_whole", [P, 6, HALF])
        self.share = s.ps("share", [P, HALF])
        self.wp_loaded, self.wo_loaded, self.share_ps, self.share_read, self.rotated, self.whole_done = (
            s.sem(n) for n in ("w_group_loaded", "w_o_loaded", "share_psum", "share_read", "rotated", "qk_whole_done"))

    def before_job(self, g, s, last):
        jobs = [j for j in self.JOBS if not last or j[1] == "output"]
        return 12 + 20 * g + sum(j[0] < s for j in jobs)

    def job(self, s, last):
        for at, kind, j in self.JOBS:
            if at == s and not (last and kind == "project"):
                return kind, j
        return None, None

    def project(self, j):
        u, r = j // 2, j % 2
        which, half = u // 2, u % 2
        at, step = (KD * 2 * D, P) if which == 0 else ((which - 1) * P, D)
        for k in range(KD):
            w = at + (r * KD + k) * step
            done = self.nc.tensor.matmul(self.share[:], self.wp[:, w:w + P], self.hT[:, k, half * HALF:(half + 1) * HALF],
                                         start=k == 0, stop=k == KD - 1)
        done.then_inc(self.share_ps, 1)

    def rotate(self, dve, to, j):
        u, r = j // 2, j % 2
        if j % 2 == 0 and (u >= 2 or not isinstance(to, int)):
            dve.wait_ge(self.whole_done, 6 * to + u - 1)
        table = self.rope[:, r, u % 2 * HALF:(u % 2 + 1) * HALF]
        if u < 2:
            done = self.nc.vector.tensor_tensor(self.rot[:, u % 2, r, :], self.share[:], table, ALU.mult)
        else:
            done = self.nc.vector.scalar_tensor_tensor(self.rot[:, u % 2, r, :], self.share[:], 0.125, table,
                                                       ALU.mult, ALU.mult)
        done.then_inc(self.share_read, 1)
        if r:
            dve.wait_ge(self.share_read, self.read)
            dve.sem_inc(self.rotated, 1)

    def add(self, pool, to, u):
        pool.wait_ge(self.rotated, 6 * to + u + 1)
        self.nc.gpsimd.tensor_tensor(self.whole[:, u, :], self.rot[:, u % 2, 0, :], self.rot[:, u % 2, 1, :],
                                     ALU.add).then_inc(self.whole_done, 1)

    def whole_ready(self, act, to):
        act.wait_ge(self.whole_done, 6 * to + 6)

    def round_piece(self, to, i):
        pair, half = self.PIECES[i]
        cols = slice(half * HALF, (half + 1) * HALF)
        if pair is None:
            return self.nc.scalar.activation(self.att.k[0][:, cols], self.whole[:, half, :], ACT.Copy)
        for m in range(2):
            rows = slice(64 * m, 64 * m + 64)
            done = self.nc.scalar.activation(self.att.q[rows, 2 * pair + m, cols],
                                             self.whole[rows, 2 + 2 * pair + half, :], ACT.Copy)
        return done

    def split_piece(self, engine, to, i):
        pair, half = self.PIECES[i]
        cols = slice(half * HALF, (half + 1) * HALF)
        if pair is None:
            e = self.nc.vector if i == 3 else self.nc.gpsimd
            return e.tensor_tensor(self.att.k[1][:, cols], self.whole[:, half, :], self.att.k[0][:, cols].bitcast(F32),
                                   ALU.subtract)
        for m in range(2):
            rows, other = slice(64 * m, 64 * m + 64), slice(64 - 64 * m, 128 - 64 * m)
            if m:
                engine.wait_ge(self.part_split, 4 * to + 2 * (1 - half) + pair + 1)
            done = self.nc.gpsimd.tensor_tensor(self.att.q[other, 2 * pair + m, cols],
                                                self.whole[rows, 2 + 2 * pair + half, :],
                                                self.att.q[rows, 2 * pair + m, cols].bitcast(F32), ALU.subtract)
            if m == 0:
                done.then_inc(self.part_split, 1)
        return done

    def keep(self, dve, g, tile, half, first, second):
        if half == 0:
            q = GroupAttention.ORDER.index(tile)
            dve.wait_ge(self.share_ps, self.before_job(g, self.OUTPUT[q - 1] + 1 if q else 0, self.last))
        return self.nc.vector.tensor_tensor(self.oT[64 * half:64 * half + 64, :, :], first, second, ALU.add)

    def pe_step(self, pe, g, s, last):
        kind, j = self.job(s, last)
        if kind is None or s < 0:
            return
        pe.wait_ge(self.share_read, self.before_job(g, s, last))
        if kind == "project":
            if j == 0:
                pe.wait_ge(self.wp_loaded, 16 * g + 32)
            self.project(j)
            return
        if j == 0:
            pe.wait_ge(self.wo_loaded, 16 * g + 16)
        pe.wait_ge(self.att.kept, NT * g + j + 2)
        for k in range(KD):
            done = self.nc.tensor.matmul(self.share[:, 0:D], self.oT[:, k, :], self.wo[:, k, :], start=k == 0,
                                         stop=k == KD - 1)
        done.then_inc(self.share_ps, 1)

    def pool_step(self, pool, g, s, last):
        if s in self.ADD_AT and not last:
            self.add(pool, g + 1, self.ADD_AT[s])
        super().pool_step(pool, g, s, last)

    def dve_step(self, dve, g, s, last):
        super().dve_step(dve, g, s, last)
        self.last = last
        kind, j = self.job(s, last)
        if kind is None or s < 0:
            return
        count = self.before_job(g, s, last) + 1
        dve.wait_ge(self.share_ps, count)
        if kind == "project":
            self.read = count
            self.rotate(dve, g + 1, j)
            return
        t = GroupAttention.ORDER[j]
        self.nc.vector.tensor_tensor(self.acc[:, t, :], self.share[:, 0:D], self.acc[:, t, :],
                                     ALU.add).then_inc(self.share_read, 1)


def l2_attention(core):
    nc, s = core.nc, Stage(core)
    x, xn, hT, acc, ident = core.x, core.xn, core.xnT, core.acc, core.ident
    G, DV = 8, 64
    att_mask = s.sb("causal_mask", [P, P])
    hooks = L2Hooks(core, s)
    att = GroupAttention(s, nc, ident, DV, att_mask, hooks)
    wv = s.sb("w_v", [P, KD, G * DV])
    v_all = s.sb("v_all", [P, NT, G * DV])
    hooks.setup(s, nc, att, v_all, DV)
    psS = att.psS
    mask_loaded, rope_loaded, wv_loaded, v_ps, v_sb, acc_set = (s.sem(n) for n in (
        "mask_loaded", "rope_loaded", "w_v_loaded", "v_psum", "v_sbuf", "acc_set"))

    with s.block() as block:
        @block.sync
        def _(sp):
            def load(to, tile, name, sem):
                sp.dma_start(tile[:], core.dram[name][to]).then_inc(sem, 16)

            sp.dma_start(wv[:], core.dram["l2_wv"]).then_inc(wv_loaded, 16)
            load(0, hooks.wp, "l2_wgroup", hooks.wp_loaded)
            sp.dma_start(hooks.rope[:], core.dram["l2_rope"]).then_inc(rope_loaded, 16)
            sp.dma_start(att_mask[:], core.dram["l2_mask"]).then_inc(mask_loaded, 16)
            load(0, hooks.wo, "l2_wo", hooks.wo_loaded)
            sp.wait_ge(hooks.share_ps, 12)
            load(1, hooks.wp, "l2_wgroup", hooks.wp_loaded)
            with sp.Fori(0, G - 2) as g:
                sp.wait_ge(hooks.share_ps, hooks.before_job(g, 16, False))
                load(g + 2, hooks.wp, "l2_wgroup", hooks.wp_loaded)
                sp.wait_ge(hooks.share_ps, 20 * g + 32)
                load(g + 1, hooks.wo, "l2_wo", hooks.wo_loaded)
            sp.wait_ge(hooks.share_ps, 20 * (G - 2) + 32)
            load(G - 1, hooks.wo, "l2_wo", hooks.wo_loaded)

        @block.gpsimd
        def _(pool):
            nc.gpsimd.tensor_copy(acc[:], xn[:]).then_inc(acc_set, 1)
            for u in range(6):
                hooks.add(pool, 0, u)
            pool.wait_ge(v_sb, NT)
            hooks.pool_start(pool)
            att.pool(pool, G)

        @block.tensor
        def _(pe):
            pe.wait_ge(wv_loaded, 16)
            for t in range(NT):
                if t >= 4:
                    pe.wait_ge(v_sb, t - 3)
                for k in range(KD):
                    last = nc.tensor.matmul(psS[:, t % 4 // 2, t % 2, :], hT[:, k, t * P:(t + 1) * P], wv[:, k, :],
                                            start=k == 0, stop=k == KD - 1)
                last.then_inc(v_ps, 1)
            pe.wait_ge(hooks.wp_loaded, 16)
            for j in range(12):
                if j:
                    pe.wait_ge(hooks.share_read, j)
                hooks.project(j)
            pe.wait_ge(v_sb, NT)
            pe.wait_ge(att.const16, 1)
            att.pe(pe, G)

        @block.scalar
        def _(act):
            for t in range(NT):
                act.wait_ge(v_ps, t + 1)
                nc.scalar.activation(v_all[:, t, :], psS[:, t % 4 // 2, t % 2, :], ACT.Copy).then_inc(v_sb, 1)
            hooks.act_start(act)
            att.act(act, G)

        @block.vector
        def _(dve):
            dve.wait_ge(mask_loaded, 16)
            att.constants(dve)
            dve.wait_ge(rope_loaded, 16)
            for j in range(12):
                dve.wait_ge(hooks.share_ps, j + 1)
                hooks.read = j + 1
                hooks.rotate(dve, 0, j)
            dve.wait_ge(acc_set, 1)
            hooks.dve_start(dve)
            att.dve(dve, G)
            dve.wait_ge(hooks.share_read, 20 * (G - 1) + 20)
            nc.vector.scalar_tensor_tensor(x[:].rearrange("p t d -> p (t d)"), acc[:].rearrange("p t d -> p (t d)"),
                                           0.5, x[:].rearrange("p t d -> p (t d)"), ALU.mult, ALU.add)
    s.close()


class L0Hooks(Splits):

    def __init__(self, core, s, rows):
        self.qs = s.sb("q_whole", [P, 4, T])
        self.ks = s.sb("k_whole", [P, T])
        self.oG = s.sb("o_group", [rows, 4, T])
        self.q_loaded = [s.sem(f"q_loaded{i}") for i in range(8)]
        self.k_loaded = [s.sem(f"k_loaded{i}") for i in range(2)]
        self.stored = s.sem("o_stored_plus_one")

    def whole_ready(self, act, to):
        for sem in self.k_loaded + self.q_loaded:
            act.wait_ge(sem, 16 * to + 16)

    def parts(self, i):
        pair, half = self.PIECES[i]
        cols = slice(half * HALF, (half + 1) * HALF)
        if pair is None:
            return self.att.k[0][:, cols], self.att.k[1][:, cols], self.ks[:, cols]
        heads = slice(2 * pair, 2 * pair + 2)
        return self.att.q[:, heads, cols], self.att.q[64:P, heads, cols], self.qs[:, heads, cols]

    def round_piece(self, to, i):
        first, _, whole = self.parts(i)
        return self.nc.scalar.activation(first, whole, ACT.Copy)

    def split_piece(self, engine, to, i):
        first, second, whole = self.parts(i)
        if self.PIECES[i][0] is not None:
            first, whole = first[64:P], whole[64:P]
        e = self.nc.vector if i == 3 else self.nc.gpsimd
        return e.tensor_tensor(second, whole, first.bitcast(F32), ALU.subtract)

    def keep(self, dve, g, tile, half, first, second):
        if half == 0 and tile == GroupAttention.ORDER[0]:
            dve.wait_ge(self.stored, 16 * g + 16)
        out = self.oG[:].rearrange("p (k h) t -> p k h t", h=2)[:, :, half, tile * P:(tile + 1) * P]
        return self.nc.vector.tensor_tensor(out, first, second, ALU.add)


def l0_attention(core):
    nc, s = core.nc, Stage(core)
    x, xnT, ident = core.x, core.xnT, core.ident
    G, NB, W, H = 4, 8, 4, 16
    HN = H * NB
    KV = G * NB
    att_mask = s.sb("causal_mask", [P, P])
    F = NB * W
    hooks = L0Hooks(core, s, NB)
    att = GroupAttention(s, nc, ident, NB, att_mask, hooks)
    qs, ks, oG, q_loaded, k_loaded, stored = (
        hooks.qs, hooks.ks, hooks.oG, hooks.q_loaded, hooks.k_loaded, hooks.stored)
    wq = s.sb("w_q", [P, KD, HN])
    wk = s.sb("w_k", [P, KD, KV])
    wv = s.sb("w_v", [P, KD, KV])
    wo = s.sb("w_o", [P, D])
    emb = s.sb("v_embeddings", [P, 2])
    tau = s.sb("tau", [P, 1])
    itau = s.sb("inverse_tau", [P, 1])
    qT = s.sb("q_tanh", [HN, T])
    kT = s.sb("k_tanh", [KV, T])
    pad = s.sb("pad", [P, W])
    irow = s.sb("inverse_position", [1, T])
    v_all = s.sb("v_all", [P, NT, KV])
    o_neg = s.sb("one_minus_o", [HN, T])
    oT = s.sb("oT", [HN, T])
    hooks.setup(s, nc, att, v_all, NB)
    psS = att.psS
    names = ("l0_wq", "l0_wk", "l0_wv", "l0_wo", "l0_emb", "l0_tau", "l0_mask", "l0_inverse")
    ld = {n: s.sem(n + "_loaded") for n in names[:-1]}
    ld["l0_inverse"] = stored
    j_loaded = [s.sem(f"key_positions_loaded{i}") for i in range(2)]
    i_loaded = [s.sem(f"query_rows_loaded{i}") for i in range(8)]
    itau_ready, irow_ready, pad_ready, v_zero = (s.sem(n) for n in (
        "itau_ready", "irow_ready", "pad_ready", "v_zeroed"))
    q_ps, q_tanh, q_scaled, k_ps, k_tanh, v_ps, v_sb = (s.sem(n) for n in (
        "q_psum", "q_tanh_done", "q_scaled", "k_psum", "k_tanh_done", "v_psum", "v_sbuf"))
    q_stored = [s.sem(f"q_step_stored{w}") for w in range(W)]
    k_stored = [s.sem(f"k_step_stored{w}") for w in range(W)]
    q_pad = [s.sem(f"q_pad_stored{w}") for w in range(W - 1)]
    k_pad = [s.sem(f"k_pad_stored{w}") for w in range(W - 1)]
    zeroed, oT_loaded, mixed, out_ps = (s.sem(n) for n in (
        "staging_zeroed", "oT_loaded", "mixed", "out_psum"))
    q_rows, k_rows = core.q_steps, core.k_steps

    with s.block() as block:
        @block.sync
        def _(sp):
            for sb, n in zip((wq, wk, wv, wo, emb, tau, att_mask, irow), names):
                sp.dma_start(sb[:], core.dram[n]).then_inc(ld[n], 16)
            sp.wait_ge(zeroed, 1)
            for i in range(2):
                sp.dma_start(ks[64 * i + F:64 * i + F + 1, :], core.dram["l0_positions"]).then_inc(j_loaded[i], 16)
            sp.wait_ge(pad_ready, 1)
            for w in range(W - 1):
                sp.dma_start(q_rows[w, :, 0:W - 1 - w], pad[:, 0:W - 1 - w],
                             allow_slow_non_contiguous=True).then_inc(q_pad[w], 16)
                sp.dma_start(k_rows[w, :, 0:W - 1 - w], pad[0:KV, 0:W - 1 - w],
                             allow_slow_non_contiguous=True).then_inc(k_pad[w], 16)
            sp.wait_ge(irow_ready, 1)
            for i in range(8):
                at = 64 * (i % 2) + F
                sp.dma_start(qs[at:at + 1, i // 2, :], irow[:]).then_inc(i_loaded[i], 16)
            sp.wait_ge(k_tanh, NH)
            for w in range(W):
                late = W - 1 - w
                sp.dma_start(k_rows[w, :, late:T], kT[:, 0:T - late]).then_inc(k_stored[w], 16)
            sp.wait_ge(q_scaled, 1)
            for w in range(W):
                late = W - 1 - w
                sp.dma_start(q_rows[w, :, late:T], qT[:, 0:T - late]).then_inc(q_stored[w], 16)
            for w in range(W):
                sp.wait_ge(q_stored[w], 16)
                sp.wait_ge(k_stored[w], 16)
            for w in range(W - 1):
                sp.wait_ge(q_pad[w], 16)
                sp.wait_ge(k_pad[w], 16)

            def load_queries(g):
                for i in range(8):
                    at = 64 * (i % 2)
                    sp.dma_start(qs[at:at + F, i // 2, :],
                                 q_rows[:, bass.ds((4 * g + i // 2) * NB, NB), :]).then_inc(q_loaded[i], 16)

            def load_keys(g):
                for i in range(2):
                    sp.dma_start(ks[64 * i:64 * i + F, :], k_rows[:, bass.ds(g * NB, NB), :]).then_inc(k_loaded[i], 16)

            def store(g):
                sp.wait_ge(att.kept, NT * g + NT + 1)
                sp.dma_start(core.o_rows[bass.ds(4 * g, 4)].rearrange("h p t -> p h t"), oG[:]).then_inc(stored, 16)
            load_keys(0)
            load_queries(0)
            with sp.Fori(0, G - 1) as g:
                sp.wait_ge(hooks.split, 5 * g + 5)
                load_queries(g + 1)
                sp.wait_ge(hooks.k_split, g + 1)
                load_keys(g + 1)
                store(g)
            store(G - 1)
            sp.wait_ge(stored, 16 * G + 16)
            sp.dma_start(oT[:], core.o_rows.rearrange("h p t -> (h p) t")).then_inc(oT_loaded, 16)

        @block.gpsimd
        def _(pool):
            nc.gpsimd.memset(pad[:], 0.0).then_inc(pad_ready, 1)
            nc.gpsimd.memset(qs[:], 0.0)
            nc.gpsimd.memset(ks[:], 0.0).then_inc(zeroed, 1)
            nc.gpsimd.memset(v_all[:], 0.0).then_inc(v_zero, 1)
            nc.gpsimd.memset(att.v[:].bitcast(F32), 0.0).then_inc(v_zero, 1)
            pool.wait_ge(v_zero, 2)
            pool.wait_ge(v_sb, NT)
            hooks.pool_start(pool)
            att.pool(pool, G)

        @block.tensor
        def _(pe):
            pe.wait_ge(ld["l0_wk"], 16)
            for half in range(NH):
                for k in range(KD):
                    last = nc.tensor.matmul(psS[0:KV, 0, half, :], wk[:, k, :],
                                            xnT[:, k, half * HALF:(half + 1) * HALF], start=k == 0, stop=k == KD - 1)
                last.then_inc(k_ps, 1)
            pe.wait_ge(ld["l0_wq"], 16)
            for half in range(NH):
                for k in range(KD):
                    last = nc.tensor.matmul(psS[:, 1, half, :], wq[:, k, :],
                                            xnT[:, k, half * HALF:(half + 1) * HALF], start=k == 0, stop=k == KD - 1)
                last.then_inc(q_ps, 1)
            pe.wait_ge(ld["l0_wv"], 16)
            for t in range(NT):
                rows = P if t < NT - 1 else P - 1
                for k in range(KD):
                    last = nc.tensor.matmul(att.psO[0:rows, t * KV:(t + 1) * KV],
                                            xnT[:, k, t * P + 1:t * P + 1 + rows], wv[:, k, :],
                                            start=k == 0, stop=k == KD - 1)
            last.then_inc(v_ps, 1)
            pe.wait_ge(v_sb, NT)
            pe.wait_ge(att.const16, 1)
            att.pe(pe, G)
            pe.wait_ge(mixed, 4)
            pe.wait_ge(ld["l0_wo"], 16)
            for b in range(4):
                for t in (2 * b, 2 * b + 1):
                    last = nc.tensor.matmul(psS[:, b // 2, b % 2, (t % 2) * D:(t % 2 + 1) * D],
                                            oT[:, t * P:(t + 1) * P], wo[:], start=True, stop=True)
                last.then_inc(out_ps, 1)

        @block.scalar
        def _(act):
            act.wait_ge(itau_ready, 1)
            for half in range(NH):
                act.wait_ge(k_ps, half + 1)
                nc.scalar.activation(kT[:, half * HALF:(half + 1) * HALF], psS[0:KV, 0, half, :], ACT.Tanh,
                                     scale=itau[0:KV, 0:1]).then_inc(k_tanh, 1)
            for half in range(NH):
                act.wait_ge(q_ps, half + 1)
                nc.scalar.activation(qT[:, half * HALF:(half + 1) * HALF], psS[:, 1, half, :], ACT.Tanh,
                                     scale=itau[:, 0:1]).then_inc(q_tanh, 1)
            act.wait_ge(v_ps, 1)
            act.wait_ge(v_zero, 1)
            for t in range(NT):
                rows = P if t < NT - 1 else P - 1
                nc.scalar.activation(v_all[0:rows, t, :], att.psO[0:rows, t * KV:(t + 1) * KV], ACT.Sigmoid,
                                     scale=itau[0:rows, 0:1]).then_inc(v_sb, 1)
            for i in range(8):
                act.wait_ge(i_loaded[i], 16)
            for i in range(2):
                act.wait_ge(j_loaded[i], 16)
            hooks.act_start(act)
            att.act(act, G)

        @block.vector
        def _(dve):
            dve.wait_ge(ld["l0_tau"], 16)
            nc.vector.reciprocal(itau[:], tau[:]).then_inc(itau_ready, 1)
            dve.wait_ge(ld["l0_inverse"], 16)
            dve.wait_ge(itau_ready, 1)
            nc.vector.tensor_scalar(irow[:], irow[:], itau[0:1, 0:1], None, ALU.mult).then_inc(irow_ready, 1)
            dve.wait_ge(q_tanh, NH)
            nc.vector.tensor_scalar(qT[:], qT[:], itau[:, 0:1], float((NB * W) ** -0.5), ALU.mult,
                                    ALU.mult).then_inc(q_scaled, 1)
            dve.wait_ge(ld["l0_mask"], 16)
            att.constants(dve)
            hooks.dve_start(dve)
            att.dve(dve, G)
            dve.wait_ge(oT_loaded, 16)
            dve.wait_ge(ld["l0_emb"], 16)
            nc.vector.memset(oT[:, 0:1], 0.0).then_inc(mixed, 1)
            dve.wait_ge(mixed, 1)
            nc.vector.tensor_scalar(o_neg[:], oT[:], -1.0, 1.0, ALU.mult, ALU.add).then_inc(mixed, 1)
            dve.wait_ge(mixed, 2)
            nc.vector.tensor_scalar(o_neg[:], o_neg[:], emb[:, 0:1], None, ALU.mult).then_inc(mixed, 1)
            dve.wait_ge(mixed, 3)
            nc.vector.scalar_tensor_tensor(oT[:], oT[:], emb[:, 1:2], o_neg[:], ALU.mult,
                                           ALU.add).then_inc(mixed, 1)
            xb = x[:, :, :].rearrange("p (b t) d -> p b (t d)", b=4)
            for b in range(4):
                dve.wait_ge(out_ps, b + 1)
                nc.vector.tensor_tensor(xb[:, b, :], psS[:, b // 2, b % 2, :], xb[:, b, :], ALU.add)
    s.close()


class Delta:

    H, DK, DV = 6, 32, 64
    QK = 2 * H * DK
    V = H * DV
    CH = QK + V
    CT = CH // P

    def __init__(self, core):
        self.memory = s = Stage(core)
        H = self.H
        self.nat = s.sb("qkv", [P, NT, self.CH])
        self.beta = s.sb("beta", [P, NT, H])
        self.g = s.sb("log_decay", [P, NT, H])
        self.eg = s.sb("decay_from_start", [P, NT, H])
        self.ek = s.sb("decay_to_end", [P, NT, H])
        self.ec = s.sb("decay_of_chunk", [P, NT, H])
        self.tri = s.sb("triangles", [P, 3, P])
        self.o = s.sb("o", [P, NT, self.V])


def l2_delta_inputs(core, d):
    nc, s = core.nc, Stage(core)
    xnT, ident = core.xnT, core.ident
    H, DK, CT = d.H, d.DK, d.CT
    K = 4
    w = s.sb("w_qkv", [P, KD, d.CH])
    wc = s.sb("w_conv", [P, CT, K])
    wba = s.sb("w_beta_decay", [P, KD, 2 * H])
    bias = s.sb("dt_bias", [P, H])
    alog = s.sb("a_log", [P, H])
    na = s.sb("neg_a", [P, H])
    raw = s.sb("raw", [P, 2, K - 1 + T])
    cv = s.sb("conv", [P, 2, T])
    act_out = s.sb("conv_silu", [P, 2, T])
    z = s.sb("z", [P, NT, H])
    za = s.sb("z_abs", [P, NT, H])
    zl = s.sb("z_log", [P, NT, H])
    sq = s.sb("squares", [P, NT, d.QK])
    ss = s.sb("norms", [P, NT, 2 * H])
    eps = s.sb("eps", [P, 1])
    ones = s.sb("ones", [P, P])
    ps = s.ps("ps", [P, 4, HALF])
    psT = s.ps("psT", [P, 2, HALF])
    psG = s.ps("psG", [P, NT, 4 * H])
    psC = s.ps("psC", [P, 3, NT * H])
    names = ("l2_wqkv", "l2_wconv", "l2_wba", "l2_dt_bias", "l2_alog", "l2_tri")
    ld = {n: s.sem(n + "_loaded") for n in names}
    pad_set, const_set, proj, raw_done, conv_step, conv_done, silu_done, turned, nat_done = (s.sem(n) for n in (
        "pad_set", "const_set", "projected", "raw_done", "conv_step", "conv_done", "silu_done", "transposed",
        "qkv_done"))
    ba_ps, beta_done, z_done, zabs_done, zexp_done, zln_done, a_exp, g_step, g_done = (s.sem(n) for n in (
        "ba_psum", "beta_done", "z_done", "z_abs_done", "z_exp_done", "z_ln_done", "a_exp_done", "g_step",
        "g_done"))
    cum_ps, ss_done, sqrt_done, norm_step = (s.sem(n) for n in (
        "cumulated", "squares_summed", "sqrt_done", "norm_step"))
    with s.block() as block:
        @block.sync
        def _(sp):
            for sb, n in zip((w, wc, wba, bias, alog, d.tri), names):
                sp.dma_start(sb[:], core.dram[n]).then_inc(ld[n], 16)

        @block.gpsimd
        def _(pool):
            nc.gpsimd.memset(raw[:, 0, 0:K - 1], 0.0)
            nc.gpsimd.memset(raw[:, 1, 0:K - 1], 0.0).then_inc(pad_set, 1)
            nc.gpsimd.memset(eps[:], 1e-6)
            nc.gpsimd.memset(ones[:], 1.0).then_inc(const_set, 1)

        @block.tensor
        def _(pe):
            pe.wait_ge(ld["l2_wqkv"], 16)

            def project(c):
                for half in range(NH):
                    if c >= 2:
                        pe.wait_ge(raw_done, 2 * c + half - 3)
                    for k in range(KD):
                        last = nc.tensor.matmul(ps[:, c % 2 * 2 + half, :], w[:, k, c * P:(c + 1) * P],
                                                xnT[:, k, half * HALF:(half + 1) * HALF],
                                                start=k == 0, stop=k == KD - 1)
                    last.then_inc(proj, 1)

            def turn(c):
                pe.wait_ge(silu_done, c + 1)
                for half in range(NH):
                    if c >= 1:
                        pe.wait_ge(nat_done, 2 * c + half - 1)
                    for q in range(4):
                        t = half * 4 + q
                        last = nc.tensor.transpose(psT[:, half, q * P:(q + 1) * P],
                                                   act_out[:, c % 2, t * P:(t + 1) * P], ident[:])
                    last.then_inc(turned, 1)

            project(0)
            pe.wait_ge(ld["l2_wba"], 16)
            for t in range(NT):
                for k in range(KD):
                    last = nc.tensor.matmul(psG[:, t, 0:2 * H], xnT[:, k, t * P:(t + 1) * P], wba[:, k, :],
                                            start=k == 0, stop=k == KD - 1)
            last.then_inc(ba_ps, 1)
            project(1)
            for c in range(CT):
                if c + 2 < CT:
                    project(c + 2)
                turn(c)
            pe.wait_ge(g_done, 1)
            pe.wait_ge(ld["l2_tri"], 16)
            pe.wait_ge(const_set, 1)
            gf = d.g[:].rearrange("p t h -> p (t h)")
            for m, lhsT in enumerate((d.tri[:, 0, :], d.tri[:, 1, :], ones[:])):
                last = nc.tensor.matmul(psC[:, m, :], lhsT, gf, start=True, stop=True)
            last.then_inc(cum_ps, 1)

        @block.scalar
        def _(act):
            def evacuate(c):
                if c >= 2:
                    act.wait_ge(conv_done, c - 1)
                for half in range(NH):
                    act.wait_ge(proj, 2 * c + half + 1)
                    nc.scalar.activation(raw[:, c % 2, K - 1 + half * HALF:K - 1 + (half + 1) * HALF],
                                         ps[:, c % 2 * 2 + half, :], ACT.Copy).then_inc(raw_done, 1)

            act.wait_ge(ba_ps, 1)
            nc.scalar.activation(d.beta[:], psG[:, :, 0:H], ACT.Sigmoid).then_inc(beta_done, 1)
            evacuate(0)
            for c in range(CT):
                if c + 1 < CT:
                    evacuate(c + 1)
                act.wait_ge(conv_done, c + 1)
                if c >= 2:
                    act.wait_ge(turned, 2 * c - 2)
                nc.scalar.activation(act_out[:, c % 2, :], cv[:, c % 2, :], ACT.Silu).then_inc(silu_done, 1)
            act.wait_ge(z_done, 1)
            nc.scalar.activation(za[:], z[:], ACT.Abs).then_inc(zabs_done, 1)
            act.wait_ge(zabs_done, 1)
            nc.scalar.activation(zl[:], za[:], ACT.Exp, scale=-1.0).then_inc(zexp_done, 1)
            act.wait_ge(zexp_done, 1)
            nc.scalar.activation(za[:], zl[:], ACT.Ln, bias=1.0).then_inc(zln_done, 1)
            act.wait_ge(ld["l2_alog"], 16)
            nc.scalar.activation(na[:], alog[:], ACT.Exp).then_inc(a_exp, 1)
            act.wait_ge(cum_ps, 1)
            for m, out in enumerate((d.eg, d.ek, d.ec)):
                nc.scalar.activation(out[:].rearrange("p t h -> p (t h)"), psC[:, m, :], ACT.Exp)
            act.wait_ge(ss_done, 1)
            act.wait_ge(const_set, 1)
            nc.scalar.activation(ss[:], ss[:], ACT.Sqrt, bias=eps[:, 0:1]).then_inc(sqrt_done, 1)

        @block.vector
        def _(dve):
            link = chain(dve, conv_step)
            dve.wait_ge(ld["l2_wconv"], 16)
            dve.wait_ge(pad_set, 1)

            def convolve(c):
                dve.wait_ge(raw_done, 2 * c + 2)
                if c >= 2:
                    dve.wait_ge(silu_done, c - 1)
                out, b = cv[:, c % 2, :], c % 2
                link(nc.vector.tensor_scalar(out, raw[:, b, K - 1:K - 1 + T], wc[:, c, K - 1:K], None, ALU.mult))
                for k in range(K - 1):
                    last = nc.vector.scalar_tensor_tensor(out, raw[:, b, k:k + T], wc[:, c, k:k + 1], out,
                                                          ALU.mult, ALU.add)
                    if k < K - 2:
                        link(last)
                last.then_inc(conv_done, 1)

            def keep(c):
                for half in range(NH):
                    dve.wait_ge(turned, 2 * c + half + 1)
                    nc.vector.tensor_copy(d.nat[:, half * 4:half * 4 + 4, c * P:(c + 1) * P],
                                          psT[:, half, :].rearrange("p (t w) -> p t w", t=4)).then_inc(nat_done, 1)

            dve.wait_ge(ba_ps, 1)
            dve.wait_ge(beta_done, 1)
            dve.wait_ge(ld["l2_dt_bias"], 16)
            nc.vector.tensor_tensor(z[:], psG[:, :, H:2 * H], bias[:].unsqueeze(1).to_broadcast([P, NT, H]),
                                    ALU.add).then_inc(z_done, 1)
            convolve(0)
            for c in range(CT):
                if c + 1 < CT:
                    convolve(c + 1)
                keep(c)
            step = chain(dve, g_step)
            dve.wait_ge(zln_done, 1)
            dve.wait_ge(z_done, 1)
            step(nc.vector.tensor_scalar(z[:], z[:], 0.0, None, ALU.max))
            step(nc.vector.tensor_tensor(za[:], za[:], z[:], ALU.add))
            dve.wait_ge(a_exp, 1)
            step(nc.vector.tensor_scalar(na[:], na[:], -1.0, None, ALU.mult))
            nc.vector.tensor_tensor(d.g[:], za[:], na[:].unsqueeze(1).to_broadcast([P, NT, H]),
                                    ALU.mult).then_inc(g_done, 1)
            norm = chain(dve, norm_step)
            dve.wait_ge(nat_done, 2 * CT)
            qk = d.nat[:, :, 0:d.QK]
            norm(nc.vector.tensor_tensor(sq[:], qk, qk, ALU.mult))
            nc.vector.tensor_reduce(ss[:], sq[:].rearrange("p t (h k) -> p t h k", k=DK), AX.X,
                                    ALU.add).then_inc(ss_done, 1)
            dve.wait_ge(sqrt_done, 1)
            norm(nc.vector.reciprocal(ss[:], ss[:]))
            norm(nc.vector.tensor_scalar(ss[:, :, 0:H], ss[:, :, 0:H], float(DK) ** -0.5, None, ALU.mult))
            qk4 = qk.rearrange("p t (h k) -> p t h k", k=DK)
            nc.vector.tensor_tensor(qk4, qk4, ss[:].unsqueeze(3).to_broadcast([P, NT, 2 * H, DK]), ALU.mult)
    s.close()


def l2_delta_chunks(core, d):
    nc, s = core.nc, Stage(core)
    ident = core.ident
    H, DK, DV, QK = d.H, d.DK, d.DV, d.QK
    HK = H * DK
    LEVELS = 6
    B = 3
    masks = s.sb("level_masks", [P, LEVELS + 1, P])
    sg = s.sb("staged", [P, 2, 4, HK])
    kd = s.sb("k_to_end", [P, 2, HK])
    st = s.sb("staged_T", [DK, H, 8, P])
    lg = s.sb("summed_g", [P, B, 4, P])
    bm = s.sb("beta_mask", [P, B, 4, P])
    ed = s.sb("decays", [P, B, 2, HALF])
    em = s.sb("decays_masked", [P, B, 2, HALF])
    L = s.sb("L", [P, B, 4, P])
    AT = s.sb("AT", [P, B, 4, P])
    t0 = s.sb("joined0", [P, B, 4, P])
    X = s.sb("X", [P, B, 4, P])
    Y = s.sb("Y", [P, B, 4, P])
    ml = s.sb("L_level", [P, B, 4, P])
    bs = s.sb("B_level", [P, B, 4, P])
    S = s.sb("state", [DK, H, DV])
    Sd = s.sb("state_decayed", [DK, H, DV])
    vd = s.sb("v_less", [P, H, DV])
    R = s.sb("R", [P, H, DV])
    U = s.sb("u", [P, H, DV])
    ps = s.ps("ps", [P, 8, HALF])
    flat = lambda ap: ap.rearrange("p s n -> p (s n)")
    four = lambda ap: ap.unsqueeze(1).to_broadcast([P, 4, P])
    (masks_loaded, staged, copied, bmask, summed, turned, st_done, d_ps, d_exp, masked, kq_ps, la_done, t0_done,
     x0_done, y0_ps, y0_done, ml_done, b_ps, b_sb, yx_ps, yx_done, p1_ps, vd_done, r_done, u_ps, u_sb, o_ps, o_sb,
     sd_ps, s_done, sd_done) = (s.sem(n) for n in (
         "masks_loaded", "staged", "qk_copied", "beta_mask_done", "g_summed", "staged_turned", "staged_T_done",
         "decay_logs", "decays_done", "decays_masked", "kk_qk_psum", "l_a_done", "joined0_done", "x0_done",
         "y0_psum", "y0_done", "l_level_done", "b_psum", "b_sbuf", "yx_psum", "yx_done", "p1_psum", "v_less_done",
         "r_done", "u_psum", "u_sbuf", "o_psum", "o_sbuf", "s_psum", "s_done", "s_decayed"))

    def systems(b):
        return [(b, h) for h in range(4)] if b < 2 else [(e, h) for e in range(2) for h in (4, 5)]

    def place(e, h):
        return (e, h) if h < 4 else (2, 2 * e + h - 4)

    def kqT(e, which, h):
        return st[:, h, e * 4 + which, :]

    with s.block() as block:
        @block.sync
        def _(sp):
            sp.dma_start(masks[:], core.dram["l2_levels"]).then_inc(masks_loaded, 16)

        @block.gpsimd
        def _(pool):
            pool.wait_ge(masks_loaded, 16)
            with pool.Fori(0, NT // 2) as i:
                two = bass.ds(2 * i, 2)
                nc.gpsimd.tensor_copy(sg[:, :, 2:4, :].rearrange("p e a n -> p e (a n)"),
                                      d.nat[:, two, 0:QK]).then_inc(copied, 1)
                for b in range(B):
                    if b < 2:
                        beta = d.beta[:, bass.ds(2 * i + b, 1), 0:4].rearrange("p a h -> p (a h)").unsqueeze(2)
                        nc.gpsimd.tensor_tensor(bm[:, b, :, :], four(d.tri[:, 2, :]), beta.to_broadcast([P, 4, P]),
                                                ALU.mult).then_inc(bmask, 1)
                    else:
                        for e in range(2):
                            beta = d.beta[:, bass.ds(2 * i + e, 1), 4:6].rearrange("p a h -> p (a h)").unsqueeze(2)
                            nc.gpsimd.tensor_tensor(bm[:, b, 2 * e:2 * e + 2, :],
                                                    d.tri[:, 2, :].unsqueeze(1).to_broadcast([P, 2, P]),
                                                    beta.to_broadcast([P, 2, P]), ALU.mult).then_inc(bmask, 1)
                pool.wait_ge(bmask, 4 * i + 4)
                for b in range(B):
                    pool.wait_ge(d_exp, B * i + b + 1)
                    nc.gpsimd.tensor_tensor(em[:, b, 0, :], ed[:, b, 0, :], flat(bm[:, b, :, :]), ALU.mult)
                    nc.gpsimd.tensor_tensor(em[:, b, 1, :].rearrange("p (s n) -> p s n", s=4),
                                            ed[:, b, 1, :].rearrange("p (s n) -> p s n", s=4),
                                            four(d.tri[:, 0, :]), ALU.mult).then_inc(masked, 1)
                for k in range(LEVELS):
                    for b in range(B):
                        if k == 0:
                            pool.wait_ge(la_done, B * i + b + 1)
                        else:
                            pool.wait_ge(b_ps, B * LEVELS * i + B * (k - 1) + b + 1)
                        nc.gpsimd.tensor_tensor(ml[:, b, :, :], L[:, b, :, :], four(masks[:, k + 1, :]),
                                                ALU.mult).then_inc(ml_done, 1)

        @block.tensor
        def _(pe):
            with pe.Fori(0, NT // 2) as i:
                pe.wait_ge(staged, i + 1)
                pe.wait_ge(copied, i + 1)
                for h in range(H):
                    if h >= 2:
                        pe.wait_ge(st_done, H * i + h - 1)
                    for e in range(2):
                        for a in range(4):
                            last = nc.tensor.transpose(ps[0:DK, 2 * (h % 2) + e, a * P:(a + 1) * P],
                                                       sg[:, e, a, h * DK:(h + 1) * DK], ident[:])
                    last.then_inc(turned, 1)
                pe.wait_ge(summed, i + 1)
                for b in range(B):
                    if b < 2:
                        pe.wait_ge(st_done, H * i + H - 1 + b)
                    else:
                        pe.wait_ge(s_done, 2 * i + 1)
                    for j in range(4):
                        nc.tensor.matmul(ps[:, 2 * b, j * P:(j + 1) * P], lg[:, b, j, :], d.tri[:, 1, :],
                                         start=True, stop=True)
                    nc.tensor.matmul(ps[:, 2 * b + 1, :], d.tri[:, 1, :], flat(lg[:, b, :, :]), start=True,
                                     stop=True).then_inc(d_ps, 1)
                pe.wait_ge(st_done, H * i + H)
                for b in range(B):
                    pe.wait_ge(d_exp, B * i + b + 1)
                    for j, (e, h) in enumerate(systems(b)):
                        to = slice(j * P, (j + 1) * P)
                        nc.tensor.matmul(ps[:, 2 * b, to], kqT(e, 3, h), kqT(e, 3, h), start=True, stop=True)
                        last = nc.tensor.matmul(ps[:, 2 * b + 1, to], kqT(e, 3, h), kqT(e, 2, h), start=True,
                                                stop=True)
                    last.then_inc(kq_ps, 1)
                for b in range(B):
                    pe.wait_ge(x0_done, B * i + b + 1)
                    for j in range(4):
                        last = nc.tensor.transpose(ps[:, 2 * b, j * P:(j + 1) * P], X[:, b, j, :], ident[:])
                    last.then_inc(y0_ps, 1)
                for k in range(LEVELS):
                    for b in range(B):
                        pe.wait_ge(ml_done, B * LEVELS * i + B * k + b + 1)
                        if k == 0:
                            pe.wait_ge(y0_done, B * i + b + 1)
                        else:
                            pe.wait_ge(yx_done, B * LEVELS * i + B * (k - 1) + b + 1)
                        for j in range(4):
                            last = nc.tensor.matmul(ps[:, 2 * b, j * P:(j + 1) * P], ml[:, b, j, :], Y[:, b, j, :],
                                                    start=True, stop=True)
                        last.then_inc(b_ps, 1)
                    for b in range(B):
                        pe.wait_ge(b_sb, B * LEVELS * i + B * k + b + 1)
                        for j in range(4):
                            to = slice(j * P, (j + 1) * P)
                            last = nc.tensor.matmul(ps[:, 2 * b, to], X[:, b, j, :], bs[:, b, j, :], start=True,
                                                    stop=True)
                            if k < LEVELS - 1:
                                last = nc.tensor.matmul(ps[:, 2 * b + 1, to], bs[:, b, j, :], X[:, b, j, :],
                                                        start=True, stop=True)
                        last.then_inc(yx_ps, 1)
                for e in range(2):
                    pe.wait_ge(s_done, 2 * i + e + 1)
                    for h in range(H):
                        last = nc.tensor.matmul(ps[:, 6, h * DV:(h + 1) * DV], kqT(e, 1, h),
                                                S[:, h, :], start=True, stop=True)
                    last.then_inc(p1_ps, 1)
                    pe.wait_ge(r_done, 2 * i + e + 1)
                    if e == 0:
                        pe.wait_ge(yx_done, B * LEVELS * i + B * LEVELS)
                    for h in range(H):
                        b, j = place(e, h)
                        last = nc.tensor.matmul(ps[:, 7, h * DV:(h + 1) * DV], Y[:, b, j, :], R[:, h, :],
                                                start=True, stop=True)
                    last.then_inc(u_ps, 1)
                    pe.wait_ge(u_sb, 2 * i + e + 1)
                    if e == 1:
                        pe.wait_ge(o_sb, 2 * i + 1)
                    for h in range(H):
                        b, j = place(e, h)
                        to = slice(h * DV, (h + 1) * DV)
                        nc.tensor.matmul(ps[:, 4, to], kqT(e, 0, h), S[:, h, :],
                                         start=True, stop=False)
                        last = nc.tensor.matmul(ps[:, 4, to], AT[:, b, j, :], U[:, h, :], start=False, stop=True)
                    last.then_inc(o_ps, 1)
                    for h in range(H):
                        last = nc.tensor.matmul(ps[0:DK, 5, h * DV:(h + 1) * DV],
                                                kd[:, e, h * DK:(h + 1) * DK], U[:, h, :], start=True, stop=True)
                    last.then_inc(sd_ps, 1)

        @block.scalar
        def _(act):
            with act.Fori(0, NT // 2) as i:
                for h in range(H):
                    act.wait_ge(turned, H * i + h + 1)
                    nc.scalar.activation(st[:, h, :, :].rearrange("p a n -> p (a n)"),
                                         ps[0:DK, 2 * (h % 2):2 * (h % 2) + 2, :].rearrange("p b n -> p (b n)"),
                                         ACT.Copy).then_inc(st_done, 1)
                for b in range(B):
                    act.wait_ge(d_ps, B * i + b + 1)
                    nc.scalar.activation(ed[:, b, :, :], ps[:, 2 * b:2 * b + 2, :], ACT.Exp).then_inc(d_exp, 1)
                for b in range(B):
                    act.wait_ge(y0_ps, B * i + b + 1)
                    nc.scalar.activation(flat(Y[:, b, :, :]), ps[:, 2 * b, :], ACT.Copy).then_inc(y0_done, 1)
                for k in range(LEVELS):
                    for b in range(B):
                        act.wait_ge(b_ps, B * LEVELS * i + B * k + b + 1)
                        nc.scalar.activation(flat(bs[:, b, :, :]), ps[:, 2 * b, :], ACT.Copy).then_inc(b_sb, 1)
                for e in range(2):
                    act.wait_ge(u_ps, 2 * i + e + 1)
                    nc.scalar.activation(U[:].rearrange("p h n -> p (h n)"), ps[:, 7, 0:H * DV],
                                         ACT.Copy).then_inc(u_sb, 1)
                    act.wait_ge(o_ps, 2 * i + e + 1)
                    nc.scalar.activation(d.o[:, bass.ds(2 * i + e, 1), :].rearrange("p a n -> p (a n)"),
                                         ps[:, 4, 0:H * DV], ACT.Copy).then_inc(o_sb, 1)

        @block.vector
        def _(dve):
            nc.vector.memset(S[:], 0.0).then_inc(s_done, 1)
            dve.wait_ge(masks_loaded, 16)
            with dve.Fori(0, NT // 2) as i:
                def heads(ap, e, lo, hi):
                    return ap[:, bass.ds(2 * i + e, 1), lo:hi].rearrange("p a h -> p (a h)")

                for e in range(2):
                    q3, k3 = (heads(d.nat, e, lo, lo + HK).rearrange("p (h n) -> p h n", n=DK) for lo in (0, HK))
                    g3, k_end = (heads(ap, e, 0, H).unsqueeze(2).to_broadcast([P, H, DK]) for ap in (d.eg, d.ek))
                    for out, a, decay in ((sg[:, e, 0, :], q3, g3), (sg[:, e, 1, :], k3, g3), (kd[:, e, :], k3, k_end)):
                        last = nc.vector.tensor_tensor(out.rearrange("p (h n) -> p h n", n=DK), a, decay, ALU.mult)
                last.then_inc(staged, 1)
                for b in range(B):
                    if b < 2:
                        last = nc.vector.tensor_tensor(lg[:, b, :, :], four(d.tri[:, 0, :]),
                                                       heads(d.g, b, 0, 4).unsqueeze(2).to_broadcast([P, 4, P]),
                                                       ALU.mult)
                    else:
                        for e in range(2):
                            last = nc.vector.tensor_tensor(
                                lg[:, b, 2 * e:2 * e + 2, :], d.tri[:, 0, :].unsqueeze(1).to_broadcast([P, 2, P]),
                                heads(d.g, e, 4, 6).unsqueeze(2).to_broadcast([P, 2, P]), ALU.mult)
                last.then_inc(summed, 1)
                for b in range(B):
                    dve.wait_ge(masked, B * i + b + 1)
                    dve.wait_ge(kq_ps, B * i + b + 1)
                    nc.vector.tensor_tensor(flat(L[:, b, :, :]), ps[:, 2 * b, :], em[:, b, 0, :], ALU.mult)
                    nc.vector.tensor_tensor(flat(AT[:, b, :, :]), ps[:, 2 * b + 1, :], em[:, b, 1, :],
                                            ALU.mult).then_inc(la_done, 1)
                    dve.wait_ge(la_done, B * i + b + 1)
                    nc.vector.tensor_tensor(t0[:, b, :, :], L[:, b, :, :], four(masks[:, 0, :]),
                                            ALU.mult).then_inc(t0_done, 1)
                    dve.wait_ge(t0_done, B * i + b + 1)
                    nc.vector.tensor_tensor(X[:, b, :, :], four(ident[:]), t0[:, b, :, :],
                                            ALU.subtract).then_inc(x0_done, 1)
                for k in range(LEVELS):
                    for b in range(B):
                        dve.wait_ge(yx_ps, B * LEVELS * i + B * k + b + 1)
                        last = nc.vector.tensor_tensor(flat(Y[:, b, :, :]), flat(Y[:, b, :, :]), ps[:, 2 * b, :],
                                                       ALU.subtract)
                        if k < LEVELS - 1:
                            last = nc.vector.tensor_tensor(flat(X[:, b, :, :]), flat(X[:, b, :, :]),
                                                           ps[:, 2 * b + 1, :], ALU.subtract)
                        last.then_inc(yx_done, 1)
                for e in range(2):
                    dve.wait_ge(s_done, 2 * i + e + 1)
                    nc.vector.tensor_tensor(
                        Sd[:], S[:],
                        d.ec[0:DK, bass.ds(2 * i + e, 1), :].rearrange("p a h -> p (a h)").unsqueeze(2)
                        .to_broadcast([DK, H, DV]), ALU.mult).then_inc(sd_done, 1)
                    dve.wait_ge(p1_ps, 2 * i + e + 1)
                    nc.vector.tensor_tensor(vd[:].rearrange("p h n -> p (h n)"), heads(d.nat, e, QK, QK + H * DV),
                                            ps[:, 6, 0:H * DV], ALU.subtract).then_inc(vd_done, 1)
                    dve.wait_ge(vd_done, 2 * i + e + 1)
                    nc.vector.tensor_tensor(R[:], vd[:], heads(d.beta, e, 0, H).unsqueeze(2).to_broadcast([P, H, DV]),
                                            ALU.mult).then_inc(r_done, 1)
                    dve.wait_ge(sd_done, 2 * i + e + 1)
                    dve.wait_ge(sd_ps, 2 * i + e + 1)
                    if e == 1:
                        dve.wait_ge(o_sb, 2 * i + 2)
                    nc.vector.tensor_tensor(S[:].rearrange("p h n -> p (h n)"),
                                            Sd[:].rearrange("p h n -> p (h n)"), ps[0:DK, 5, 0:H * DV],
                                            ALU.add).then_inc(s_done, 1)
    s.close()


def l2_delta_output(core, d):
    nc, s = core.nc, Stage(core)
    x, xnT, ident = core.x, core.xnT, core.ident
    H, DV, V = d.H, d.DV, d.V
    VT = V // P
    wg = s.sb("w_gate", [P, KD, V])
    wo = s.sb("w_out", [P, VT, D])
    nw = s.sb("norm_w", [P, V])
    gate = s.sb("gate", [P, NT, V])
    sq = s.sb("squares", [P, NT, V])
    ms = s.sb("mean_square", [P, NT, H])
    oT = s.sb("oT", [P, VT, T])
    ps = s.ps("ps", [P, 4, HALF])
    psT = s.ps("psT", [P, 4, HALF])
    ld = {n: s.sem(n + "_loaded") for n in ("l2_wg", "l2_norm_w", "l2_dwo")}
    gate_ps, gate_sb, step, ms_done, sqrt_done, gated, turned, oT_sb, out_ps = (s.sem(n) for n in (
        "gate_psum", "gate_sbuf", "dve_step", "ms_done", "sqrt_done", "gated", "transposed", "oT_sbuf", "out_psum"))
    with s.block() as block:
        @block.sync
        def _(sp):
            for sb, n in zip((wg, nw, wo), ld):
                sp.dma_start(sb[:], core.dram[n]).then_inc(ld[n], 16)

        @block.tensor
        def _(pe):
            pe.wait_ge(ld["l2_wg"], 16)
            for t in range(NT):
                if t >= 4:
                    pe.wait_ge(gate_sb, t - 3)
                for k in range(KD):
                    last = nc.tensor.matmul(ps[:, t % 4, 0:V], xnT[:, k, t * P:(t + 1) * P], wg[:, k, :],
                                            start=k == 0, stop=k == KD - 1)
                last.then_inc(gate_ps, 1)
            for c in range(VT):
                for half in range(NH):
                    n = 2 * c + half
                    if n >= 4:
                        pe.wait_ge(oT_sb, n - 3)
                    for q in range(4):
                        t = half * 4 + q
                        if c == 0:
                            pe.wait_ge(gated, t + 1)
                        last = nc.tensor.transpose(psT[:, n % 4, q * P:(q + 1) * P], d.o[:, t, c * P:(c + 1) * P],
                                                   ident[:])
                    last.then_inc(turned, 1)
            pe.wait_ge(oT_sb, 2 * VT)
            pe.wait_ge(ld["l2_dwo"], 16)
            for b in range(4):
                for t in (2 * b, 2 * b + 1):
                    for c in range(VT):
                        last = nc.tensor.matmul(ps[:, b, (t % 2) * D:(t % 2 + 1) * D], oT[:, c, t * P:(t + 1) * P],
                                                wo[:, c, :], start=c == 0, stop=c == VT - 1)
                last.then_inc(out_ps, 1)

        @block.scalar
        def _(act):
            for t in range(NT):
                act.wait_ge(gate_ps, t + 1)
                nc.scalar.activation(gate[:, t, :], ps[:, t % 4, 0:V], ACT.Silu).then_inc(gate_sb, 1)
            act.wait_ge(ms_done, 1)
            nc.scalar.activation(ms[:], ms[:], ACT.Sqrt, bias=core.eps[:, 0:1], scale=1.0 / DV).then_inc(sqrt_done, 1)
            for n in range(2 * VT):
                act.wait_ge(turned, n + 1)
                nc.scalar.activation(oT[:, n // 2, n % 2 * HALF:(n % 2 + 1) * HALF], psT[:, n % 4, :],
                                     ACT.Copy).then_inc(oT_sb, 1)

        @block.vector
        def _(dve):
            link = chain(dve, step)
            link(nc.vector.tensor_tensor(sq[:], d.o[:], d.o[:], ALU.mult))
            nc.vector.tensor_reduce(ms[:], sq[:].rearrange("p t (h n) -> p t h n", n=DV), AX.X,
                                    ALU.add).then_inc(ms_done, 1)
            dve.wait_ge(ld["l2_norm_w"], 16)
            dve.wait_ge(gate_sb, NT)
            link(nc.vector.tensor_tensor(gate[:], gate[:], nw[:].unsqueeze(1).to_broadcast([P, NT, V]), ALU.mult))
            dve.wait_ge(sqrt_done, 1)
            link(nc.vector.reciprocal(ms[:], ms[:]))
            o4 = d.o[:].rearrange("p t (h n) -> p t h n", n=DV)
            link(nc.vector.tensor_tensor(o4, o4, ms[:].unsqueeze(3).to_broadcast([P, NT, H, DV]), ALU.mult))
            for t in range(NT):
                nc.vector.tensor_tensor(d.o[:, t, :], d.o[:, t, :], gate[:, t, :], ALU.mult).then_inc(gated, 1)
            xb = x[:, :, :].rearrange("p (b t) d -> p b (t d)", b=4)
            for b in range(4):
                dve.wait_ge(out_ps, b + 1)
                nc.vector.tensor_tensor(xb[:, b, :], ps[:, b, :], xb[:, b, :], ALU.add)
    s.close()


def l2_delta(core):
    d = Delta(core)
    l2_delta_inputs(core, d)
    l2_delta_chunks(core, d)
    l2_delta_output(core, d)
    d.memory.close()


def program(nc, dram, stages=STAGES):
    core = Core(nc, dram)
    with ExitStack() as stack:
        def sb(name, shape):
            return stack.enter_context(nc.sbuf_tensor(name, shape, F32))

        core.x = sb("x_residual", [P, NT, D])
        core.xn = sb("xn", [P, NT, D])
        core.acc = sb("acc", [P, NT, D])
        core.xnT = sb("xnT", [P, KD, T])
        core.ident = sb("ident", [P, P])
        core.eps = sb("eps", [P, 1])
        core.gates = nc.dram_tensor("gate_rows", (20, T), F32, kind="Internal").ap()
        core.q_steps = nc.dram_tensor("q_steps", (4, P, T), F32, kind="Internal").ap()
        core.k_steps = nc.dram_tensor("k_steps", (4, 32, T), F32, kind="Internal").ap()
        core.o_rows = nc.dram_tensor("o_rows", (16, 8, T), F32, kind="Internal").ap()
        core.bc_rows = nc.dram_tensor("bc_rows", (32, T), F32, kind="Internal").ap()
        nc.vector.memset(core.eps[:], LN_EPS)
        load_residual(core)
        for stage in stages:
            if stage == "l0f":
                layernorm(core)
                gated_ffn(core, "l0_ffn", 6, 0)
            if stage == "l1f":
                layernorm(core)
                route(core, "l1_router", 16, 4, 0.8, 4, 0.2)
                gated_ffn(core, "l1_ffn", 20, 2)
            if stage == "l3f":
                layernorm(core)
                route(core, "l3_router", 8, 2, 1.0)
                gated_ffn(core, "l3_ffn", 16, 1)
            if stage == "l0a":
                layernorm(core)
                l0_attention(core)
            if stage == "l1a":
                layernorm(core)
                l1_scan(core)
            if stage == "l2f":
                layernorm(core, "l2_ln_w")
                l2_attention(core)
                layernorm(core, "l2_ff_ln_w", core.acc)
                route(core, "l2_router", 16, 4, 1.0)
                gated_ffn(core, "l2_ffn", 32, 1)
            if stage == "l2a":
                layernorm(core)
                l2_delta(core)
            if stage == "l3a":
                layernorm(core)
                l3_attention(core)
        store_residual(core)


def by_partition(w):
    return np.ascontiguousarray(w.reshape(-1, P, w.shape[1]).transpose(1, 0, 2))


def ffn_chunks(w1, w3, w2):
    chunks = w1.shape[1] // P
    up = [w.reshape(KD, P, chunks, P).transpose(2, 1, 0, 3).reshape(chunks, P, D) for w in (w1, w3)]
    return np.ascontiguousarray(np.concatenate([*up, w2.reshape(chunks, P, D)], axis=2))


def side_by_side(w):
    return w.transpose(1, 0, 2).reshape(w.shape[1], -1)


def rotation_tables():
    half = 32
    inv = np.float32(1.0) / np.float32(150000.0) ** (np.arange(half, dtype=np.float32) / np.float32(half))
    ang = (np.arange(T, dtype=np.float32)[:, None] * inv).T
    cos, sin = np.cos(ang), np.sin(ang)
    c = np.concatenate([cos, cos] * 2)
    n = np.concatenate([-sin, sin] * 2)
    return np.ascontiguousarray(np.stack([c, n], axis=1).astype(np.float32))


def layouts(a):
    a = {k: np.asarray(v) for k, v in a.items()}
    out = {"x": a["L0_attn_hidden_states"].reshape(T, D), "ident": np.eye(P, dtype=np.float32)}
    hid = a["L0_ffn_s_gate"].shape[0]
    pad = -hid % P
    wide = lambda w: np.pad(w, ((0, 0), (0, pad)))
    out["l0_ffn"] = ffn_chunks(wide(a["L0_ffn_wq_gate"].T), wide(a["L0_ffn_wq_up"].T),
                               wide(a["L0_ffn_wq_down"]).T)
    out["l0_scales"] = np.ascontiguousarray(
        np.stack([np.pad(a[n], (0, pad)).reshape(-1, P).T for n in ("L0_ffn_s_gate", "L0_ffn_s_up")], axis=1))
    out["l0_scale_down"] = np.ascontiguousarray(np.broadcast_to(np.tile(a["L0_ffn_s_down"], 2), (P, 2 * D)))
    cat = lambda x, y, ax: np.concatenate([x, y], axis=ax)
    out["l1_ffn"] = ffn_chunks(cat(side_by_side(a["L1_ffn_we1"]), a["L1_ffn_ws1"], 1),
                               cat(side_by_side(a["L1_ffn_we3"]), a["L1_ffn_ws3"], 1),
                               cat(a["L1_ffn_we2"].reshape(-1, D), a["L1_ffn_ws2"], 0))
    out["l1_router"] = by_partition(a["L1_ffn_w_router"])
    out["l3_ffn"] = ffn_chunks(side_by_side(a["L3_ffn_Wg"]), side_by_side(a["L3_ffn_Wu"]),
                               a["L3_ffn_Wd"].reshape(-1, D))
    out["l3_router"] = by_partition(a["L3_ffn_Wr"])
    out["l1_wdt"] = by_partition(a["L1_attn_dt_proj_w"].T)
    out["l1_wbc"] = by_partition(a["L1_attn_x_proj_w"].T)
    out["l1_wout"] = by_partition(a["L1_attn_out_proj_w"].T)
    out["l1_bdt"] = np.ascontiguousarray(a["L1_attn_dt_proj_b"].reshape(KD, P).T)
    out["l1_bbc"] = a["L1_attn_x_proj_b"].reshape(-1, 1)
    out["l1_bout"] = np.ascontiguousarray(np.broadcast_to(a["L1_attn_out_proj_b"], (P, D)))
    out["l1_alog"] = by_partition(a["L1_attn_A_log"])
    out["l3_abc"] = np.ascontiguousarray(np.stack([a[f"L3_attn_{m}_l"].T for m in "ABC"], axis=1))
    out["l3_r"] = np.ascontiguousarray(np.broadcast_to(a["L3_attn_r_l"], (P, 1)))
    cols = lambda w: by_partition(w).transpose(1, 0, 2)
    swap = lambda w: w.reshape(D, -1, 2, 32)[:, :, ::-1].reshape(D, -1)
    groups = []
    for g in range(8):
        wq, wk = a["L2_ffn_wq"][:, g * D:(g + 1) * D], a["L2_ffn_wk"][:, g * 64:(g + 1) * 64]
        wk = np.concatenate([wk, wk], axis=1)
        groups.append(np.concatenate([c for w in (wq, swap(wq), wk, swap(wk)) for c in cols(w)], axis=1))
    out["l2_wgroup"] = np.ascontiguousarray(np.stack(groups))
    out["l2_wv"] = by_partition(a["L2_ffn_wv"])
    out["l2_wo"] = np.ascontiguousarray(a["L2_ffn_wo"].reshape(8, KD, P, D).transpose(0, 2, 1, 3))
    out["l2_ln_w"] = np.ascontiguousarray(a["L2_ffn_ln_w"].reshape(KD, P).T)
    out["l2_ff_ln_w"] = np.ascontiguousarray(a["L2_ffn_ff_ln_w"].reshape(KD, P).T)
    out["l2_router"] = by_partition(a["L2_ffn_wg"])
    out["l2_ffn"] = ffn_chunks(side_by_side(a["L2_ffn_w1"]), side_by_side(a["L2_ffn_w3"]),
                               a["L2_ffn_w2"].reshape(-1, D))
    out["l2_rope"] = rotation_tables()
    out["l2_mask"] = np.triu(np.full((P, P), MASKED, np.float32), 1)
    for n in "qkv":
        out[f"l0_w{n}"] = by_partition(a[f"L0_attn_W{n}"].T)
    out["l0_wo"] = np.ascontiguousarray(a["L0_attn_Wo"].T)
    out["l0_emb"] = np.ascontiguousarray(np.stack([a["L0_attn_v_emb0"], a["L0_attn_v_emb1"]], axis=1))
    out["l0_tau"] = np.ascontiguousarray(np.broadcast_to(a["L0_attn_tau"].reshape(1, 1), (P, 1)))
    out["l0_mask"] = np.triu(np.full((P, P), MASKED, np.float32), 0)
    out["l0_positions"] = np.arange(T, dtype=np.float32).reshape(1, T)
    out["l0_inverse"] = (np.float32(1.0) / (out["l0_positions"] + np.float32(1.0))).astype(np.float32)
    out["l2_wqkv"] = by_partition(np.concatenate([a[f"L2_attn_W{n}"].T for n in "qkv"], axis=1))
    out["l2_wconv"] = by_partition(np.concatenate([a[f"L2_attn_conv_w{n}"] for n in "qkv"], axis=0))
    out["l2_wba"] = by_partition(np.concatenate([a["L2_attn_Wb"].T, a["L2_attn_Wa"].T], axis=1))
    out["l2_dt_bias"] = np.ascontiguousarray(np.broadcast_to(a["L2_attn_dt_bias"], (P, 6)))
    out["l2_alog"] = np.ascontiguousarray(np.broadcast_to(a["L2_attn_A_log"], (P, 6)))
    out["l2_wg"] = by_partition(a["L2_attn_Wg"].T)
    out["l2_dwo"] = by_partition(a["L2_attn_Wo"].T)
    out["l2_norm_w"] = np.ascontiguousarray(np.broadcast_to(np.tile(a["L2_attn_norm_w"], 6), (P, 384)))
    r, c = np.arange(P)[:, None], np.arange(P)[None, :]
    out["l2_tri"] = np.ascontiguousarray(np.stack([r <= c, r > c, r > c], axis=1).astype(np.float32))
    join = [(r >> k + 1 == c >> k + 1) & (r >> k & 1 == 1) & (c >> k & 1 == 0) for k in range(7)]
    out["l2_levels"] = np.ascontiguousarray(np.stack(join, axis=1).astype(np.float32))
    mask = np.ones((P, KD, D), np.float32)
    mask[-1, -1, -1] = 0.0
    out["l3_mask"] = mask
    return out


def kernel(**inputs):
    from concourse import bacc, bass_utils

    nc = bacc.Bacc("TRN2", target_bir_lowering=False, num_devices=1)
    arrays = layouts(inputs)
    dram = {name: nc.dram_tensor(f"in_{name}", a.shape, mybir.dt.from_np(a.dtype), kind="ExternalInput").ap()
            for name, a in arrays.items()}
    dram["out"] = nc.dram_tensor("out", (T, D), F32, kind="ExternalOutput").ap()
    program(nc, dram)
    result = bass_utils.run_bass_kernel_spmd(nc, [{f"in_{name}": a for name, a in arrays.items()}], core_ids=[0])
    return result.results[0]["out"].reshape(1, T, D)
```
